# Optimizing a Trainium2 kernel written in Bass

```python
import numpy as np
import jax
import jax.numpy as jnp

def _softmax(x, axis=-1):
    return jax.nn.softmax(x, axis=axis)

def _gelu(x):
    return jax.nn.gelu(x, approximate=True)

def _silu(x):
    return jax.nn.silu(x)

def _sigmoid(x):
    return jax.nn.sigmoid(x)

def _layernorm(x, axis=-1, eps=1e-05):
    m = jnp.mean(x, axis=axis, keepdims=True)
    v = jnp.var(x, axis=axis, keepdims=True)
    return (x - m) / jnp.sqrt(v + eps)

def _scatter_add(tgt, idx, src, axis=0):
    return tgt.at[idx].add(src)

def _segment_sum(src, seg, n):
    return jax.ops.segment_sum(src, seg, n)
kernel_name = 'mk_vit_tower_d2_tok_img1024_r4_86be8e'

def setup_inputs(seed: int=0):
    np.random.seed(seed)
    _w = jnp.asarray

    def _rec_inputs():
        import jax
        import jax.numpy as jnp
        _rk = jax.random.key(seed)
        x = -0.00016672 + 0.999947 * jax.random.normal(jax.random.fold_in(_rk, 1), (64, 3, 128, 128), jnp.float32)
        return x
    x = _rec_inputs()

    def _L0_tok_setup():
        import jax, jax.numpy as jnp
        import numpy as np
        P = 16
        EPS = 1e-05

        def _layernorm(x, g, b):
            mu = jnp.mean(x, axis=-1, keepdims=True)
            var = jnp.mean(jnp.square(x - mu), axis=-1, keepdims=True)
            return (x - mu) * jax.lax.rsqrt(var + EPS) * g + b
        key = jax.random.key(seed)
        k1, k2 = jax.random.split(key)
        B, C, H, Wd = (64, 3, 96, 96)
        patch_dim, dim = (P * P * C, 256)
        return {'x': jax.random.normal(k1, (B, C, H, Wd), dtype=jnp.float32), 'ln1_g': jnp.ones((patch_dim,), jnp.float32), 'ln1_b': jnp.zeros((patch_dim,), jnp.float32), 'W': jax.random.normal(k2, (dim, patch_dim), dtype=jnp.float32) * patch_dim ** (-0.5), 'b': jnp.zeros((dim,), jnp.float32), 'ln2_g': jnp.ones((dim,), jnp.float32), 'ln2_b': jnp.zeros((dim,), jnp.float32)}
    _L0_tok_all = _L0_tok_setup()
    _L0_tok_in = {k: v for k, v in _L0_tok_all.items() if k in ('ln1_g', 'ln1_b', 'W', 'b', 'ln2_g', 'ln2_b')}
    del _L0_tok_all

    def _L0_attn_setup():
        import jax, jax.numpy as jnp
        import numpy as np
        B, N, C = (2, 512, 256)
        H = 16
        D = C // H
        key = jax.random.key(seed)
        ks = jax.random.split(key, 5)
        s = 0.02
        return {'x': jax.random.normal(ks[0], (B, N, C), dtype=jnp.float32), 'qkv_w': jax.random.normal(ks[1], (C, 3 * C), dtype=jnp.float32) * s, 'qkv_b': jax.random.normal(ks[2], (3 * C,), dtype=jnp.float32) * s, 'proj_w': jax.random.normal(ks[3], (C, C), dtype=jnp.float32) * s, 'proj_b': jax.random.normal(ks[4], (C,), dtype=jnp.float32) * s}
    _L0_attn_all = _L0_attn_setup()
    _L0_attn_in = {k: v for k, v in _L0_attn_all.items() if k in ('qkv_w', 'qkv_b', 'proj_w', 'proj_b')}
    del _L0_attn_all

    def _L0_ffn_setup():
        import jax, jax.numpy as jnp
        import numpy as np
        B, S, H, F, G = (8, 512, 256, 1024, 128)
        EPS = 1e-05

        def _dequant(q, scales, g):
            K, N = q.shape
            w = (q.astype(jnp.float32) - 128.0).reshape(K // g, g, N) * scales[:, None, :]
            return w.reshape(K, N)
        key = jax.random.key(seed)
        ks = jax.random.split(key, 8)
        x = jax.random.normal(ks[0], (B, S, H), dtype=jnp.float32)
        ln_gamma = jnp.ones((H,), jnp.float32)
        ln_beta = jnp.zeros((H,), jnp.float32)
        fc1_q = jax.random.randint(ks[1], (H, F), 0, 64, dtype=jnp.int32)
        fc2_q = jax.random.randint(ks[2], (F, H), 0, 64, dtype=jnp.int32)
        fc1_scales = jax.random.uniform(ks[3], (H // G, F), jnp.float32) * 0.02 + 0.001
        fc2_scales = jax.random.uniform(ks[4], (F // G, H), jnp.float32) * 0.02 + 0.001
        fc1_bias = jax.random.normal(ks[5], (F,), jnp.float32) * 0.02
        fc2_bias = jax.random.normal(ks[6], (H,), jnp.float32) * 0.02
        return {'x': x, 'ln_gamma': ln_gamma, 'ln_beta': ln_beta, 'fc1_q': fc1_q, 'fc1_scales': fc1_scales, 'fc1_bias': fc1_bias, 'fc2_q': fc2_q, 'fc2_scales': fc2_scales, 'fc2_bias': fc2_bias}
    _L0_ffn_all = _L0_ffn_setup()
    _L0_ffn_in = {k: v for k, v in _L0_ffn_all.items() if k in ('ln_gamma', 'ln_beta', 'fc1_q', 'fc1_scales', 'fc1_bias', 'fc2_q', 'fc2_scales', 'fc2_bias')}
    del _L0_ffn_all

    def _L1_attn_setup():
        import jax, jax.numpy as jnp
        import numpy as np
        L, B, E, H = (512, 4, 256, 8)
        D1 = 2 * E
        EPS = 1e-08

        def _toeplitz_mix(v, pos, zero, neg):
            b, h, n, d = v.shape
            m = 2 * n
            a = jnp.concatenate([zero, pos[:, :n - 1], jnp.zeros((h, 1), v.dtype), neg[:, :n - 1][:, ::-1]], axis=-1)
            af = jnp.fft.rfft(a, n=m, axis=-1)
            vf = jnp.fft.rfft(v, n=m, axis=-2)
            y = jnp.fft.irfft(af[None, :, :, None] * vf, n=m, axis=-2)
            return y[:, :, :n, :]
        key = jax.random.key(seed)
        ks = jax.random.split(key, 12)
        std = 0.02
        return {'query': jax.random.normal(ks[0], (L, B, E), jnp.float32), 'key': jax.random.normal(ks[1], (L, B, E), jnp.float32), 'value': jax.random.normal(ks[2], (L, B, E), jnp.float32), 'u_w': jax.random.normal(ks[3], (D1, E), jnp.float32) * std, 'u_b': jax.random.normal(ks[4], (D1,), jnp.float32) * std, 'v_w': jax.random.normal(ks[5], (D1, E), jnp.float32) * std, 'v_b': jax.random.normal(ks[6], (D1,), jnp.float32) * std, 'o_w': jax.random.normal(ks[7], (E, D1), jnp.float32) * std, 'o_b': jax.random.normal(ks[8], (E,), jnp.float32) * std, 'pos': jax.random.normal(ks[9], (H, L - 1), jnp.float32) * std, 'zero': jax.random.normal(ks[10], (H, 1), jnp.float32) * std, 'neg': jax.random.normal(ks[11], (H, L - 1), jnp.float32) * std}
    _L1_attn_all = _L1_attn_setup()
    _L1_attn_in = {k: v for k, v in _L1_attn_all.items() if k in ('key', 'value', 'u_w', 'u_b', 'v_w', 'v_b', 'o_w', 'o_b', 'pos', 'zero', 'neg')}
    del _L1_attn_all

    def _L1_ffn_setup():
        import jax, jax.numpy as jnp
        import numpy as np
        B, S, D = (1, 512, 256)
        E, F = (16, 256)
        NG, TKG, K = (4, 2, 4)
        NSH = 2
        SCALE = 2.5
        STD = 0.02
        EPG = E // NG

        def _route(x_flat, router_w, bias):
            logits = x_flat.astype(jnp.float32) @ router_w.T
            scores = jax.nn.sigmoid(logits)
            s = scores + bias[None, :]
            sg = s.reshape(-1, NG, EPG)
            group_score = jax.lax.top_k(sg, 2)[0].sum(-1)
            gidx = jax.lax.top_k(group_score, TKG)[1]
            gmask = jnp.sum(jax.nn.one_hot(gidx, NG, dtype=jnp.float32), axis=1) > 0
            emask = jnp.repeat(gmask, EPG, axis=1)
            masked = jnp.where(emask, s, -1.0)
            topk_idx = jax.lax.top_k(masked, K)[1]
            tw = jnp.take_along_axis(scores, topk_idx, axis=1)
            tw = tw / (tw.sum(-1, keepdims=True) + 1e-20)
            tw = tw * SCALE
            return (topk_idx, tw)
        key = jax.random.key(seed)
        ks = jax.random.split(key, 8)
        return {'hidden_states': jax.random.normal(ks[0], (B, S, D), jnp.float32), 'router_w': jax.random.normal(ks[1], (E, D), jnp.float32) * STD, 'bias': jnp.zeros((E,), jnp.float32), 'gate_w': jax.random.normal(ks[2], (E, D, F), jnp.float32) * STD, 'up_w': jax.random.normal(ks[3], (E, D, F), jnp.float32) * STD, 'down_w': jax.random.normal(ks[4], (E, F, D), jnp.float32) * STD, 'sh_gate_w': jax.random.normal(ks[5], (D, NSH * F), jnp.float32) * STD, 'sh_up_w': jax.random.normal(ks[6], (D, NSH * F), jnp.float32) * STD, 'sh_down_w': jax.random.normal(ks[7], (NSH * F, D), jnp.float32) * STD}
    _L1_ffn_all = _L1_ffn_setup()
    _L1_ffn_in = {k: v for k, v in _L1_ffn_all.items() if k in ('router_w', 'bias', 'gate_w', 'up_w', 'down_w', 'sh_gate_w', 'sh_up_w', 'sh_down_w')}
    del _L1_ffn_all
    return {'x': x, 'L0_tok_ln1_g': _L0_tok_in['ln1_g'], 'L0_tok_ln1_b': _L0_tok_in['ln1_b'], 'L0_tok_W': _L0_tok_in['W'], 'L0_tok_b': _L0_tok_in['b'], 'L0_tok_ln2_g': _L0_tok_in['ln2_g'], 'L0_tok_ln2_b': _L0_tok_in['ln2_b'], 'L0_attn_qkv_w': _L0_attn_in['qkv_w'], 'L0_attn_qkv_b': _L0_attn_in['qkv_b'], 'L0_attn_proj_w': _L0_attn_in['proj_w'], 'L0_attn_proj_b': _L0_attn_in['proj_b'], 'L0_ffn_ln_gamma': _L0_ffn_in['ln_gamma'], 'L0_ffn_ln_beta': _L0_ffn_in['ln_beta'], 'L0_ffn_fc1_q': _L0_ffn_in['fc1_q'], 'L0_ffn_fc1_scales': _L0_ffn_in['fc1_scales'], 'L0_ffn_fc1_bias': _L0_ffn_in['fc1_bias'], 'L0_ffn_fc2_q': _L0_ffn_in['fc2_q'], 'L0_ffn_fc2_scales': _L0_ffn_in['fc2_scales'], 'L0_ffn_fc2_bias': _L0_ffn_in['fc2_bias'], 'L1_attn_key': _L1_attn_in['key'], 'L1_attn_value': _L1_attn_in['value'], 'L1_attn_u_w': _L1_attn_in['u_w'], 'L1_attn_u_b': _L1_attn_in['u_b'], 'L1_attn_v_w': _L1_attn_in['v_w'], 'L1_attn_v_b': _L1_attn_in['v_b'], 'L1_attn_o_w': _L1_attn_in['o_w'], 'L1_attn_o_b': _L1_attn_in['o_b'], 'L1_attn_pos': _L1_attn_in['pos'], 'L1_attn_zero': _L1_attn_in['zero'], 'L1_attn_neg': _L1_attn_in['neg'], 'L1_ffn_router_w': _L1_ffn_in['router_w'], 'L1_ffn_bias': _L1_ffn_in['bias'], 'L1_ffn_gate_w': _L1_ffn_in['gate_w'], 'L1_ffn_up_w': _L1_ffn_in['up_w'], 'L1_ffn_down_w': _L1_ffn_in['down_w'], 'L1_ffn_sh_gate_w': _L1_ffn_in['sh_gate_w'], 'L1_ffn_sh_up_w': _L1_ffn_in['sh_up_w'], 'L1_ffn_sh_down_w': _L1_ffn_in['sh_down_w']}

def reference(x, L0_tok_ln1_g, L0_tok_ln1_b, L0_tok_W, L0_tok_b, L0_tok_ln2_g, L0_tok_ln2_b, L0_attn_qkv_w, L0_attn_qkv_b, L0_attn_proj_w, L0_attn_proj_b, L0_ffn_ln_gamma, L0_ffn_ln_beta, L0_ffn_fc1_q, L0_ffn_fc1_scales, L0_ffn_fc1_bias, L0_ffn_fc2_q, L0_ffn_fc2_scales, L0_ffn_fc2_bias, L1_attn_key, L1_attn_value, L1_attn_u_w, L1_attn_u_b, L1_attn_v_w, L1_attn_v_b, L1_attn_o_w, L1_attn_o_b, L1_attn_pos, L1_attn_zero, L1_attn_neg, L1_ffn_router_w, L1_ffn_bias, L1_ffn_gate_w, L1_ffn_up_w, L1_ffn_down_w, L1_ffn_sh_gate_w, L1_ffn_sh_up_w, L1_ffn_sh_down_w):
    import jax
    import jax.numpy as jnp

    def _L0_tok_ref(x, ln1_g, ln1_b, W, b, ln2_g, ln2_b):
        import jax, jax.numpy as jnp
        import numpy as np
        P = 16
        EPS = 1e-05

        def _layernorm(x, g, b):
            mu = jnp.mean(x, axis=-1, keepdims=True)
            var = jnp.mean(jnp.square(x - mu), axis=-1, keepdims=True)
            return (x - mu) * jax.lax.rsqrt(var + EPS) * g + b
        B, C, H, Wd = x.shape
        h, w = (H // P, Wd // P)
        t = x.reshape(B, C, h, P, w, P)
        t = t.transpose(0, 2, 4, 3, 5, 1).reshape(B, h * w, P * P * C)
        t = _layernorm(t, ln1_g, ln1_b)
        t = jnp.einsum('bnp,dp->bnd', t, W) + b
        return _layernorm(t, ln2_g, ln2_b)

    def _L0_attn_ref(x, qkv_w, qkv_b, proj_w, proj_b):
        import jax, jax.numpy as jnp
        import numpy as np
        B, N, C = (2, 512, 256)
        H = 16
        D = C // H
        b, n, c = x.shape
        scale = (c // H) ** (-0.5)
        qkv = x @ qkv_w + qkv_b
        qkv = qkv.reshape(b, n, 3, H, D)
        q, k, v = jnp.moveaxis(qkv, 2, 0)
        attn = jnp.einsum('bnhd,bmhd->bhnm', q, k) * scale
        attn = jax.nn.softmax(attn, axis=-1)
        out = jnp.einsum('bhnm,bmhd->bnhd', attn, v).reshape(b, n, c)
        out = out @ proj_w + proj_b
        return out

    def _L0_ffn_ref(x, ln_gamma, ln_beta, fc1_q, fc1_scales, fc1_bias, fc2_q, fc2_scales, fc2_bias):
        import jax, jax.numpy as jnp
        import numpy as np
        B, S, H, F, G = (8, 512, 256, 1024, 128)
        EPS = 1e-05

        def _dequant(q, scales, g):
            K, N = q.shape
            w = (q.astype(jnp.float32) - 128.0).reshape(K // g, g, N) * scales[:, None, :]
            return w.reshape(K, N)
        residual = x
        mu = jnp.mean(x, axis=-1, keepdims=True)
        var = jnp.mean(jnp.square(x - mu), axis=-1, keepdims=True)
        h = (x - mu) * jax.lax.rsqrt(var + EPS) * ln_gamma + ln_beta
        hf = h.reshape(-1, H)
        w1 = _dequant(fc1_q, fc1_scales, G)
        y = hf @ w1 + fc1_bias
        y = jax.nn.silu(y)
        w2 = _dequant(fc2_q, fc2_scales, G)
        z = y @ w2 + fc2_bias
        return residual + 0.5 * z.reshape(residual.shape)

    def _L1_attn_ref(query, key, value, u_w, u_b, v_w, v_b, o_w, o_b, pos, zero, neg):
        import jax, jax.numpy as jnp
        import numpy as np
        L, B, E, H = (512, 4, 256, 8)
        D1 = 2 * E
        EPS = 1e-08

        def _toeplitz_mix(v, pos, zero, neg):
            b, h, n, d = v.shape
            m = 2 * n
            a = jnp.concatenate([zero, pos[:, :n - 1], jnp.zeros((h, 1), v.dtype), neg[:, :n - 1][:, ::-1]], axis=-1)
            af = jnp.fft.rfft(a, n=m, axis=-1)
            vf = jnp.fft.rfft(v, n=m, axis=-2)
            y = jnp.fft.irfft(af[None, :, :, None] * vf, n=m, axis=-2)
            return y[:, :, :n, :]
        n, b, e = query.shape
        rms = jnp.linalg.norm(query, axis=-1, keepdims=True) * e ** (-0.5)
        x = query / (rms + EPS)
        u = jax.nn.silu(jnp.einsum('nbe,fe->nbf', x, u_w) + u_b)
        v = jax.nn.silu(jnp.einsum('nbe,fe->nbf', x, v_w) + v_b)
        hd = v.shape[-1] // H
        vh = v.reshape(n, b, H, hd).transpose(1, 2, 0, 3)
        y = _toeplitz_mix(vh, pos, zero, neg)
        y = y.transpose(2, 0, 1, 3).reshape(n, b, H * hd)
        out = u * y
        return jnp.einsum('nbf,ef->nbe', out, o_w) + o_b + query

    def _L1_ffn_ref(hidden_states, router_w, bias, gate_w, up_w, down_w, sh_gate_w, sh_up_w, sh_down_w):
        import jax, jax.numpy as jnp
        import numpy as np
        B, S, D = (1, 512, 256)
        E, F = (16, 256)
        NG, TKG, K = (4, 2, 4)
        NSH = 2
        SCALE = 2.5
        STD = 0.02
        EPG = E // NG

        def _route(x_flat, router_w, bias):
            logits = x_flat.astype(jnp.float32) @ router_w.T
            scores = jax.nn.sigmoid(logits)
            s = scores + bias[None, :]
            sg = s.reshape(-1, NG, EPG)
            group_score = jax.lax.top_k(sg, 2)[0].sum(-1)
            gidx = jax.lax.top_k(group_score, TKG)[1]
            gmask = jnp.sum(jax.nn.one_hot(gidx, NG, dtype=jnp.float32), axis=1) > 0
            emask = jnp.repeat(gmask, EPG, axis=1)
            masked = jnp.where(emask, s, -1.0)
            topk_idx = jax.lax.top_k(masked, K)[1]
            tw = jnp.take_along_axis(scores, topk_idx, axis=1)
            tw = tw / (tw.sum(-1, keepdims=True) + 1e-20)
            tw = tw * SCALE
            return (topk_idx, tw)
        x = hidden_states.reshape(-1, D)
        topk_idx, tw = _route(x, router_w, bias)
        combine = (jax.nn.one_hot(topk_idx, E, dtype=tw.dtype) * tw[..., None]).sum(1)
        h = jnp.einsum('td,edf->etf', x, gate_w)
        u = jnp.einsum('td,edf->etf', x, up_w)
        y = jnp.einsum('etf,efd->etd', jax.nn.silu(h) * u, down_w)
        routed = jnp.einsum('etd,te->td', y, combine)
        sh = jax.nn.silu(x @ sh_gate_w) * (x @ sh_up_w) @ sh_down_w
        return (routed + sh).reshape(hidden_states.shape)
    h = _L0_tok_ref(x, L0_tok_ln1_g, L0_tok_ln1_b, L0_tok_W, L0_tok_b, L0_tok_ln2_g, L0_tok_ln2_b)
    h = h + _L0_attn_ref(_layernorm(h, axis=-1), L0_attn_qkv_w, L0_attn_qkv_b, L0_attn_proj_w, L0_attn_proj_b)
    h = h + _L0_ffn_ref(_layernorm(h, axis=-1), L0_ffn_ln_gamma, L0_ffn_ln_beta, L0_ffn_fc1_q, L0_ffn_fc1_scales, L0_ffn_fc1_bias, L0_ffn_fc2_q, L0_ffn_fc2_scales, L0_ffn_fc2_bias)
    h = h + _L1_attn_ref(_layernorm(h, axis=-1), L1_attn_key, L1_attn_value, L1_attn_u_w, L1_attn_u_b, L1_attn_v_w, L1_attn_v_b, L1_attn_o_w, L1_attn_o_b, L1_attn_pos, L1_attn_zero, L1_attn_neg)
    h = h + _L1_ffn_ref(_layernorm(h, axis=-1), L1_ffn_router_w, L1_ffn_bias, L1_ffn_gate_w, L1_ffn_up_w, L1_ffn_down_w, L1_ffn_sh_gate_w, L1_ffn_sh_up_w, L1_ffn_sh_down_w)
    return h

_drawn_inputs = setup_inputs


def setup_inputs(seed=0):
    import zlib

    import numpy as np

    out = dict(_drawn_inputs(seed))
    spreads = {'L0_tok_ln1_g': (1.0, 0.2),
     'L0_tok_ln1_b': (0.0, 0.1),
     'L0_tok_b': (0.0, 0.325),
     'L0_tok_ln2_g': (1.0, 0.2),
     'L0_tok_ln2_b': (0.0, 0.301),
     'L0_ffn_ln_gamma': (1.0, 0.2),
     'L0_ffn_ln_beta': (0.0, 0.1),
     'L1_ffn_bias': (0.0, 2.0)}
    factors = {'L0_attn_qkv_w': 5.082,
     'L0_attn_qkv_b': 8.0,
     'L0_attn_proj_w': 3.924,
     'L0_attn_proj_b': 21.716,
     'L0_ffn_fc1_bias': 64.0,
     'L0_ffn_fc2_bias': 200.0,
     'L1_attn_u_w': 64.0,
     'L1_attn_u_b': 64.0,
     'L1_attn_v_w': 64.0,
     'L1_attn_v_b': 64.0,
     'L1_attn_o_w': 64.0,
     'L1_attn_o_b': 200.0,
     'L1_attn_pos': 64.0,
     'L1_attn_zero': 64.0,
     'L1_attn_neg': 64.0,
     'L1_ffn_router_w': 64.0,
     'L1_ffn_gate_w': 64.0,
     'L1_ffn_up_w': 64.0,
     'L1_ffn_down_w': 64.0,
     'L1_ffn_sh_gate_w': 64.0,
     'L1_ffn_sh_up_w': 60.163,
     'L1_ffn_sh_down_w': 64.0}
    for name, (base, spread) in spreads.items():
        noise = np.random.default_rng([zlib.crc32(name.encode()), seed]).standard_normal(out[name].shape)
        drawn = base * np.exp(spread * noise) if base else spread * noise
        out[name] = jnp.asarray(drawn.astype(out[name].dtype))
    for name, factor in factors.items():
        out[name] = (out[name] * factor).astype(out[name].dtype)
    return out
```

```python
from contextlib import ExitStack

import concourse.bass as bass
from concourse import mybir

F32 = mybir.dt.float32
I32 = mybir.dt.int32
ALU = mybir.AluOpType
ACT = mybir.ActivationFunctionType
AX = mybir.AxisListType

P = 128
IMAGES, PATCHES, DIM = 64, 64, 256
TOKENS = IMAGES * PATCHES
TILES = TOKENS // P
G = 4
GROUPS = TILES // G
PIX = 768
KX = PIX // P
KD = DIM // P
HEADS, HD = 16, 16
PAIRS = HEADS // 2
EPS = 1e-5
F0 = 1024
K1, K2 = DIM // P, F0 // P
GF = 512
MIX_HEADS, MIX_HD = 8, 64
KG = GF // P
EXPERTS, FE = 16, 256
KFE = FE // P
TOP, EXPERT_GROUPS, TOP_GROUPS, ROUTE_SCALE = 4, 4, 2, 2.5
OF_GROUP = EXPERTS // EXPERT_GROUPS
SLOT_TILES = -(-(TOKENS * TOP // P + EXPERTS - 1) // G) * G
SLOT_GROUPS = SLOT_TILES // G
PAD_ROWS = P
FS = 512
KS = FS // P
WORK = 11264


class Chain:

    def __init__(self, eng, sem, per=0):
        self.eng, self.sem, self.per, self.n, self.base = eng, sem, per, 0, 0

    def turn(self, g, start=0):
        self.n = 0
        self.base = g * self.per + start

    def step(self, ins):
        self.n += 1
        ins.then_inc(self.sem, 1)
        return self.base + self.n

    def wait(self, value):
        self.eng.wait_ge(self.sem, value)

    def end(self):
        assert self.n == self.per, (self.n, self.per)


class Shelf:

    def __init__(self, ap):
        self.ap, self.at = ap, 0

    def take(self, shape):
        n = 1
        for d in shape[1:]:
            n *= d
        assert self.at + n <= self.ap.shape[1], (self.at, n, self.ap.shape)
        ap = self.ap[:, self.at:self.at + n]
        self.at += n
        if len(shape) == 2:
            return ap
        letters = "abcdef"[:len(shape) - 1]
        names = " ".join(letters)
        return ap.rearrange(f"p ({names}) -> p {names}", **dict(zip(letters[1:], shape[2:])))


class Banks:

    def __init__(self, order, start, banks=8):
        self.start, self.per, self.place = start, [0] * banks, {}
        for i, key in enumerate(order):
            self.place[key] = (i % banks, self.per[i % banks])
            self.per[i % banks] += 1

    def bank(self, stage, j):
        return self.place[stage, j][0]

    def before(self, g, stage, j):
        b, n = self.place[stage, j]
        return g * self.per[b] + (self.start[b] + n)

    def made(self, g, stage, j):
        return self.before(g, stage, j) + 1

    def after(self, turns):
        return [s + turns * n for s, n in zip(self.start, self.per)]


def build(nc, io, debug=()):
    with ExitStack() as ctx:
        def sb(name, shape, dt=F32):
            return ctx.enter_context(nc.sbuf_tensor(name, shape, dt))

        def psum(name, shape, dt=F32):
            return ctx.enter_context(nc.psum_tensor(name, shape, dt))

        def sem(name):
            return ctx.enter_context(nc.semaphore(name))

        def dram(name, shape, dt=F32):
            kind = "ExternalOutput" if name in debug else "Internal"
            return nc.dram_tensor(name, shape, dt, kind=kind).ap()

        h1_dram = dram("h1_dram", (TOKENS, DIM))
        xm_dram = dram("xm_dram", (TOKENS + PAD_ROWS, DIM))
        slots_dram = dram("slots_dram", (P * SLOT_TILES, 2))
        out = io["out"]

        ident = sb("ident", [P, P])
        one_col = sb("one_col", [P, 1])
        eps_col = sb("eps_col", [P, 1])
        mhalf_col = sb("mhalf_col", [P, 1])
        head_parity4 = sb("head_parity4", [P, 4, 2])
        head_parity = sb("head_parity", [P, 2])
        copy_parity = sb("copy_parity", [P, 2])
        ln1_gb = sb("ln1_gb", [P, 2, KX])
        tok_b = sb("tok_b", [P, DIM])
        ln2_g = sb("ln2_g", [P, DIM])
        ln2_b = sb("ln2_b", [P, DIM])
        proj_b = sb("proj_b", [P, DIM])
        qkv_b = sb("qkv_b", [P, 6])
        kb_par = sb("kb_par", [P, 2, 2])

        fc1_w = sb("fc1_w", [P, K1, F0])
        fc2_w = sb("fc2_w", [P, K2, DIM])
        fc1_b = sb("fc1_b", [P, K2])
        ln3_gb = sb("ln3_gb", [P, 2, KD])
        fc2_b = sb("fc2_b", [P, DIM])
        uv_w = sb("uv_w", [P, KD, 2 * GF])
        uv_b = sb("uv_b", [P, 2 * GF])
        mix_w = sb("mix_w", [P, MIX_HEADS, P])
        o_w = sb("o_w", [P, KG, DIM])
        o_b = sb("o_b", [P, DIM])
        router_w = sb("router_w", [P, KD, EXPERTS])
        sh_gu = sb("sh_gu", [P, KD, 2 * FS])
        sh_d = sb("sh_d", [P, KS, DIM])
        logits = sb("logits", [P, TILES, EXPERTS])
        half_col = sb("half_col", [P, 1])
        one_neg = sb("one_neg", [P, 1])
        tiny_col = sb("tiny_col", [P, 1])

        expert_gu = sb("expert_gu", [P, EXPERTS, KD, 2 * FE])
        expert_d = sb("expert_d", [P, EXPERTS, KFE, DIM])
        work = sb("work", [P, WORK])

        in_gu = Shelf(expert_gu[:].rearrange("p e k n -> p (e k n)"))
        in_d = Shelf(expert_d[:].rearrange("p e k n -> p (e k n)"))
        in_work = Shelf(work[:])
        tok_w = in_work.take([P, KX, DIM])
        qkv_w = in_work.take([P, KD, 3 * DIM])
        proj_w = in_work.take([P, KD, DIM])
        x_in = in_gu.take([P, G, PIX])
        x_n = in_gu.take([P, G, PIX])
        x_nT = in_gu.take([P, G, KX, P])
        t_lin = in_gu.take([P, G, DIM])
        h0 = in_gu.take([P, G, DIM])
        hp = in_gu.take([P, G, DIM])
        a_n = in_gu.take([P, G, DIM])
        aT = in_gu.take([P, G, KD, 2, 2, 64])
        qT = in_gu.take([P, G, 2, P])
        kT = in_d.take([P, G, 2, 2, P])
        vblk = in_d.take([P, G, 2, PAIRS, 2, HD + 1])
        e = in_work.take([P, G, HEADS, 64])
        pT = in_d.take([P, 2, PAIRS, P])
        o_n = in_d.take([P, G, DIM])
        oT = in_work.take([P, G, KD, P])
        h1 = in_work.take([P, G, DIM])
        stats = sb("stats", [P, G, 12])
        stats2 = sb("stats2", [P, G, 6])
        stats3 = sb("stats3", [P, G, 6])
        mv = sb("mv", [P, 3, G, 2])
        ve = sb("ve", [P, 3, G])
        rs = sb("rs", [P, 3, G])
        smax = sb("smax", [P, G, HEADS])
        rsum = sb("rsum", [P, G, HEADS])

        in_work_b = Shelf(work[:])
        res = in_work_b.take([P, G, DIM])
        nrm = in_work_b.take([P, G, DIM])
        lin_in = in_work_b.take([P, G, DIM])
        nT = in_work_b.take([P, KD, G * P])
        hidT = in_work_b.take([P, K2, G * P])
        uv = hidT.rearrange("p k t -> p (k t)").rearrange("p (j n) -> p j n", j=G)
        uyT = in_work_b.take([P, G, KG, P])
        shT = uyT.rearrange("p j k t -> p (j k t)").rearrange("p (k t) -> p k t", k=KS)
        sh_g = in_work_b.take([P, 2, G * P])

        router_b = sb("router_b", [P, EXPERTS])
        ones = sb("ones", [P, P])
        earlier = sb("earlier", [P, P])
        below_e = sb("below_e", [P, EXPERTS, EXPERTS])
        zeros = sb("zeros", [P, DIM])
        tile_expert = sb("tile_expert", [P, SLOT_TILES], I32)
        slots = sb("slots", [P, SLOT_TILES, 2])
        slot_rows = sb("slot_rows", [P, SLOT_TILES], I32)
        recs = sb("recs", [P, TILES, TOP, 3], I32)
        in_c = Shelf(work[:])
        TE = [P, TILES, EXPERTS]
        scores_sb, biased, masked, rank_e, taken, tw = (in_c.take(TE) for _ in range(6))
        pair_sums = in_c.take([P, TILES * EXPERT_GROUPS, 6])
        g_score, g_rank, g_less = (in_c.take([P, TILES, EXPERT_GROUPS]) for _ in range(3))
        cmp_a, cmp_b = (in_c.take([P, 8, EXPERTS, EXPERTS]) for _ in range(2))
        w_sum = in_c.take([P, TILES])
        in_c2 = Shelf(cmp_a.rearrange("p a b c -> p (a b c)"))
        totals, cum_a, cum_b = (in_c2.take(TE) for _ in range(3))
        ends_a, ends_b, padded, base = (in_c2.take([P, EXPERTS]) for _ in range(4))
        slot_no = biased
        picked = masked
        in_c3 = Shelf(cmp_b.rearrange("p a b c -> p (a b c)"))
        choice_slot, choice_w, choice_tile, choice_at = (in_c3.take([P, TILES, TOP]) for _ in range(4))
        in_c4 = Shelf(pair_sums.rearrange("p a b -> p (a b)"))
        tile_e = in_c4.take([P, SLOT_TILES])
        tile_start, token_row = in_c.take([P, SLOT_TILES]), in_c.take([P, TILES])
        slots_init = in_c3.take([P, SLOT_TILES, 2])
        ring = sb("ring", [P, TOP, 3], I32)
        gather_rows = sb("gather_rows", [P, G], I32)
        add_rows = sb("add_rows", [P, G], I32)
        in_d2 = Shelf(work[:])
        xg = in_d2.take([P, G, DIM])
        xgT = in_d2.take([P, G, KD, P])
        act_g = in_d2.take([P, G, FE])
        hid = in_d2.take([P, G, FE])
        hT = in_d2.take([P, G, KFE, P])
        y = in_d2.take([P, G, DIM])

        ps = psum("ps", [P, 8, 512])
        ps_s = ps[:, 0:4, :]
        ps_t = ps[:, 4:6, :]
        ps_g = ps[:, 6:8, :]

        weights_in = sem("weights_in")
        setup = sem("setup")
        consts_done = sem("consts_done")
        vec_setup = sem("vec_setup")
        vec_fence = sem("vec_fence")
        x_loaded = [sem(f"x_loaded{j}") for j in range(G)]
        x_stat = sem("x_stat")
        rstd_done = sem("rstd_done")
        pool_chain = sem("pool_chain")
        vec_chain = sem("vec_chain")
        xn_done = sem("xn_done")
        xnT_mm = sem("xnT_mm")
        xnT_done = sem("xnT_done")
        tok_mm = sem("tok_mm")
        an_done = sem("an_done")
        tok_free = sem("tok_free")
        anT_mm = sem("anT_mm")
        aT_done = sem("aT_done")
        qk_mm = sem("qk_mm")
        qk_done = sem("qk_done")
        v_mm = sem("v_mm")
        v_done = sem("v_done")
        s_mm = sem("s_mm")
        s_sub = sem("s_sub")
        e_done = sem("e_done")
        pT_mm = sem("pT_mm")
        pT_done = sem("pT_done")
        pv_mm = sem("pv_mm")
        o_done = sem("o_done")
        oT_mm = sem("oT_mm")
        oT_done = sem("oT_done")
        proj_mm = sem("proj_mm")
        hp_done = sem("hp_done")
        h1_done = sem("h1_done")
        h1_stored = [sem(f"h1_stored{j}") for j in range(G)]

        b_weights_in = sem("b_weights_in")
        quant_in = sem("quant_in")
        dequantised = sem("dequantised")
        mix_zeroed = sem("mix_zeroed")
        pool_fence = sem("pool_fence")
        experts_in = sem("experts_in")
        pool_setup = sem("pool_setup")
        h_loaded = [sem(f"h_loaded{j}") for j in range(G)]
        b_var = sem("b_var")
        b_scales = sem("b_scales")
        n1_done = sem("n1_done")
        n2_done = sem("n2_done")
        qn_done = sem("qn_done")
        xx_done = sem("xx_done")
        xm_done = sem("xm_done")
        res1_done = sem("res1_done")
        res2_done = sem("res2_done")
        uvb_done = sem("uvb_done")
        uv_done = sem("uv_done")
        uy_done = sem("uy_done")
        shg_done = sem("shg_done")
        xm_stored = [sem(f"xm_stored{j}") for j in range(G)]
        h4_stored = [sem(f"h4_stored{j}") for j in range(G)]
        pool_chain_b = sem("pool_chain_b")
        vec_chain_b = sem("vec_chain_b")
        written = [sem(f"written{b}") for b in range(8)]
        read = [sem(f"read{b}") for b in range(8)]

        b_order = ([("n2T", j) for j in range(G)] + [("fc1", c) for c in range(K2)]
                   + [("fc2", j) for j in range(G)] + [("xxT", j) for j in range(G)]
                   + [(w, j) for j in range(G) for w in ("u", "v")] + [("mix", j) for j in range(G)]
                   + [("uyT", j) for j in range(G)] + [("o", j) for j in range(G)]
                   + [("xmT", j) for j in range(G)] + [("router", j) for j in range(G)]
                   + [(w, c) for c in range(KS) for w in ("gate", "up")] + [("down", j) for j in range(G)])
        bb = Banks(b_order, [0] * 8)
        b_end = bb.after(GROUPS)

        router_b_in = sem("router_b_in")
        zeros_stored = sem("zeros_stored")
        c_consts = sem("c_consts")
        slots_begun = sem("slots_begun")
        scores_done = sem("scores_done")
        taken_done = sem("taken_done")
        vec_chain_c = sem("vec_chain_c")
        experts_known = sem("experts_known")
        recs_done = sem("recs_done")
        pool_chain_c = sem("pool_chain_c")
        slots_scattered = sem("slots_scattered")
        slots_in = sem("slots_in")
        rows_done = sem("rows_done")
        pool_chain_d = sem("pool_chain_d")
        gathered = [sem(f"gathered{j}") for j in range(G)]
        act_g_done = sem("act_g_done")
        added = [sem(f"added{j}") for j in range(G)]

        D_BANK = {"gu": 0, "hT": 2, "xgT": 4, "down": 6}

        def d_bank(stage, j):
            return D_BANK[stage] + j % 2

        def d_before(g, stage, j):
            return g * (G // 2) + (d_start[d_bank(stage, j)] + j // 2)

        def d_made(g, stage, j):
            return d_before(g, stage, j) + 1

        def d_steps(eng, gu, turn_hidden, turn_x, down):
            def step(g, j):
                t = g * G + j if isinstance(g, int) else None
                if gu and (t is None or t < SLOT_TILES):
                    gu(g, j)
                if turn_hidden and (t is None or 1 <= t <= SLOT_TILES):
                    turn_hidden(g, j - 1)
                if turn_x and (t is None or t + 1 < SLOT_TILES):
                    turn_x(g, j + 1)
                if down and (t is None or 2 <= t):
                    down(g, j - 2)

            if turn_x:
                turn_x(0, 0)
            for j in range(G):
                step(0, j)
            with eng.Fori(1, SLOT_GROUPS - 1) as g:
                for j in range(G):
                    step(g, j)
            for j in range(G + 2):
                step(SLOT_GROUPS - 1, j)

        d_start = [n + (b < 2) for b, n in enumerate(b_end)]

        block = ctx.enter_context(nc.Block())

        @block.sync
        def _(sp):
            def row(dst, src):
                sp.dma_start(dst, src.rearrange("(a n) -> a n", a=1).to_broadcast([P, src.shape[0]])
                             ).then_inc(weights_in, 16)
            sp.dma_start(tok_w[:], io["tok_w"].rearrange("(k p) n -> p k n", p=P)).then_inc(weights_in, 16)
            sp.dma_start(ln1_gb[:, 0, :], io["ln1_g"]).then_inc(weights_in, 16)
            sp.dma_start(ln1_gb[:, 1, :], io["ln1_b"]).then_inc(weights_in, 16)
            row(tok_b[:], io["tok_b"])
            row(ln2_g[:], io["ln2_g"])
            row(ln2_b[:], io["ln2_b"])
            row(proj_b[:], io["proj_b"])
            sp.dma_start(qkv_w[:], io["qkv_w"].rearrange("(k p) n -> p k n", p=P)).then_inc(weights_in, 16)
            sp.dma_start(qkv_b[:], io["qkv_b"]).then_inc(weights_in, 16)
            sp.dma_start(proj_w[:], io["proj_w"].rearrange("(k p) n -> p k n", p=P)).then_inc(weights_in, 16)

            sp.dma_start(fc1_w[:].bitcast(I32), io["fc1_q"].rearrange("(k p) n -> p k n", p=P)).then_inc(quant_in, 16)
            sp.dma_start(fc2_w[:].bitcast(I32), io["fc2_q"].rearrange("(k p) n -> p k n", p=P)).then_inc(quant_in, 16)
            for dst, src in ((sh_gu, io["fc1_s"]), (uv_w, io["fc2_s"])):
                sp.dma_start(dst[:].rearrange("p k n -> p (k n)"), src.rearrange("k n -> (k n)")
                             .rearrange("(a n) -> a n", a=1).to_broadcast([P, 2 * F0])).then_inc(quant_in, 16)

            def b_row(dst, src):
                sp.dma_start(dst, src.rearrange("(a n) -> a n", a=1).to_broadcast([P, src.shape[0]])
                             ).then_inc(b_weights_in, 16)
            sp.dma_start(router_b[:], io["router_b"].rearrange("(a n) -> a n", a=1).to_broadcast([P, EXPERTS])
                         ).then_inc(router_b_in, 16)
            sp.wait_ge(c_consts, 6)
            sp.dma_start(xm_dram[TOKENS:, :], zeros[:]).then_inc(zeros_stored, 16)
            sp.dma_start(out[TOKENS:, :], zeros[:]).then_inc(zeros_stored, 16)
            b_row(fc2_b[:], io["fc2_b"])
            b_row(uv_b[:], io["uv_b"])
            b_row(o_b[:], io["o_b"])
            sp.dma_start(fc1_b[:], io["fc1_b"]).then_inc(b_weights_in, 16)
            sp.dma_start(ln3_gb[:, 0, :], io["ln3_g"]).then_inc(b_weights_in, 16)
            sp.dma_start(ln3_gb[:, 1, :], io["ln3_b"]).then_inc(b_weights_in, 16)
            sp.wait_ge(mix_zeroed, 1)
            for i in range(2):
                sp.dma_start(mix_w[64 * i:64 * i + 64, :, 64 * i:64 * i + 64], io["mix"]).then_inc(b_weights_in, 16)
            sp.dma_start(o_w[:], io["o_w"].rearrange("(k p) n -> p k n", p=P)).then_inc(b_weights_in, 16)
            sp.dma_start(router_w[:], io["router_w"].rearrange("(k p) n -> p k n", p=P)).then_inc(b_weights_in, 16)
            sp.dma_start(sh_d[:], io["sh_d"].rearrange("(k p) n -> p k n", p=P)).then_inc(b_weights_in, 16)
            sp.wait_ge(dequantised, 4)
            sp.dma_start(sh_gu[:], io["sh_gu"].rearrange("(k p) n -> p k n", p=P)).then_inc(b_weights_in, 16)
            sp.dma_start(uv_w[:], io["uv_w"].rearrange("(k p) n -> p k n", p=P)).then_inc(b_weights_in, 16)

            with sp.Fori(0, GROUPS) as g:
                for j in range(G):
                    sp.wait_ge(xn_done, g * G)
                    sp.dma_start(x_in[:, j, :], io["x"][bass.ds((g * G + j) * P, P), :]).then_inc(x_loaded[j], 16)

            h1_by_patch = h1_dram.rearrange("(i b) d -> b i d", b=PATCHES)
            xm_by_patch = xm_dram[0:TOKENS, :].rearrange("(i b) d -> b i d", b=PATCHES)
            out_by_patch = out[0:TOKENS, :].rearrange("(i b) d -> b i d", b=PATCHES)
            for j in range(G):
                sp.wait_ge(h1_stored[j], 16 * GROUPS)
            sp.wait_ge(h1_done, TILES)
            sp.dma_start(expert_gu[:], io["expert_gu"].rearrange("e (k p) n -> p e k n", p=P)).then_inc(experts_in, 16)
            sp.dma_start(expert_d[:], io["expert_d"].rearrange("e (k p) n -> p e k n", p=P)).then_inc(experts_in, 16)
            with sp.Fori(0, GROUPS) as g:
                for j in range(G):
                    sp.wait_ge(h4_stored[j], g * 32)
                    for i in range(2):
                        sp.dma_start(res[64 * i:64 * i + 64, j, :],
                                     h1_by_patch[bass.ds(g * (2 * G) + (2 * j + i), 1), :, :]
                                     .rearrange("b i d -> (b i) d")).then_inc(h_loaded[j], 16)
                for j in range(G):
                    sp.wait_ge(xm_done, g * G + j + 1)
                    for i in range(2):
                        sp.dma_start(xm_by_patch[bass.ds(g * (2 * G) + (2 * j + i), 1), :, :]
                                     .rearrange("b i d -> (b i) d"), nrm[64 * i:64 * i + 64, j, :]
                                     ).then_inc(xm_stored[j], 16)
                for j in range(G):
                    b = bb.bank("down", j)
                    sp.wait_ge(read[b], bb.made(g, "down", j))
                    for i in range(2):
                        sp.dma_start(out_by_patch[bass.ds(g * (2 * G) + (2 * j + i), 1), :, :]
                                     .rearrange("b i d -> (b i) d"), res[64 * i:64 * i + 64, j, :]
                                     ).then_inc(h4_stored[j], 16)
            for j in range(G):
                sp.wait_ge(h4_stored[j], 32 * GROUPS)
                sp.wait_ge(xm_stored[j], 32 * GROUPS)

            sp.wait_ge(slots_scattered, 16 * TILES * TOP)
            sp.dma_start(slots[:], slots_dram.rearrange("(p t) c -> p t c", p=P)).then_inc(slots_in, 16)

        @block.gpsimd
        def _(pool):
            pool.memset(mix_w[:], 0.0).then_inc(mix_zeroed, 1)
            pool.memset(ident[:], 0.0).then_inc(setup, 1)
            pool.memset(one_col[:], 1.0).then_inc(setup, 1)
            pool.memset(eps_col[:], EPS).then_inc(setup, 1)
            pool.memset(mhalf_col[:], -0.5).then_inc(setup, 1)
            pool.memset(head_parity4[:], 1.0).then_inc(setup, 1)
            pool.memset(copy_parity[:], 1.0).then_inc(setup, 1)
            pool.wait_ge(setup, 6)
            pool.affine_select(out=ident[:], in_=ident[:], compare_op=ALU.not_equal, fill=1.0, base=0,
                               pattern=[[-1, P]], channel_multiplier=1).then_inc(setup, 1)
            pool.affine_select(out=head_parity4[:], in_=head_parity4[:], compare_op=ALU.is_ge, fill=0.0, base=0,
                               pattern=[[-32, 4], [-16, 2]], channel_multiplier=1).then_inc(setup, 1)
            pool.affine_select(out=copy_parity[:], in_=copy_parity[:], compare_op=ALU.is_ge, fill=0.0, base=0,
                               pattern=[[-64, 2]], channel_multiplier=1).then_inc(setup, 1)
            pool.wait_ge(setup, 9)
            pool.affine_select(out=head_parity4[:], in_=head_parity4[:], compare_op=ALU.is_ge, fill=0.0, base=15,
                               pattern=[[32, 4], [16, 2]], channel_multiplier=-1).then_inc(setup, 1)
            pool.affine_select(out=copy_parity[:], in_=copy_parity[:], compare_op=ALU.is_ge, fill=0.0, base=63,
                               pattern=[[64, 2]], channel_multiplier=-1).then_inc(setup, 1)

            pool.memset(ones[:], 1.0).then_inc(c_consts, 1)
            pool.memset(earlier[:], 1.0).then_inc(c_consts, 1)
            pool.memset(below_e[:], 1.0).then_inc(c_consts, 1)
            pool.memset(zeros[:], 0.0).then_inc(c_consts, 1)
            pool.wait_ge(c_consts, 4)
            pool.affine_select(out=earlier[:], in_=earlier[:], compare_op=ALU.is_gt, fill=0.0, base=0,
                               pattern=[[1, P]], channel_multiplier=-1).then_inc(c_consts, 1)
            pool.affine_select(out=below_e[:], in_=below_e[:], compare_op=ALU.is_gt, fill=0.0, base=0,
                               pattern=[[1, EXPERTS], [-1, EXPERTS]], channel_multiplier=0).then_inc(c_consts, 1)
            pool.memset(half_col[:], 0.5).then_inc(pool_setup, 1)
            pool.memset(one_neg[:], -1.0).then_inc(pool_setup, 1)
            pool.memset(tiny_col[:], 1e-8).then_inc(pool_setup, 1)

            pool.wait_ge(setup, 11)
            pool.wait_ge(weights_in, 16 * 10)
            chain = Chain(pool, pool_chain, 3 * G)

            def rstd(g, which, j, ready, count):
                pool.wait_ge(ready, count)
                chain.wait(chain.step(pool.tensor_tensor(ve[:, which, j:j + 1], mv[:, which, j, 1:2], eps_col[:],
                                                         ALU.add)))
                pool.tensor_tensor(rs[:, which, j:j + 1], ve[:, which, j:j + 1], mhalf_col[:],
                                   ALU.pow).then_inc(rstd_done, 1)

            with pool.Fori(0, GROUPS) as g:
                chain.turn(g)
                for j in range(G):
                    rstd(g, 0, j, x_stat, g * (3 * G) + j + 1)
                for j in range(G):
                    rstd(g, 1, j, x_stat, g * (3 * G) + G + 2 * j + 1)
                    rstd(g, 2, j, x_stat, g * (3 * G) + G + 2 * j + 2)
                    pool.wait_ge(an_done, g * G + j + 1)
                    pool.tensor_tensor(hp[:, j, :], h0[:, j, :], proj_b[:], ALU.add).then_inc(hp_done, 1)
                chain.end()

            pool.wait_ge(pool_setup, 3)
            pool.wait_ge(b_weights_in, 16 * 13)
            pool.tensor_tensor(fc2_b[:], fc2_b[:], half_col[:].to_broadcast([P, DIM]), ALU.mult).then_inc(pool_setup, 1)
            pool.wait_ge(pool_setup, 4)
            chain = Chain(pool, pool_chain_b, 16 * G)

            def tt(out, a, b, op):
                chain.wait(chain.step(pool.tensor_tensor(out, a, b, op)))

            with pool.Fori(0, GROUPS) as g:
                chain.turn(g)
                for j in range(G):
                    t, r1, r2 = ve[:, 0, j:j + 1], rs[:, 0, j:j + 1], rs[:, 1, j:j + 1]
                    pool.wait_ge(b_var, g * (3 * G) + j + 1)
                    tt(t, mv[:, 0, j, 1:2], eps_col[:], ALU.add)
                    tt(r1, t, mhalf_col[:], ALU.pow)
                    tt(t, mv[:, 0, j, 1:2], r1, ALU.mult)
                    tt(t, t, r1, ALU.mult)
                    tt(t, t, eps_col[:], ALU.add)
                    tt(r2, t, mhalf_col[:], ALU.pow)
                    pool.tensor_tensor(r2, r2, r1, ALU.mult).then_inc(b_scales, 1)
                for j in range(G):
                    pool.wait_ge(n1_done, g * G + j + 1)
                    pool.wait_ge(n2_done, g * G + j + 1)
                    tt(res[:, j, :], res[:, j, :], nrm[:, j, :], ALU.add)
                    pool.tensor_tensor(res[:, j, :], res[:, j, :], fc2_b[:], ALU.add).then_inc(res1_done, 1)
                for j in range(G):
                    t, r1, r2 = ve[:, 1, j:j + 1], rs[:, 0, j:j + 1], rs[:, 1, j:j + 1]
                    pool.wait_ge(b_var, g * (3 * G) + G + j + 1)
                    tt(t, mv[:, 1, j, 1:2], eps_col[:], ALU.add)
                    tt(r1, t, mhalf_col[:], ALU.pow)
                    tt(t, mv[:, 1, j, 1:2], r1, ALU.mult)
                    tt(t, t, r1, ALU.mult)
                    tt(t, t, half_col[:], ALU.pow)
                    tt(t, t, tiny_col[:], ALU.add)
                    tt(r2, t, one_neg[:], ALU.pow)
                    pool.tensor_tensor(r2, r2, r1, ALU.mult).then_inc(b_scales, 1)
                    pool.wait_ge(qn_done, g * G + j + 1)
                    pool.wait_ge(xx_done, g * G + j + 1)
                    tt(res[:, j, :], res[:, j, :], nrm[:, j, :], ALU.add)
                    pool.tensor_tensor(res[:, j, :], res[:, j, :], o_b[:], ALU.add).then_inc(res2_done, 1)
                for j in range(G):
                    pool.wait_ge(b_var, g * (3 * G) + 2 * G + j + 1)
                    tt(ve[:, 2, j:j + 1], mv[:, 2, j, 1:2], eps_col[:], ALU.add)
                    pool.tensor_tensor(rs[:, 2, j:j + 1], ve[:, 2, j:j + 1], mhalf_col[:],
                                       ALU.pow).then_inc(b_scales, 1)
                chain.end()

            for j in range(G):
                pool.wait_ge(h4_stored[j], 32 * GROUPS)
            pool.iota(tile_start, pattern=[[P, SLOT_TILES]], base=0, channel_multiplier=0,
                      allow_small_or_imprecise_dtypes=True).then_inc(c_consts, 1)
            for i in range(2):
                pool.wait_ge(c_consts, 7 + i)
                pool.iota(token_row[64 * i:64 * i + 64, :], pattern=[[2, TILES]], base=i,
                          channel_multiplier=PATCHES, allow_small_or_imprecise_dtypes=True).then_inc(c_consts, 1)
            pool.wait_ge(c_consts, 9)
            pool.memset(slots_init[:, :, 1], 0.0).then_inc(c_consts, 1)
            pool.iota(slots_init[:, :, 0], pattern=[[0, SLOT_TILES]], base=TOKENS, channel_multiplier=1,
                      allow_small_or_imprecise_dtypes=True).then_inc(c_consts, 1)
            pool.wait_ge(c_consts, 11)
            pool.dma_start(slots_dram.rearrange("(p t) c -> p t c", p=P), slots_init).then_inc(slots_begun, 16)
            pool.wait_ge(slots_begun, 16)
            pool.wait_ge(recs_done, 3)
            chain = Chain(pool, pool_chain_c, 1)
            with pool.Fori(0, TILES) as t:
                chain.turn(t)
                pool.wait_ge(slots_scattered, t * (16 * TOP))
                pool.sem_inc(pool_fence, 1)
                chain.wait(chain.step(pool.tensor_copy(ring[:], recs[:, bass.ds(t, 1), :, :]
                                                       .rearrange("p t k c -> p (t k) c"))))
                pool.sem_inc(pool_fence, 1)
                for k in range(TOP):
                    pool.indirect_dma_start(
                        slots_dram, bass.IndirectOffsetOnAxis(ap=ring[:, k, 0:1], axis=0),
                        ring[:, k, 1:3].bitcast(F32), None).then_inc(slots_scattered, 16)
                chain.end()

            pool.wait_ge(rows_done, 1)
            pool.wait_ge(zeros_stored, 32)
            chain = Chain(pool, pool_chain_d, 2)

            def gather(g, j):
                pool.indirect_dma_start(xg[:, j, :], None, xm_dram,
                                        bass.IndirectOffsetOnAxis(ap=gather_rows[:, j:j + 1], axis=0)
                                        ).then_inc(gathered[j], 16)

            def add_out(g, j):
                pool.wait_ge(read[d_bank("down", j)], d_made(g, "down", j))
                pool.wait_ge(added[(j - 1) % G], g * 16 + (16 if j else 0))
                pool.sem_inc(pool_fence, 1)
                pool.indirect_dma_start(out, bass.IndirectOffsetOnAxis(ap=add_rows[:, j:j + 1], axis=0),
                                        y[:, j, :], None, compute_op=ALU.add).then_inc(added[j], 16)

            def rows_to(dst, g):
                return pool.tensor_copy(dst[:], slot_rows[:, bass.ds(g * G, G)])

            pool.tensor_copy(gather_rows[:], slot_rows[:, 0:G]).then_inc(rows_done, 1)
            pool.wait_ge(rows_done, 2)
            for j in range(G):
                gather(0, j)
            with pool.Fori(0, SLOT_GROUPS - 1) as g:
                chain.turn(g)
                for j in range(G):
                    pool.wait_ge(gathered[j], g * 16 + 16)
                pool.sem_inc(pool_fence, 1)
                chain.step(rows_to(gather_rows, g + 1))
                for j in range(G):
                    pool.wait_ge(added[j], g * 16)
                pool.sem_inc(pool_fence, 1)
                chain.wait(chain.step(rows_to(add_rows, g)))
                for j in range(G):
                    pool.wait_ge(written[d_bank("xgT", j)], d_made(g, "xgT", j))
                    pool.sem_inc(pool_fence, 1)
                    gather(g + 1, j)
                    add_out(g, j)
                chain.end()
            g = SLOT_GROUPS - 1
            pool.wait_ge(added[G - 1], 16 * g)
            chain.turn(g)
            chain.wait(chain.step(pool.tensor_copy(add_rows[:], slot_rows[:, g * G:(g + 1) * G])))
            for j in range(G):
                add_out(g, j)
            pool.wait_ge(added[G - 1], 16 * SLOT_GROUPS)

        @block.scalar
        def _(act):
            act.wait_ge(consts_done, 2)
            act.wait_ge(weights_in, 16 * 10)
            with act.Fori(0, GROUPS) as g:
                for j in range(G):
                    act.wait_ge(xnT_mm, g * G + j + 1)
                    for k in range(KX):
                        ins = act.activation(x_nT[:, j, k, :], ps_t[:, k // 4, (k % 4) * P:(k % 4 + 1) * P],
                                             ACT.Identity, scale=ln1_gb[:, 0, k:k + 1], bias=ln1_gb[:, 1, k:k + 1])
                    ins.then_inc(xnT_done, 1)
                for j in range(G):
                    act.wait_ge(anT_mm, g * G + j + 1)
                    src = ps_g[:, j % 2, 0:DIM].rearrange("p (a t) -> p a t", t=64)
                    act.activation(aT[:, j].rearrange("p k i c t -> p (k i) c t"),
                                   src.unsqueeze(2).to_broadcast([P, 2 * KD, 2, 64]), ACT.Copy).then_inc(aT_done, 1)
                for j in range(G):
                    act.wait_ge(qk_mm, g * G + j + 1)
                    for c in range(2):
                        act.activation(qT[:, j, c, :], ps_g[:, 0, c * P:(c + 1) * P], ACT.Identity,
                                       bias=qkv_b[:, c:c + 1])
                    for c in range(2):
                        for par in range(2):
                            ins = act.activation(kT[:, j, c, par, :], ps_g[:, 0, (2 + c) * P:(3 + c) * P],
                                                 ACT.Identity, scale=head_parity[:, par:par + 1],
                                                 bias=kb_par[:, c, par:par + 1])
                    ins.then_inc(qk_done, 1)
                def turned_out(j):
                    act.wait_ge(pT_mm, g * G + j + 1)
                    act.activation(pT[:, j % 2].rearrange("p a t -> p (a t)"),
                                   ps_t[:].rearrange("p b n -> p (b n)"), ACT.Copy).then_inc(pT_done, 1)

                for j in range(G):
                    act.wait_ge(s_sub, g * G + j + 1)
                    act.activation(e[:, j], e[:, j], ACT.Exp, scale=HD ** -0.5).then_inc(e_done, 1)
                    if j >= 1:
                        turned_out(j - 1)
                turned_out(G - 1)
                for j in range(G):
                    act.wait_ge(oT_mm, g * G + j + 1)
                    for k in range(KD):
                        ins = act.activation(oT[:, j, k, :], ps_g[:, j % 2, k * P:(k + 1) * P], ACT.Identity,
                                             bias=qkv_b[:, 4 + k:5 + k])
                    ins.then_inc(oT_done, 1)
                for j in range(G):
                    act.wait_ge(h1_done, g * G + j + 1)
                    act.dma_start(h1_dram[bass.ds((g * G + j) * P, P), :], h1[:, j, :]).then_inc(h1_stored[j], 16)
            for j in range(G):
                act.wait_ge(h1_stored[j], 16 * GROUPS)

            act.wait_ge(b_weights_in, 16 * 13)

            def turned(g, stage, j, affine=False):
                b = bb.bank(stage, j)
                act.wait_ge(written[b], bb.made(g, stage, j))
                dst = nT[:, :, j * P:(j + 1) * P]
                if affine:
                    for k in range(KD):
                        ins = act.activation(dst[:, k, :], ps[:, b, k * P:(k + 1) * P], ACT.Identity,
                                             scale=ln3_gb[:, 0, k:k + 1], bias=ln3_gb[:, 1, k:k + 1])
                else:
                    ins = act.activation(dst, ps[:, b, 0:DIM].rearrange("p (k t) -> p k t", k=KD), ACT.Copy)
                ins.then_inc(read[b], 1)

            with act.Fori(0, GROUPS) as g:
                for j in range(G):
                    turned(g, "n2T", j, affine=True)
                for c in range(K2):
                    b = bb.bank("fc1", c)
                    act.wait_ge(written[b], bb.made(g, "fc1", c))
                    act.activation(hidT[:, c, :], ps[:, b, :], ACT.Silu, bias=fc1_b[:, c:c + 1]).then_inc(read[b], 1)
                for j in range(G):
                    turned(g, "xxT", j)
                for j in range(G):
                    act.wait_ge(uvb_done, g * G + j + 1)
                    act.activation(uv[:, j, :], uv[:, j, :], ACT.Silu).then_inc(uv_done, 1)
                for j in range(G):
                    b = bb.bank("uyT", j)
                    act.wait_ge(written[b], bb.made(g, "uyT", j))
                    act.activation(uyT[:, j].rearrange("p k t -> p (k t)"), ps[:, b, :],
                                   ACT.Copy).then_inc(read[b], 1)
                for j in range(G):
                    turned(g, "xmT", j)
                for c in range(KS):
                    b = bb.bank("gate", c)
                    act.wait_ge(written[b], bb.made(g, "gate", c))
                    if c >= 2:
                        act.wait_ge(read[bb.bank("up", c - 2)], bb.made(g, "up", c - 2))
                    act.activation(sh_g[:, c % 2, :], ps[:, b, :], ACT.Silu).then_inc(read[b], 1)

            act.wait_ge(read[bb.bank("router", G - 1)], bb.made(GROUPS - 1, "router", G - 1))
            for j in range(G):
                act.wait_ge(h4_stored[j], 32 * GROUPS)
            act.activation(scores_sb, logits[:], ACT.Sigmoid).then_inc(scores_done, 1)

            def x_turned(g, j):
                b = d_bank("xgT", j)
                act.wait_ge(written[b], d_made(g, "xgT", j))
                act.activation(xgT[:, j % G].rearrange("p k t -> p (k t)"), ps[:, b, 0:DIM], ACT.Copy
                               ).then_inc(read[b], 1)

            def gated(g, j):
                b = d_bank("gu", j)
                act.wait_ge(written[b], d_made(g, "gu", j))
                act.activation(act_g[:, j % G, :], ps[:, b, 0:FE], ACT.Silu).then_inc(act_g_done, 1)

            def hidden_turned(g, j):
                b = d_bank("hT", j)
                act.wait_ge(written[b], d_made(g, "hT", j))
                act.activation(hT[:, j % G].rearrange("p k t -> p (k t)"), ps[:, b, 0:FE], ACT.Copy
                               ).then_inc(read[b], 1)

            d_steps(act, lambda g, j: gated(g, j), lambda g, j: hidden_turned(g, j), lambda g, j: x_turned(g, j), None)

        @block.vector
        def _(dve):
            dve.wait_ge(setup, 11)
            dve.tensor_reduce(head_parity[:], head_parity4[:].rearrange("p g c -> p c g"), AX.X,
                              ALU.add).then_inc(vec_setup, 1)
            dve.wait_ge(vec_setup, 1)
            dve.wait_ge(weights_in, 16 * 10)
            for c in range(2):
                dve.tensor_tensor(kb_par[:, c, :], head_parity[:], qkv_b[:, 2 + c:3 + c].to_broadcast([P, 2]),
                                  ALU.mult).then_inc(consts_done, 1)
            for j in range(G):
                for i in range(2):
                    dve.tensor_copy(vblk[:, j, i, :, :, HD], copy_parity[:].unsqueeze(1).to_broadcast([P, PAIRS, 2])
                                    ).then_inc(consts_done, 1)
            dve.wait_ge(quant_in, 64)
            for w in (fc1_w, fc2_w):
                dve.tensor_scalar(w[:], w[:].bitcast(I32), -128.0, None, ALU.add).then_inc(dequantised, 1)
            dve.wait_ge(dequantised, 2)
            for w, scales in ((fc1_w, sh_gu), (fc2_w, uv_w)):
                flat = w[:].rearrange("p k n -> p (k n)")
                dve.tensor_tensor(flat, flat, scales[:].rearrange("p k n -> p (k n)"), ALU.mult
                                  ).then_inc(dequantised, 1)
            chain = Chain(dve, vec_chain, 9 * G)

            def moments(src, n, st, out):
                parts = (n + 511) // 512
                for i in range(parts):
                    last = chain.step(dve.bn_stats(st[:, 6 * i:6 * i + 6], src[:, i * n // parts:(i + 1) * n // parts]))
                chain.wait(last)
                dve.sem_inc(vec_fence, 1)
                dve.bn_aggr(out, st[:, 0:6 * parts]).then_inc(x_stat, 1)

            with dve.Fori(0, GROUPS) as g:
                chain.turn(g)
                for j in range(G):
                    dve.wait_ge(x_loaded[j], g * 16 + 16)
                    moments(x_in[:, j, :], PIX, stats[:, j, :], mv[:, 0, j, :])
                for j in range(G):
                    dve.wait_ge(rstd_done, g * (3 * G) + j + 1)
                    dve.tensor_scalar(x_n[:, j, :], x_in[:, j, :], mv[:, 0, j, 0:1], rs[:, 0, j:j + 1],
                                      ALU.subtract, ALU.mult).then_inc(xn_done, 1)
                for j in range(G):
                    dve.wait_ge(tok_mm, g * G + j + 1)
                    dve.tensor_tensor(t_lin[:, j, :], ps_g[:, j % 2, 0:DIM], tok_b[:], ALU.add).then_inc(tok_free, 1)
                    dve.wait_ge(tok_free, g * G + j + 1)
                    moments(t_lin[:, j, :], DIM, stats2[:, j, :], mv[:, 1, j, :])
                    dve.wait_ge(rstd_done, g * (3 * G) + G + 2 * j + 1)
                    chain.wait(chain.step(dve.tensor_scalar(
                        h0[:, j, :], t_lin[:, j, :], mv[:, 1, j, 0:1], rs[:, 1, j:j + 1], ALU.subtract, ALU.mult)))
                    chain.wait(chain.step(dve.tensor_tensor(h0[:, j, :], h0[:, j, :], ln2_g[:], ALU.mult)))
                    chain.wait(chain.step(dve.tensor_tensor(h0[:, j, :], h0[:, j, :], ln2_b[:], ALU.add)))
                    moments(h0[:, j, :], DIM, stats3[:, j, :], mv[:, 2, j, :])
                    dve.wait_ge(rstd_done, g * (3 * G) + G + 2 * j + 2)
                    dve.tensor_scalar(a_n[:, j, :], h0[:, j, :], mv[:, 2, j, 0:1], rs[:, 2, j:j + 1],
                                      ALU.subtract, ALU.mult).then_inc(an_done, 1)
                for j in range(G):
                    dve.wait_ge(v_mm, g * G + j + 1)
                    dve.tensor_tensor(
                        vblk[:, j, :, :, :, 0:HD].rearrange("p i a c d -> p (i a) c d"),
                        ps_g[:, 1, :].rearrange("p (a c d) -> p a c d", c=2, d=HD),
                        copy_parity[:].unsqueeze(1).unsqueeze(3).to_broadcast([P, 2 * PAIRS, 2, HD]),
                        ALU.mult).then_inc(v_done, 1)
                def normalise(j):
                    dve.wait_ge(pv_mm, g * G + j + 1)
                    pv = ps_g[:, j % 2, 0:HEADS * (HD + 1)].rearrange("p (h d) -> p h d", d=HD + 1)
                    chain.wait(chain.step(dve.reciprocal(rsum[:, j, :], pv[:, :, HD])))
                    dve.tensor_tensor(o_n[:, j, :].rearrange("p (h d) -> p h d", d=HD), pv[:, :, 0:HD],
                                      rsum[:, j, :].unsqueeze(2).to_broadcast([P, HEADS, HD]),
                                      ALU.mult).then_inc(o_done, 1)

                for j in range(G):
                    dve.wait_ge(s_mm, g * G + j + 1)
                    half = ps_s[:, :, 0:256].rearrange("p g (a m) -> p g a m", m=64)
                    chain.wait(chain.step(dve.tensor_reduce(smax[:, j, :].rearrange("p (g a) -> p g a", g=4), half,
                                                            AX.X, ALU.max)))
                    dve.tensor_tensor(e[:, j].rearrange("p (g a) m -> p g a m", g=4), half,
                                      smax[:, j, :].rearrange("p (g a) -> p g a", g=4).unsqueeze(3)
                                      .to_broadcast([P, 4, 4, 64]), ALU.subtract).then_inc(s_sub, 1)
                    if j >= 1:
                        normalise(j - 1)
                normalise(G - 1)
                for j in range(G):
                    dve.wait_ge(proj_mm, g * G + j + 1)
                    dve.wait_ge(hp_done, g * G + j + 1)
                    dve.wait_ge(h1_stored[j], g * 16)
                    dve.tensor_tensor(h1[:, j, :], ps_g[:, j % 2, 0:DIM], hp[:, j, :], ALU.add).then_inc(h1_done, 1)
                chain.end()

            chain = Chain(dve, vec_chain_b, 3 * G)

            def b_moments(src, st, out):
                chain.wait(chain.step(dve.bn_stats(st, src)))
                dve.sem_inc(vec_fence, 1)
                dve.bn_aggr(out, st).then_inc(b_var, 1)

            def normed(out, which, j, r):
                return dve.tensor_scalar(out, res[:, j, :], mv[:, which, j, 0:1], r, ALU.subtract, ALU.mult)

            def mix_in(g, j):
                dve.wait_ge(b_scales, g * (3 * G) + G + j + 1)
                normed(nrm[:, j, :], 1, j, rs[:, 0, j:j + 1]).then_inc(qn_done, 1)
                normed(lin_in[:, j, :], 1, j, rs[:, 1, j:j + 1]).then_inc(xx_done, 1)

            def moe_in(g, j):
                dve.wait_ge(b_scales, g * (3 * G) + 2 * G + j + 1)
                normed(nrm[:, j, :], 2, j, rs[:, 2, j:j + 1]).then_inc(xm_done, 1)

            dve.wait_ge(b_weights_in, 16 * 13)
            with dve.Fori(0, GROUPS) as g:
                chain.turn(g)
                for j in range(G):
                    dve.wait_ge(h_loaded[j], g * 32 + 32)
                    b_moments(res[:, j, :], stats2[:, j, :], mv[:, 0, j, :])
                for j in range(G):
                    dve.wait_ge(xm_stored[j], g * 32)
                    dve.wait_ge(b_scales, g * (3 * G) + j + 1)
                    normed(nrm[:, j, :], 0, j, rs[:, 0, j:j + 1]).then_inc(n1_done, 1)
                    normed(lin_in[:, j, :], 0, j, rs[:, 1, j:j + 1]).then_inc(n2_done, 1)
                for j in range(G):
                    b = bb.bank("fc2", j)
                    dve.wait_ge(written[b], bb.made(g, "fc2", j))
                    dve.wait_ge(res1_done, g * G + j + 1)
                    dve.scalar_tensor_tensor(out=res[:, j, :], in0=ps[:, b, 0:DIM], scalar=0.5, in1=res[:, j, :],
                                             op0=ALU.mult, op1=ALU.add).then_inc(read[b], 1)
                    dve.wait_ge(read[b], bb.made(g, "fc2", j))
                    b_moments(res[:, j, :], stats3[:, j, :], mv[:, 1, j, :])
                    if j >= 1:
                        mix_in(g, j - 1)
                mix_in(g, G - 1)
                for j in range(G):
                    for h, stage in enumerate(("u", "v")):
                        b = bb.bank(stage, j)
                        dve.wait_ge(written[b], bb.made(g, stage, j))
                        ins = dve.tensor_tensor(uv[:, j, h * GF:(h + 1) * GF], ps[:, b, :], uv_b[:, h * GF:(h + 1) * GF],
                                                ALU.add)
                        ins.then_inc(read[b], 1)
                    dve.wait_ge(read[b], bb.made(g, "v", j))
                    dve.sem_inc(uvb_done, 1)
                for j in range(G):
                    b = bb.bank("mix", j)
                    dve.wait_ge(written[b], bb.made(g, "mix", j))
                    dve.tensor_tensor(uv[:, j, 0:GF], uv[:, j, 0:GF], ps[:, b, :], ALU.mult).then_inc(read[b], 1)
                for j in range(G):
                    b = bb.bank("o", j)
                    dve.wait_ge(written[b], bb.made(g, "o", j))
                    dve.wait_ge(res2_done, g * G + j + 1)
                    dve.tensor_tensor(res[:, j, :], ps[:, b, 0:DIM], res[:, j, :], ALU.add).then_inc(read[b], 1)
                    dve.wait_ge(read[b], bb.made(g, "o", j))
                    b_moments(res[:, j, :], stats3[:, j, :], mv[:, 2, j, :])
                    if j >= 1:
                        moe_in(g, j - 1)
                moe_in(g, G - 1)
                for j in range(G):
                    b = bb.bank("router", j)
                    dve.wait_ge(written[b], bb.made(g, "router", j))
                    dve.tensor_copy(logits[:, bass.ds(g * G + j, 1), :], ps[:, b, 0:EXPERTS].unsqueeze(1)
                                    ).then_inc(read[b], 1)
                for c in range(KS):
                    b = bb.bank("up", c)
                    dve.wait_ge(written[b], bb.made(g, "up", c))
                    dve.wait_ge(read[bb.bank("gate", c)], bb.made(g, "gate", c))
                    dve.tensor_tensor(shT[:, c, :], sh_g[:, c % 2, :], ps[:, b, :], ALU.mult).then_inc(read[b], 1)
                for j in range(G):
                    b = bb.bank("down", j)
                    dve.wait_ge(written[b], bb.made(g, "down", j))
                    dve.tensor_tensor(res[:, j, :], ps[:, b, 0:DIM], res[:, j, :], ALU.add).then_inc(read[b], 1)
                chain.end()

            cn = [0]

            def do(ins):
                cn[0] += 1
                ins.then_inc(vec_chain_c, 1)
                dve.wait_ge(vec_chain_c, cn[0])

            dve.wait_ge(scores_done, 1)
            dve.wait_ge(c_consts, 11)
            dve.wait_ge(router_b_in, 16)
            dve.wait_ge(slots_begun, 16)
            over_tiles = [P, TILES, EXPERTS]
            do(dve.tensor_tensor(biased, scores_sb, router_b[:].unsqueeze(1).to_broadcast(over_tiles), ALU.add))
            s4 = biased.rearrange("p t (g o) -> p (t g) o", o=OF_GROUP)
            do(dve.tensor_tensor(pair_sums[:, :, 0:3], s4[:, :, 0:3], s4[:, :, 1:4], ALU.add))
            do(dve.tensor_tensor(pair_sums[:, :, 3:5], s4[:, :, 0:2], s4[:, :, 2:4], ALU.add))
            do(dve.tensor_tensor(pair_sums[:, :, 5:6], s4[:, :, 0:1], s4[:, :, 3:4], ALU.add))
            do(dve.tensor_reduce(g_score.rearrange("p t g -> p (t g)"), pair_sums, AX.X, ALU.max))

            def ranks(out, v, tiles, n, a, b):
                shape = [P, tiles, n, n]
                mine, others = v.unsqueeze(3).to_broadcast(shape), v.unsqueeze(2).to_broadcast(shape)
                tri = below_e[:, 0:n, 0:n].unsqueeze(1).to_broadcast(shape)
                do(dve.tensor_tensor(b, others, mine, ALU.is_equal))
                do(dve.tensor_tensor(b, b, tri, ALU.mult))
                do(dve.tensor_tensor(a, others, mine, ALU.is_gt))
                do(dve.tensor_tensor(a, a, b, ALU.add))
                do(dve.tensor_reduce(out, a, AX.X, ALU.add))

            def part(x, tiles, n):
                return x.rearrange("p a b c -> p (a b c)")[:, 0:tiles * n * n].rearrange(
                    "p (t a b) -> p t a b", t=tiles, a=n)

            ranks(g_rank, g_score, TILES, EXPERT_GROUPS, part(cmp_a, TILES, EXPERT_GROUPS),
                  part(cmp_b, TILES, EXPERT_GROUPS))
            do(dve.tensor_scalar(g_rank, g_rank, float(TOP_GROUPS), None, ALU.is_lt))
            do(dve.tensor_scalar(g_less, g_rank, -1.0, None, ALU.add))
            per_group = [P, TILES * EXPERT_GROUPS, OF_GROUP]
            m4 = masked.rearrange("p t (g o) -> p (t g) o", o=OF_GROUP)
            do(dve.tensor_tensor(m4, s4, g_rank.rearrange("p t g -> p (t g)").unsqueeze(2).to_broadcast(per_group),
                                 ALU.mult))
            do(dve.tensor_tensor(m4, m4, g_less.rearrange("p t g -> p (t g)").unsqueeze(2).to_broadcast(per_group),
                                 ALU.add))
            for t in range(0, TILES, 8):
                ranks(rank_e[:, t:t + 8, :], masked[:, t:t + 8, :], 8, EXPERTS, cmp_a, cmp_b)
            dve.tensor_scalar(taken, rank_e, float(TOP), None, ALU.is_lt).then_inc(taken_done, 1)
            dve.wait_ge(taken_done, 1)
            do(dve.tensor_tensor(tw, scores_sb, taken, ALU.mult))
            do(dve.tensor_reduce(w_sum, tw, AX.X, ALU.add))
            do(dve.tensor_scalar(w_sum, w_sum, 1e-20, None, ALU.add))
            do(dve.reciprocal(w_sum, w_sum))
            do(dve.scalar_tensor_tensor(out=tw, in0=tw, scalar=ROUTE_SCALE, in1=w_sum.unsqueeze(2)
                                        .to_broadcast(over_tiles), op0=ALU.mult, op1=ALU.mult))
            dve.wait_ge(written[1], b_end[1] + 1)
            flat = "p t e -> p (t e)"
            dve.tensor_copy(totals.rearrange(flat), ps[:, 1, :]).then_inc(read[1], 1)
            dve.wait_ge(read[1], b_end[1] + 1)
            src, dst = totals, cum_a
            for d in (1, 2, 4, 8, 16):
                do(dve.tensor_copy(dst[:, 0:d, :], src[:, 0:d, :]))
                do(dve.tensor_tensor(dst[:, d:, :], src[:, d:, :], src[:, 0:TILES - d, :], ALU.add))
                src, dst = dst, (cum_b if dst is cum_a else cum_a)
            cum = src
            do(dve.tensor_scalar(padded, cum[:, TILES - 1, :], float(P - 1), None, ALU.add))
            do(dve.tensor_copy(ends_a.bitcast(I32), padded))
            do(dve.tensor_scalar(ends_a.bitcast(I32), ends_a.bitcast(I32), 7, 7, ALU.logical_shift_right,
                                 ALU.logical_shift_left))
            do(dve.tensor_copy(padded, ends_a.bitcast(I32)))
            src, dst = padded, ends_a
            for d in (1, 2, 4, 8):
                do(dve.tensor_copy(dst[:, 0:d], src[:, 0:d]))
                do(dve.tensor_tensor(dst[:, d:], src[:, d:], src[:, 0:EXPERTS - d], ALU.add))
                src, dst = dst, (ends_b if dst is ends_a else ends_a)
            ends = src
            do(dve.tensor_tensor(base, ends, padded, ALU.subtract))
            for t in range(0, SLOT_TILES, P):
                n = min(P, SLOT_TILES - t)
                shape = [P, n, EXPERTS]
                do(dve.tensor_tensor(cmp_b.rearrange("p a b c -> p (a b c)")[:, 0:n * EXPERTS]
                                     .rearrange("p (t e) -> p t e", e=EXPERTS),
                                     ends.unsqueeze(1).to_broadcast(shape),
                                     tile_start[:, t:t + n].unsqueeze(2).to_broadcast(shape), ALU.is_le))
                do(dve.tensor_reduce(tile_e[:, t:t + n], cmp_b.rearrange("p a b c -> p (a b c)")[:, 0:n * EXPERTS]
                                     .rearrange("p (t e) -> p t e", e=EXPERTS), AX.X, ALU.add))
            do(dve.tensor_scalar(tile_e, tile_e, float(EXPERTS - 1), None, ALU.min))
            dve.tensor_copy(tile_expert[:], tile_e).then_inc(experts_known, 1)
            do(dve.tensor_tensor(cum, cum, totals, ALU.subtract))
            do(dve.tensor_tensor(cum, cum, base.unsqueeze(1).to_broadcast(over_tiles), ALU.add))
            dve.wait_ge(written[0], b_end[0] + 1)
            dve.tensor_tensor(slot_no.rearrange(flat), ps[:, 0, :], cum.rearrange(flat), ALU.add).then_inc(read[0], 1)
            dve.wait_ge(read[0], b_end[0] + 1)
            for k in range(TOP):
                for what, to in ((slot_no, choice_slot), (tw, choice_w)):
                    do(dve.scalar_tensor_tensor(out=picked, in0=rank_e, scalar=float(k), in1=what,
                                                op0=ALU.is_equal, op1=ALU.mult))
                    do(dve.tensor_reduce(to[:, :, k], picked, AX.X, ALU.add))
            do(dve.tensor_copy(choice_tile.bitcast(I32), choice_slot))
            do(dve.tensor_scalar(choice_tile.bitcast(I32), choice_tile.bitcast(I32), 7, None,
                                 ALU.logical_shift_right))
            do(dve.tensor_copy(choice_at, choice_tile.bitcast(I32)))
            do(dve.tensor_scalar(choice_at, choice_at, float(1 - P * SLOT_TILES), None, ALU.mult))
            do(dve.scalar_tensor_tensor(out=choice_at, in0=choice_slot, scalar=float(SLOT_TILES), in1=choice_at,
                                        op0=ALU.mult, op1=ALU.add))
            dve.tensor_copy(recs[:, :, :, 0], choice_at).then_inc(recs_done, 1)
            recs_f = recs[:].bitcast(F32)
            dve.tensor_copy(recs_f[:, :, :, 1], token_row.unsqueeze(2).to_broadcast([P, TILES, TOP])
                            ).then_inc(recs_done, 1)
            dve.tensor_copy(recs_f[:, :, :, 2], choice_w).then_inc(recs_done, 1)
            dve.wait_ge(slots_in, 16)
            dve.tensor_copy(slot_rows[:], slots[:, :, 0]).then_inc(rows_done, 1)

            def hidden(g, j):
                b = d_bank("gu", j)
                dve.wait_ge(act_g_done, g * G + (j + 1))
                dve.tensor_tensor(hid[:, j % G, :], act_g[:, j % G, :], ps[:, b, FE:2 * FE], ALU.mult
                                  ).then_inc(read[b], 1)

            def weighed(g, j):
                b = d_bank("down", j)
                dve.wait_ge(written[b], d_made(g, "down", j))
                if j >= 0:
                    dve.wait_ge(added[j], g * 16)
                else:
                    dve.wait_ge(added[j % G], g * 16 - 16)
                dve.tensor_scalar(y[:, j % G, :], ps[:, b, 0:DIM], slots[:, bass.ds(g * G + j, 1), 1]
                                  if not isinstance(g, int) else slots[:, g * G + j, 1:2], None, ALU.mult
                                  ).then_inc(read[b], 1)

            d_steps(dve, hidden, None, None, weighed)

        @block.tensor
        def _(pe):
            pe.wait_ge(consts_done, 2 + 2 * G)
            pe.wait_ge(weights_in, 16 * 10)

            def patches_out(g, j):
                pe.wait_ge(xnT_done, g * G + j + 1)
                if j < 2:
                    pe.wait_ge(h1_done, g * G)
                else:
                    pe.wait_ge(tok_free, g * G + j - 1)
                for k in range(KX):
                    ins = pe.matmul(ps_g[:, j % 2, 0:DIM], x_nT[:, j, k, :], tok_w[:, k, :],
                                    start=(k == 0), stop=(k == KX - 1))
                ins.then_inc(tok_mm, 1)

            def heads_out(g, j):
                pe.wait_ge(pT_done, g * G + j + 1)
                if j >= 2:
                    pe.wait_ge(o_done, g * G + j - 1)
                else:
                    pe.wait_ge(v_done, g * G + G)
                for i in range(2):
                    for a in range(PAIRS):
                        ins = pe.matmul(ps_g[64 * i:64 * i + 64, j % 2, a * 34:a * 34 + 34],
                                        pT[:, j % 2, a, 64 * i:64 * i + 64],
                                        vblk[:, j, i, a].rearrange("p c d -> p (c d)"), start=True, stop=True)
                ins.then_inc(pv_mm, 1)

            def scores(g, j):
                pe.wait_ge(qk_done, g * G + j + 1)
                if j >= 1:
                    pe.wait_ge(s_sub, g * G + j)
                for c in range(2):
                    for i in range(2):
                        for r in range(4):
                            ins = pe.matmul(ps_s[64 * i:64 * i + 64, r, c * P:(c + 1) * P],
                                            qT[32 * r:32 * r + 32, j, c, 64 * i:64 * i + 64],
                                            kT[32 * r:32 * r + 32, j, c, :, 64 * i:64 * i + 64],
                                            start=True, stop=True)
                ins.then_inc(s_mm, 1)

            def probs_turned(g, j):
                pe.wait_ge(e_done, g * G + j + 1)
                if j >= 1:
                    pe.wait_ge(pT_done, g * G + j)
                for a in range(PAIRS):
                    ins = pe.transpose(ps_t[:, a // 4, (a % 4) * P:(a % 4 + 1) * P],
                                       e[:, j, 2 * a:2 * a + 2].rearrange("p c m -> p (c m)"), ident[:])
                ins.then_inc(pT_mm, 1)

            with pe.Fori(0, GROUPS) as g:
                for j in range(G):
                    pe.wait_ge(xn_done, g * G + j + 1)
                    if j >= 1:
                        pe.wait_ge(xnT_done, g * G + j)
                    for k in range(KX):
                        ins = pe.transpose(ps_t[:, k // 4, (k % 4) * P:(k % 4 + 1) * P],
                                           x_n[:, j, k * P:(k + 1) * P], ident[:])
                    ins.then_inc(xnT_mm, 1)
                    if j >= 1:
                        patches_out(g, j - 1)
                patches_out(g, G - 1)
                for j in range(G):
                    pe.wait_ge(an_done, g * G + j + 1)
                    if j >= 2:
                        pe.wait_ge(aT_done, g * G + j - 1)
                    else:
                        pe.wait_ge(tok_free, g * G + j + 3)
                    for k in range(KD):
                        ins = pe.transpose(ps_g[:, j % 2, k * P:(k + 1) * P], a_n[:, j, k * P:(k + 1) * P], ident[:])
                    ins.then_inc(anT_mm, 1)
                for j in range(G):
                    if j >= 1:
                        pe.wait_ge(qk_done, g * G + j)
                    else:
                        pe.wait_ge(aT_done, g * G + G)
                    for c in range(4):
                        for k in range(KD):
                            ins = pe.matmul(ps_g[:, 0, c * P:(c + 1) * P], qkv_w[:, k, c * P:(c + 1) * P],
                                            aT[:, j, k, :, 0, :], start=(k == 0), stop=(k == KD - 1))
                    ins.then_inc(qk_mm, 1)
                    if j >= 1:
                        pe.wait_ge(v_done, g * G + j)
                    for i in range(2):
                        for k in range(KD):
                            ins = pe.matmul(ps_g[:, 1, i * DIM:(i + 1) * DIM],
                                            aT[:, j, k, i].rearrange("p c t -> p (c t)"),
                                            qkv_w[:, k, 2 * DIM:3 * DIM], start=(k == 0), stop=(k == KD - 1))
                    ins.then_inc(v_mm, 1)
                for j in range(G):
                    scores(g, j)
                    if j >= 1:
                        probs_turned(g, j - 1)
                        heads_out(g, j - 1)
                probs_turned(g, G - 1)
                heads_out(g, G - 1)
                for j in range(G):
                    pe.wait_ge(o_done, g * G + (j + 3 if j < 2 else j + 1))
                    if j >= 2:
                        pe.wait_ge(oT_done, g * G + j - 1)
                    for k in range(KD):
                        ins = pe.transpose(ps_g[:, j % 2, k * P:(k + 1) * P], o_n[:, j, k * P:(k + 1) * P], ident[:])
                    ins.then_inc(oT_mm, 1)
                for j in range(G):
                    pe.wait_ge(oT_done, g * G + (j + 3 if j < 2 else j + 1))
                    if j >= 2:
                        pe.wait_ge(h1_done, g * G + j - 1)
                    for k in range(KD):
                        ins = pe.matmul(ps_g[:, j % 2, 0:DIM], oT[:, j, k, :], proj_w[:, k, :],
                                        start=(k == 0), stop=(k == KD - 1))
                    ins.then_inc(proj_mm, 1)

            pe.wait_ge(b_weights_in, 16 * 13)
            pe.wait_ge(dequantised, 4)
            pe.wait_ge(h1_done, TILES)

            def opened(g, stage, j):
                b = bb.bank(stage, j)
                pe.wait_ge(read[b], bb.before(g, stage, j))
                return b

            def turn(g, stage, j, src, chunks, ready, count):
                pe.wait_ge(ready, count)
                b = opened(g, stage, j)
                for k in range(chunks):
                    ins = pe.transpose(ps[:, b, k * P:(k + 1) * P], src[:, k * P:(k + 1) * P], ident[:])
                ins.then_inc(written[b], 1)

            def arrived(g, stage, j):
                pe.wait_ge(read[bb.bank(stage, j)], bb.made(g, stage, j))

            def tokens_out(g, stage, j, left, right, chunks, width):
                b = opened(g, stage, j)
                for k in range(chunks):
                    ins = pe.matmul(ps[:, b, 0:width], left(k), right(k), start=(k == 0), stop=(k == chunks - 1))
                ins.then_inc(written[b], 1)

            def features_out(g, stage, c, w, col):
                b = opened(g, stage, c)
                for k in range(KD):
                    ins = pe.matmul(ps[:, b, :], w[:, k, col:col + P], nT[:, k, :], start=(k == 0), stop=(k == KD - 1))
                ins.then_inc(written[b], 1)

            with pe.Fori(0, GROUPS) as g:
                for j in range(G):
                    turn(g, "n2T", j, lin_in[:, j, :], KD, n2_done, g * G + j + 1)
                for j in range(G):
                    arrived(g, "n2T", j)
                for c in range(K2):
                    features_out(g, "fc1", c, fc1_w, c * P)
                for c in range(K2):
                    arrived(g, "fc1", c)
                for j in range(G):
                    tokens_out(g, "fc2", j, lambda k: hidT[:, k, j * P:(j + 1) * P], lambda k: fc2_w[:, k, :], K2, DIM)
                for j in range(G):
                    turn(g, "xxT", j, lin_in[:, j, :], KD, xx_done, g * G + j + 1)
                for j in range(G):
                    arrived(g, "xxT", j)
                    for h, stage in enumerate(("u", "v")):
                        tokens_out(g, stage, j, lambda k: nT[:, k, j * P:(j + 1) * P],
                                   lambda k: uv_w[:, k, h * GF:(h + 1) * GF], KD, GF)
                for j in range(G):
                    pe.wait_ge(uv_done, g * G + j + 1)
                    b = opened(g, "mix", j)
                    for h in range(MIX_HEADS):
                        ins = pe.matmul(ps[:, b, h * MIX_HD:(h + 1) * MIX_HD], mix_w[:, h, :],
                                        uv[:, j, GF + h * MIX_HD:GF + (h + 1) * MIX_HD], start=True, stop=True)
                    ins.then_inc(written[b], 1)
                for j in range(G):
                    m = bb.bank("mix", j)
                    turn(g, "uyT", j, uv[:, j, 0:GF], KG, read[m], bb.made(g, "mix", j))
                for j in range(G):
                    arrived(g, "uyT", j)
                    tokens_out(g, "o", j, lambda k: uyT[:, j, k, :], lambda k: o_w[:, k, :], KG, DIM)
                for j in range(G):
                    turn(g, "xmT", j, nrm[:, j, :], KD, xm_done, g * G + j + 1)
                for j in range(G):
                    arrived(g, "xmT", j)
                    tokens_out(g, "router", j, lambda k: nT[:, k, j * P:(j + 1) * P], lambda k: router_w[:, k, :],
                               KD, EXPERTS)
                for c in range(KS):
                    features_out(g, "gate", c, sh_gu, c * P)
                    features_out(g, "up", c, sh_gu, FS + c * P)
                for c in range(KS):
                    arrived(g, "up", c)
                for j in range(G):
                    tokens_out(g, "down", j, lambda k: shT[:, k, j * P:(j + 1) * P], lambda k: sh_d[:, k, :], KS, DIM)

            pe.wait_ge(taken_done, 1)
            pe.wait_ge(c_consts, 11)
            for b, left in ((0, earlier), (1, ones)):
                pe.wait_ge(read[b], b_end[b])
                pe.matmul(ps[:, b, :], left[:], taken.rearrange("p t e -> p (t e)"), start=True, stop=True
                          ).then_inc(written[b], 1)

            pe.wait_ge(experts_in, 32)
            pe.wait_ge(experts_known, 1)

            def d_open(g, stage, j):
                b = d_bank(stage, j)
                pe.wait_ge(read[b], d_before(g, stage, j))
                return b

            def expert_of(g, j):
                where = tile_expert[0:1, g * G + j:g * G + j + 1] if isinstance(g, int) else \
                    tile_expert[0:1, bass.ds(g * G + j, 1)]
                return pe.value_load(where, min_val=0, max_val=EXPERTS - 1)

            def gu(g, j):
                x = d_bank("xgT", j)
                e_of = expert_of(g, j)
                pe.wait_ge(read[x], d_made(g, "xgT", j))
                b = d_open(g, "gu", j)
                for k in range(KD):
                    ins = pe.matmul(ps[:, b, :], xgT[:, j % G, k, :],
                                    expert_gu[:, bass.ds(e_of, 1), k, :].rearrange("p e n -> p (e n)"),
                                    start=(k == 0), stop=(k == KD - 1))
                ins.then_inc(written[b], 1)

            def turn_hidden(g, j):
                pe.wait_ge(read[d_bank("gu", j)], d_made(g, "gu", j))
                b = d_open(g, "hT", j)
                for k in range(KFE):
                    ins = pe.transpose(ps[:, b, k * P:(k + 1) * P], hid[:, j % G, k * P:(k + 1) * P], ident[:])
                ins.then_inc(written[b], 1)

            def turn_x(g, j):
                pe.wait_ge(gathered[j % G], g * 16 + (16 * (j // G) + 16))
                b = d_open(g, "xgT", j)
                for k in range(KD):
                    ins = pe.transpose(ps[:, b, k * P:(k + 1) * P], xg[:, j % G, k * P:(k + 1) * P], ident[:])
                ins.then_inc(written[b], 1)

            def down(g, j):
                e_of = expert_of(g, j)
                pe.wait_ge(read[d_bank("hT", j)], d_made(g, "hT", j))
                b = d_open(g, "down", j)
                for k in range(KFE):
                    ins = pe.matmul(ps[:, b, 0:DIM], hT[:, j % G, k, :],
                                    expert_d[:, bass.ds(e_of, 1), k, :].rearrange("p e n -> p (e n)"),
                                    start=(k == 0), stop=(k == KFE - 1))
                ins.then_inc(written[b], 1)

            d_steps(pe, gu, turn_hidden, turn_x, down)


def layouts(np, x, L0_tok_ln1_g, L0_tok_ln1_b, L0_tok_W, L0_tok_b, L0_tok_ln2_g, L0_tok_ln2_b, L0_attn_qkv_w,
            L0_attn_qkv_b, L0_attn_proj_w, L0_attn_proj_b, L0_ffn_ln_gamma, L0_ffn_ln_beta, L0_ffn_fc1_q,
            L0_ffn_fc1_scales, L0_ffn_fc1_bias, L0_ffn_fc2_q, L0_ffn_fc2_scales, L0_ffn_fc2_bias, L1_attn_u_w,
            L1_attn_u_b, L1_attn_v_w, L1_attn_v_b, L1_attn_o_w, L1_attn_o_b, L1_attn_pos, L1_attn_zero, L1_attn_neg,
            L1_ffn_router_w, L1_ffn_bias, L1_ffn_gate_w, L1_ffn_up_w, L1_ffn_down_w, L1_ffn_sh_gate_w,
            L1_ffn_sh_up_w, L1_ffn_sh_down_w, **unused):
    tokens = x.reshape(64, 3, 8, 16, 8, 16).transpose(0, 2, 4, 3, 5, 1).reshape(TOKENS, PIX)
    order = [8 * c + 2 * r + par for r in range(4) for c in range(2) for par in range(2)]
    cols = np.concatenate([np.arange(16 * h, 16 * h + 16) for h in order])
    v_w = L0_attn_qkv_w[:, 512:][:, cols]
    qkv_w = np.concatenate([L0_attn_qkv_w[:, :512], v_w], axis=1)
    qkv_b = np.concatenate([L0_attn_qkv_b[:512], L0_attn_qkv_b[512:][cols]])
    taps = np.concatenate([L1_attn_neg[:, :IMAGES - 1][:, ::-1], L1_attn_zero, L1_attn_pos[:, :IMAGES - 1]], axis=1)
    j, i = np.arange(IMAGES)[:, None], np.arange(IMAGES)[None, :]
    mix = taps[:, i - j + IMAGES - 1].transpose(1, 0, 2)
    return {
        "fc1_q": L0_ffn_fc1_q, "fc1_s": L0_ffn_fc1_scales, "fc1_b": L0_ffn_fc1_bias.reshape(K2, P).T,
        "fc2_q": L0_ffn_fc2_q, "fc2_s": L0_ffn_fc2_scales, "fc2_b": L0_ffn_fc2_bias,
        "ln3_g": L0_ffn_ln_gamma.reshape(KD, P).T, "ln3_b": L0_ffn_ln_beta.reshape(KD, P).T,
        "uv_w": np.concatenate([L1_attn_u_w.T, L1_attn_v_w.T], axis=1), "uv_b": np.concatenate([L1_attn_u_b, L1_attn_v_b]),
        "mix": mix, "o_w": L1_attn_o_w.T, "o_b": L1_attn_o_b, "router_w": L1_ffn_router_w.T,
        "router_b": L1_ffn_bias,
        "sh_gu": np.concatenate([L1_ffn_sh_gate_w, L1_ffn_sh_up_w], axis=1), "sh_d": L1_ffn_sh_down_w,
        "expert_gu": np.concatenate([L1_ffn_gate_w, L1_ffn_up_w], axis=2), "expert_d": L1_ffn_down_w,
        "x": tokens, "ln1_g": L0_tok_ln1_g.reshape(6, P).T, "ln1_b": L0_tok_ln1_b.reshape(6, P).T,
        "tok_w": L0_tok_W.T, "tok_b": L0_tok_b, "ln2_g": L0_tok_ln2_g, "ln2_b": L0_tok_ln2_b,
        "qkv_w": qkv_w, "qkv_b": qkv_b.reshape(6, P).T, "proj_w": L0_attn_proj_w[cols, :], "proj_b": L0_attn_proj_b,
    }


def kernel(**inputs):
    import numpy as np
    import concourse.bacc as bacc
    from concourse.bass_utils import run_bass_kernel_spmd

    arrays = {"in_" + k: np.ascontiguousarray(v) for k, v in layouts(np, **inputs).items()}
    nc = bacc.Bacc("TRN2", target_bir_lowering=False, num_devices=1)
    io = {k[3:]: nc.dram_tensor(k, a.shape, mybir.dt.from_np(a.dtype), kind="ExternalInput").ap()
          for k, a in arrays.items()}
    io["out"] = nc.dram_tensor("out", (TOKENS + PAD_ROWS, DIM), F32, kind="ExternalOutput").ap()
    build(nc, io)
    r = run_bass_kernel_spmd(nc, [arrays], core_ids=[0])
    return r.results[0]["out"][:TOKENS].reshape(IMAGES, PATCHES, DIM)
```

```python
from contextlib import ExitStack

import concourse.bass as bass
from concourse import mybir

F32 = mybir.dt.float32
I32 = mybir.dt.int32
ALU = mybir.AluOpType
ACT = mybir.ActivationFunctionType
AX = mybir.AxisListType

P = 128
IMAGES, PATCHES, DIM = 64, 64, 256
TOKENS = IMAGES * PATCHES
TILES = TOKENS // P
G = 4
GROUPS = TILES // G
PIX = 768
KX = PIX // P
KD = DIM // P
HEADS, HD = 16, 16
PAIRS = HEADS // 2
EPS = 1e-5
F0 = 1024
K1, K2 = DIM // P, F0 // P
GF = 512
MIX_HEADS, MIX_HD = 8, 64
KG = GF // P
EXPERTS, FE = 16, 256
KFE = FE // P
TOP, EXPERT_GROUPS, TOP_GROUPS, ROUTE_SCALE = 4, 4, 2, 2.5
OF_GROUP = EXPERTS // EXPERT_GROUPS
SLOT_TILES = -(-(TOKENS * TOP // P + EXPERTS - 1) // 8) * 8
GD = 8
assert SLOT_TILES % GD == 0
COMBINE = 4
PAD_ROWS = P
FS = 512
KS = FS // P
WORK = 11264


class Chain:

    def __init__(self, eng, sem, per=0):
        self.eng, self.sem, self.per, self.n, self.base = eng, sem, per, 0, 0

    def turn(self, g, start=0):
        self.n = 0
        self.base = g * self.per + start

    def step(self, ins):
        self.n += 1
        ins.then_inc(self.sem, 1)
        return self.base + self.n

    def wait(self, value):
        self.eng.wait_ge(self.sem, value)

    def end(self):
        assert self.n == self.per, (self.n, self.per)


class Shelf:

    def __init__(self, ap):
        self.ap, self.at = ap, 0

    def take(self, shape):
        n = 1
        for d in shape[1:]:
            n *= d
        assert self.at + n <= self.ap.shape[1], (self.at, n, self.ap.shape)
        ap = self.ap[:, self.at:self.at + n]
        self.at += n
        if len(shape) == 2:
            return ap
        letters = "abcdef"[:len(shape) - 1]
        names = " ".join(letters)
        return ap.rearrange(f"p ({names}) -> p {names}", **dict(zip(letters[1:], shape[2:])))


class Banks:

    def __init__(self, order, start, banks=8):
        self.start, self.per, self.place = start, [0] * banks, {}
        for i, key in enumerate(order):
            self.place[key] = (i % banks, self.per[i % banks])
            self.per[i % banks] += 1

    def bank(self, stage, j):
        return self.place[stage, j][0]

    def before(self, g, stage, j):
        b, n = self.place[stage, j]
        return g * self.per[b] + (self.start[b] + n)

    def made(self, g, stage, j):
        return self.before(g, stage, j) + 1

    def after(self, turns):
        return [s + turns * n for s, n in zip(self.start, self.per)]


def at_least(eng, sem, value):
    if not isinstance(value, int) or value > 0:
        eng.wait_ge(sem, value)


def pipeline(eng, turns, per, stages, peel=1):
    total = turns * per

    def steps(g, count):
        for j in range(count):
            for fn, lag in stages:
                if not isinstance(g, int) or 0 <= g * per + j - lag < total:
                    fn(g, j - lag)

    for g in range(peel):
        steps(g, per)
    with eng.Fori(peel, turns) as g:
        steps(g, per)
    steps(turns, max(lag for _, lag in stages))


class Turns:

    def __init__(self, uses, per, turns, read, first, banks, peel=1):
        self.uses, self.per, self.turns, self.read, self.peel = uses, per, turns, read, peel
        self.place = {(stage, off % per[stage]): i for i, (stage, off) in enumerate(uses)}
        assert len(self.place) == len(uses)
        self.first, self.banks = first, banks

    def bank(self, stage, off):
        return self.first + self.place[stage, off % self.per[stage]] % self.banks

    def free(self, pe, g, stage, off):
        at = self.place[stage, off % self.per[stage]]
        turn = (off - self.uses[at][1]) // self.per[stage]
        back = 0
        k = at
        while True:
            k -= 1
            if k < 0:
                k, back = len(self.uses) - 1, back + 1
            if k % self.banks != at % self.banks:
                continue
            other, there = self.uses[k]
            n = self.per[other]
            if isinstance(g, int):
                number = (g + turn - back) * n + there
                if number < 0 and back > 3:
                    break
                if 0 <= number < self.turns * n:
                    pe.wait_ge(self.read[other], number + 1)
                    break
            else:
                assert turn == 0 and (self.peel - back) * n + there >= 0, (stage, off, other, there)
                pe.wait_ge(self.read[other], g * n + (there + 1 - back * n))
                break
        return self.bank(stage, off)


def build(nc, io, debug=()):
    with ExitStack() as ctx:
        def sb(name, shape, dt=F32):
            return ctx.enter_context(nc.sbuf_tensor(name, shape, dt))

        def psum(name, shape, dt=F32):
            return ctx.enter_context(nc.psum_tensor(name, shape, dt))

        def sem(name):
            return ctx.enter_context(nc.semaphore(name))

        def dram(name, shape, dt=F32):
            kind = "ExternalOutput" if name in debug else "Internal"
            return nc.dram_tensor(name, shape, dt, kind=kind).ap()

        h1_dram = dram("h1_dram", (TOKENS, DIM))
        xm_dram = dram("xm_dram", (TOKENS + PAD_ROWS, DIM))
        slots_dram = dram("slots_dram", (P * SLOT_TILES, 2))
        odd_out = dram("odd_out", (TOKENS + PAD_ROWS, DIM))
        out = io["out"]

        ident = sb("ident", [P, P])
        one_col = sb("one_col", [P, 1])
        eps_col = sb("eps_col", [P, 1])
        mhalf_col = sb("mhalf_col", [P, 1])
        head_parity4 = sb("head_parity4", [P, 4, 2])
        head_parity = sb("head_parity", [P, 2])
        copy_parity = sb("copy_parity", [P, 2])
        ln1_gb = sb("ln1_gb", [P, 2, KX])
        tok_b = sb("tok_b", [P, DIM])
        ln2_g = sb("ln2_g", [P, DIM])
        ln2_b = sb("ln2_b", [P, DIM])
        proj_b = sb("proj_b", [P, DIM])
        qkv_b = sb("qkv_b", [P, 6])
        kb_par = sb("kb_par", [P, 2, 2])

        fc1_w = sb("fc1_w", [P, K1, F0])
        fc2_w = sb("fc2_w", [P, K2, DIM])
        fc1_b = sb("fc1_b", [P, K2])
        ln3_gb = sb("ln3_gb", [P, 2, KD])
        fc2_b = sb("fc2_b", [P, DIM])
        uv_w = sb("uv_w", [P, KD, 2 * GF])
        uv_b = sb("uv_b", [P, 2 * GF])
        mix_w = sb("mix_w", [P, MIX_HEADS, P])
        o_w = sb("o_w", [P, KG, DIM])
        o_b = sb("o_b", [P, DIM])
        router_w = sb("router_w", [P, KD, EXPERTS])
        sh_gu = sb("sh_gu", [P, KD, 2 * FS])
        sh_d = sb("sh_d", [P, KS, DIM])
        logits = sb("logits", [P, TILES, EXPERTS])
        half_col = sb("half_col", [P, 1])
        one_neg = sb("one_neg", [P, 1])
        tiny_col = sb("tiny_col", [P, 1])

        expert_gu = sb("expert_gu", [P, EXPERTS, KD, 2 * FE])
        expert_d = sb("expert_d", [P, EXPERTS, KFE, DIM])
        work = sb("work", [P, WORK])

        in_gu = Shelf(expert_gu[:].rearrange("p e k n -> p (e k n)"))
        in_d = Shelf(expert_d[:].rearrange("p e k n -> p (e k n)"))
        in_work = Shelf(work[:])
        tok_w = in_work.take([P, KX, DIM])
        qkv_w = in_work.take([P, KD, 3 * DIM])
        proj_w = in_work.take([P, KD, DIM])
        x_in = in_gu.take([P, G, PIX])
        x_n = in_gu.take([P, G, PIX])
        x_nT = in_gu.take([P, G, KX, P])
        t_lin = in_gu.take([P, G, DIM])
        h0 = in_gu.take([P, G, DIM])
        hp = in_gu.take([P, G, DIM])
        a_n = in_gu.take([P, G, DIM])
        aT = in_gu.take([P, G, KD, 2, 2, 64])
        qT = in_gu.take([P, G, 2, P])
        kT = in_d.take([P, G, 2, 2, P])
        vblk = in_d.take([P, G, 2, PAIRS, 2, HD + 1])
        e = in_work.take([P, G, HEADS, 64])
        pT = in_d.take([P, 2, PAIRS, P])
        o_n = in_d.take([P, G, DIM])
        oT = in_work.take([P, G, KD, P])
        h1 = in_work.take([P, G, DIM])
        stats = sb("stats", [P, G, 12])
        stats2 = sb("stats2", [P, G, 6])
        stats3 = sb("stats3", [P, G, 6])
        mv = sb("mv", [P, 3, G, 2])
        ve = sb("ve", [P, 3, G])
        rs = sb("rs", [P, 3, G])
        smax = sb("smax", [P, G, HEADS])
        rsum = sb("rsum", [P, G, HEADS])

        in_work_b = Shelf(work[:])
        res = in_work_b.take([P, G, DIM])
        nrm = in_work_b.take([P, G, DIM])
        lin_in = in_work_b.take([P, G, DIM])
        nT = in_work_b.take([P, KD, G * P])
        hidT = in_work_b.take([P, K2, G * P])
        uv = hidT.rearrange("p k t -> p (k t)").rearrange("p (j n) -> p j n", j=G)
        uyT = in_work_b.take([P, G, KG, P])
        shT = uyT.rearrange("p j k t -> p (j k t)").rearrange("p (k t) -> p k t", k=KS)
        sh_g = in_work_b.take([P, 2, G * P])

        router_b = sb("router_b", [P, EXPERTS])
        ones = sb("ones", [P, P])
        earlier = sb("earlier", [P, P])
        below_e = sb("below_e", [P, EXPERTS, EXPERTS])
        zeros = sb("zeros", [P, DIM])
        tile_expert = sb("tile_expert", [P, SLOT_TILES], I32)
        slots = sb("slots", [P, SLOT_TILES, 2])
        slot_rows = sb("slot_rows", [P, SLOT_TILES], I32)
        recs = sb("recs", [P, TILES, TOP, 3], I32)
        in_c = Shelf(work[:])
        TE = [P, TILES, EXPERTS]
        scores_sb, biased, masked, rank_e, taken, tw = (in_c.take(TE) for _ in range(6))
        pair_sums = in_c.take([P, TILES * EXPERT_GROUPS, 6])
        g_score, g_rank, g_less = (in_c.take([P, TILES, EXPERT_GROUPS]) for _ in range(3))
        cmp_a, cmp_b = (in_c.take([P, 8, EXPERTS, EXPERTS]) for _ in range(2))
        w_sum = in_c.take([P, TILES])
        in_c2 = Shelf(cmp_a.rearrange("p a b c -> p (a b c)"))
        totals, cum_a, cum_b = (in_c2.take(TE) for _ in range(3))
        ends_a, ends_b, padded, base = (in_c2.take([P, EXPERTS]) for _ in range(4))
        slot_no = biased
        picked = masked
        in_c3 = Shelf(cmp_b.rearrange("p a b c -> p (a b c)"))
        choice_slot, choice_w, choice_tile, choice_at = (in_c3.take([P, TILES, TOP]) for _ in range(4))
        in_c4 = Shelf(pair_sums.rearrange("p a b -> p (a b)"))
        tile_e = in_c4.take([P, SLOT_TILES])
        tile_start, token_row = in_c.take([P, SLOT_TILES]), in_c.take([P, TILES])
        slots_init = in_c3.take([P, SLOT_TILES, 2])
        ring = sb("ring", [P, TOP, 3], I32)
        gather_rows = sb("gather_rows", [P, GD], I32)
        add_rows = sb("add_rows", [P, GD], I32)
        in_d2 = Shelf(work[:])
        xg = in_d2.take([P, G, DIM])
        xgT = in_d2.take([P, G, KD, P])
        act_g = in_d2.take([P, G, FE])
        hid = in_d2.take([P, G, FE])
        hT = in_d2.take([P, G, KFE, P])
        y = in_d2.take([P, G, DIM])

        ps = psum("ps", [P, 8, 512])
        ps_s = ps[:, 0:4, :]
        ps_t = ps[:, 4:6, :]
        ps_g = ps[:, 6:8, :]

        weights_in = sem("weights_in")
        setup = sem("setup")
        consts_done = sem("consts_done")
        vec_setup = sem("vec_setup")
        vec_fence = sem("vec_fence")
        x_loaded = [sem(f"x_loaded{j}") for j in range(G)]
        var_done = [sem(f"var_done{n}") for n in range(3)]
        ve_done = [sem(f"ve_done{n}") for n in range(3)]
        rstd_done = [sem(f"rstd_done{n}") for n in range(3)]
        stats_done = [sem(f"stats_done{n}") for n in range(3)]
        h0_part = sem("h0_part")
        h0_done = sem("h0_done")
        max_done = sem("max_done")
        rsum_done = sem("rsum_done")
        xn_done = sem("xn_done")
        xnT_mm = sem("xnT_mm")
        xnT_done = sem("xnT_done")
        tok_mm = sem("tok_mm")
        an_done = sem("an_done")
        tok_free = sem("tok_free")
        anT_mm = sem("anT_mm")
        aT_done = sem("aT_done")
        qk_mm = sem("qk_mm")
        qk_done = sem("qk_done")
        v_mm = sem("v_mm")
        v_done = sem("v_done")
        s_mm = sem("s_mm")
        s_sub = sem("s_sub")
        e_done = sem("e_done")
        pT_mm = sem("pT_mm")
        pT_done = sem("pT_done")
        pv_mm = sem("pv_mm")
        o_done = sem("o_done")
        oT_mm = sem("oT_mm")
        oT_done = sem("oT_done")
        proj_mm = sem("proj_mm")
        hp_done = sem("hp_done")
        h1_done = sem("h1_done")
        h1_stored = [sem(f"h1_stored{j}") for j in range(G)]

        a_steps = [("oT", 4), ("tok", 1), ("proj", 4), ("qk", 2), ("v", 2), ("pv", 3), ("anT", 1)]
        at = Turns([(stage, j - lag) for j in range(G) for stage, lag in a_steps],
                   {stage: G for stage, _ in a_steps}, GROUPS,
                   dict(oT=oT_done, tok=tok_free, proj=h1_done, qk=qk_done, v=v_done, pv=o_done, anT=aT_done), 6, 2)
        turn_banks = Turns([(stage, j - lag) for j in range(G) for stage, lag in (("xnT", 1), ("pT", 3))],
                           dict(xnT=G, pT=G), GROUPS, dict(xnT=xnT_done, pT=pT_done), 4, 1)

        b_weights_in = sem("b_weights_in")
        quant_in = sem("quant_in")
        dequantised = sem("dequantised")
        mix_zeroed = sem("mix_zeroed")
        pool_fence = sem("pool_fence")
        experts_in = sem("experts_in")
        pool_setup = sem("pool_setup")
        h_loaded = [sem(f"h_loaded{j}") for j in range(G)]
        b_var = sem("b_var")
        b_scales = sem("b_scales")
        n1_done = sem("n1_done")
        n2_done = sem("n2_done")
        qn_done = sem("qn_done")
        xx_done = sem("xx_done")
        xm_done = sem("xm_done")
        res1_done = sem("res1_done")
        res2_done = sem("res2_done")
        uvb_done = sem("uvb_done")
        uv_done = sem("uv_done")
        uy_done = sem("uy_done")
        shg_done = sem("shg_done")
        xm_stored = [sem(f"xm_stored{j}") for j in range(G)]
        h4_stored = [sem(f"h4_stored{j}") for j in range(G)]
        pool_chain_b = sem("pool_chain_b")
        vec_chain_b = sem("vec_chain_b")
        written = [sem(f"written{b}") for b in range(8)]
        read = [sem(f"read{b}") for b in range(8)]

        b_order = ([("n2T", j) for j in range(G)] + [("fc1", c) for c in range(K2)]
                   + [("fc2", j) for j in range(G)] + [("xxT", j) for j in range(G)]
                   + [(w, j) for j in range(G) for w in ("u", "v")] + [("mix", j) for j in range(G)]
                   + [("uyT", j) for j in range(G)] + [("o", j) for j in range(G)]
                   + [("xmT", j) for j in range(G)] + [("router", j) for j in range(G)]
                   + [(w, c) for c in range(KS) for w in ("gate", "up")] + [("down", j) for j in range(G)])
        bb = Banks(b_order, [0] * 8)
        b_end = bb.after(GROUPS)

        router_b_in = sem("router_b_in")
        zeros_stored = sem("zeros_stored")
        c_consts = sem("c_consts")
        slots_begun = sem("slots_begun")
        scores_done = sem("scores_done")
        taken_done = sem("taken_done")
        vec_chain_c = sem("vec_chain_c")
        experts_known = sem("experts_known")
        recs_done = sem("recs_done")
        pool_chain_c = sem("pool_chain_c")
        slots_scattered = sem("slots_scattered")
        slots_in = sem("slots_in")
        rows_done = sem("rows_done")
        gather_rows_done = sem("gather_rows_done")
        add_rows_done = sem("add_rows_done")
        combined = sem("combined")
        gathered = [sem(f"gathered{j}") for j in range(G)]
        act_g_done = sem("act_g_done")
        added = [sem(f"added{j}") for j in range(G)]

        D_BANK = {"gu": 0, "hT": 2, "xgT": 4, "down": 6}

        def d_bank(stage, j):
            return D_BANK[stage] + j % 2

        def d_before(g, stage, j):
            return g * (GD // 2) + (d_start[d_bank(stage, j)] + j // 2)

        def d_made(g, stage, j):
            return d_before(g, stage, j) + 1

        D_TURNS = SLOT_TILES // GD
        X_LAG, GU_LAG, HID_LAG, DOWN_LAG = 0, 1, 2, 3

        d_start = [n + (b < 2) for b, n in enumerate(b_end)]

        block = ctx.enter_context(nc.Block())

        @block.sync
        def _(sp):
            def row(dst, src):
                sp.dma_start(dst, src.rearrange("(a n) -> a n", a=1).to_broadcast([P, src.shape[0]])
                             ).then_inc(weights_in, 16)
            sp.dma_start(tok_w[:], io["tok_w"].rearrange("(k p) n -> p k n", p=P)).then_inc(weights_in, 16)
            sp.dma_start(ln1_gb[:, 0, :], io["ln1_g"]).then_inc(weights_in, 16)
            sp.dma_start(ln1_gb[:, 1, :], io["ln1_b"]).then_inc(weights_in, 16)
            row(tok_b[:], io["tok_b"])
            row(ln2_g[:], io["ln2_g"])
            row(ln2_b[:], io["ln2_b"])
            row(proj_b[:], io["proj_b"])
            sp.dma_start(qkv_w[:], io["qkv_w"].rearrange("(k p) n -> p k n", p=P)).then_inc(weights_in, 16)
            sp.dma_start(qkv_b[:], io["qkv_b"]).then_inc(weights_in, 16)
            sp.dma_start(proj_w[:], io["proj_w"].rearrange("(k p) n -> p k n", p=P)).then_inc(weights_in, 16)

            sp.dma_start(fc1_w[:].bitcast(I32), io["fc1_q"].rearrange("(k p) n -> p k n", p=P)).then_inc(quant_in, 16)
            sp.dma_start(fc2_w[:].bitcast(I32), io["fc2_q"].rearrange("(k p) n -> p k n", p=P)).then_inc(quant_in, 16)
            for dst, src in ((sh_gu, io["fc1_s"]), (uv_w, io["fc2_s"])):
                sp.dma_start(dst[:].rearrange("p k n -> p (k n)"), src.rearrange("k n -> (k n)")
                             .rearrange("(a n) -> a n", a=1).to_broadcast([P, 2 * F0])).then_inc(quant_in, 16)

            def b_row(dst, src):
                sp.dma_start(dst, src.rearrange("(a n) -> a n", a=1).to_broadcast([P, src.shape[0]])
                             ).then_inc(b_weights_in, 16)
            sp.dma_start(router_b[:], io["router_b"].rearrange("(a n) -> a n", a=1).to_broadcast([P, EXPERTS])
                         ).then_inc(router_b_in, 16)
            sp.wait_ge(c_consts, 6)
            sp.dma_start(xm_dram[TOKENS:, :], zeros[:]).then_inc(zeros_stored, 16)
            sp.dma_start(out[TOKENS:, :], zeros[:]).then_inc(zeros_stored, 16)
            sp.dma_start(odd_out.rearrange("(p r) d -> p r d", p=P),
                         zeros[:].unsqueeze(1).to_broadcast([P, (TOKENS + PAD_ROWS) // P, DIM])
                         ).then_inc(zeros_stored, 16)
            b_row(fc2_b[:], io["fc2_b"])
            b_row(uv_b[:], io["uv_b"])
            b_row(o_b[:], io["o_b"])
            sp.dma_start(fc1_b[:], io["fc1_b"]).then_inc(b_weights_in, 16)
            sp.dma_start(ln3_gb[:, 0, :], io["ln3_g"]).then_inc(b_weights_in, 16)
            sp.dma_start(ln3_gb[:, 1, :], io["ln3_b"]).then_inc(b_weights_in, 16)
            sp.wait_ge(mix_zeroed, 1)
            for i in range(2):
                sp.dma_start(mix_w[64 * i:64 * i + 64, :, 64 * i:64 * i + 64], io["mix"]).then_inc(b_weights_in, 16)
            sp.dma_start(o_w[:], io["o_w"].rearrange("(k p) n -> p k n", p=P)).then_inc(b_weights_in, 16)
            sp.dma_start(router_w[:], io["router_w"].rearrange("(k p) n -> p k n", p=P)).then_inc(b_weights_in, 16)
            sp.dma_start(sh_d[:], io["sh_d"].rearrange("(k p) n -> p k n", p=P)).then_inc(b_weights_in, 16)
            sp.wait_ge(dequantised, 4)
            sp.dma_start(sh_gu[:], io["sh_gu"].rearrange("(k p) n -> p k n", p=P)).then_inc(b_weights_in, 16)
            sp.dma_start(uv_w[:], io["uv_w"].rearrange("(k p) n -> p k n", p=P)).then_inc(b_weights_in, 16)

            def load_x(g, j):
                at_least(sp, xn_done, g * G + (j + 1 - G))
                sp.dma_start(x_in[:, j % G, :], io["x"][bass.ds((g * G + j) * P, P), :] if not isinstance(g, int)
                             else io["x"][(g * G + j) * P:(g * G + j + 1) * P, :]).then_inc(x_loaded[j % G], 16)

            pipeline(sp, GROUPS, G, [(load_x, 0)])

            h1_by_patch = h1_dram.rearrange("(i b) d -> b i d", b=PATCHES)
            xm_by_patch = xm_dram[0:TOKENS, :].rearrange("(i b) d -> b i d", b=PATCHES)
            out_by_patch = out[0:TOKENS, :].rearrange("(i b) d -> b i d", b=PATCHES)
            for j in range(G):
                sp.wait_ge(h1_stored[j], 16 * GROUPS)
            sp.wait_ge(h1_done, TILES)
            sp.dma_start(expert_gu[:], io["expert_gu"].rearrange("e (k p) n -> p e k n", p=P)).then_inc(experts_in, 16)
            sp.dma_start(expert_d[:], io["expert_d"].rearrange("e (k p) n -> p e k n", p=P)).then_inc(experts_in, 16)
            with sp.Fori(0, GROUPS) as g:
                for j in range(G):
                    sp.wait_ge(h4_stored[j], g * 32)
                    for i in range(2):
                        sp.dma_start(res[64 * i:64 * i + 64, j, :],
                                     h1_by_patch[bass.ds(g * (2 * G) + (2 * j + i), 1), :, :]
                                     .rearrange("b i d -> (b i) d")).then_inc(h_loaded[j], 16)
                for j in range(G):
                    sp.wait_ge(xm_done, g * G + j + 1)
                    for i in range(2):
                        sp.dma_start(xm_by_patch[bass.ds(g * (2 * G) + (2 * j + i), 1), :, :]
                                     .rearrange("b i d -> (b i) d"), nrm[64 * i:64 * i + 64, j, :]
                                     ).then_inc(xm_stored[j], 16)
                for j in range(G):
                    b = bb.bank("down", j)
                    sp.wait_ge(read[b], bb.made(g, "down", j))
                    for i in range(2):
                        sp.dma_start(out_by_patch[bass.ds(g * (2 * G) + (2 * j + i), 1), :, :]
                                     .rearrange("b i d -> (b i) d"), res[64 * i:64 * i + 64, j, :]
                                     ).then_inc(h4_stored[j], 16)
            for j in range(G):
                sp.wait_ge(h4_stored[j], 32 * GROUPS)
                sp.wait_ge(xm_stored[j], 32 * GROUPS)

            sp.wait_ge(slots_scattered, 16 * TILES * TOP)
            sp.dma_start(slots[:], slots_dram.rearrange("(p t) c -> p t c", p=P)).then_inc(slots_in, 16)

        @block.gpsimd
        def _(pool):
            pool.memset(mix_w[:], 0.0).then_inc(mix_zeroed, 1)
            pool.memset(ident[:], 0.0).then_inc(setup, 1)
            pool.memset(one_col[:], 1.0).then_inc(setup, 1)
            pool.memset(eps_col[:], EPS).then_inc(setup, 1)
            pool.memset(mhalf_col[:], -0.5).then_inc(setup, 1)
            pool.memset(head_parity4[:], 1.0).then_inc(setup, 1)
            pool.memset(copy_parity[:], 1.0).then_inc(setup, 1)
            pool.wait_ge(setup, 6)
            pool.affine_select(out=ident[:], in_=ident[:], compare_op=ALU.not_equal, fill=1.0, base=0,
                               pattern=[[-1, P]], channel_multiplier=1).then_inc(setup, 1)
            pool.affine_select(out=head_parity4[:], in_=head_parity4[:], compare_op=ALU.is_ge, fill=0.0, base=0,
                               pattern=[[-32, 4], [-16, 2]], channel_multiplier=1).then_inc(setup, 1)
            pool.affine_select(out=copy_parity[:], in_=copy_parity[:], compare_op=ALU.is_ge, fill=0.0, base=0,
                               pattern=[[-64, 2]], channel_multiplier=1).then_inc(setup, 1)
            pool.wait_ge(setup, 9)
            pool.affine_select(out=head_parity4[:], in_=head_parity4[:], compare_op=ALU.is_ge, fill=0.0, base=15,
                               pattern=[[32, 4], [16, 2]], channel_multiplier=-1).then_inc(setup, 1)
            pool.affine_select(out=copy_parity[:], in_=copy_parity[:], compare_op=ALU.is_ge, fill=0.0, base=63,
                               pattern=[[64, 2]], channel_multiplier=-1).then_inc(setup, 1)

            pool.memset(ones[:], 1.0).then_inc(c_consts, 1)
            pool.memset(earlier[:], 1.0).then_inc(c_consts, 1)
            pool.memset(below_e[:], 1.0).then_inc(c_consts, 1)
            pool.memset(zeros[:], 0.0).then_inc(c_consts, 1)
            pool.wait_ge(c_consts, 4)
            pool.affine_select(out=earlier[:], in_=earlier[:], compare_op=ALU.is_gt, fill=0.0, base=0,
                               pattern=[[1, P]], channel_multiplier=-1).then_inc(c_consts, 1)
            pool.affine_select(out=below_e[:], in_=below_e[:], compare_op=ALU.is_gt, fill=0.0, base=0,
                               pattern=[[1, EXPERTS], [-1, EXPERTS]], channel_multiplier=0).then_inc(c_consts, 1)
            pool.memset(half_col[:], 0.5).then_inc(pool_setup, 1)
            pool.memset(one_neg[:], -1.0).then_inc(pool_setup, 1)
            pool.memset(tiny_col[:], 1e-8).then_inc(pool_setup, 1)

            pool.wait_ge(setup, 11)
            pool.wait_ge(weights_in, 16 * 10)
            def rstd(g, which, j, ready):
                j4 = j % G
                pool.wait_ge(ready, g * G + (j + 1))
                pool.tensor_tensor(ve[:, which, j4:j4 + 1], mv[:, which, j4, 1:2], eps_col[:], ALU.add
                                   ).then_inc(ve_done[which], 1)
                pool.wait_ge(ve_done[which], g * G + (j + 1))
                pool.tensor_tensor(rs[:, which, j4:j4 + 1], ve[:, which, j4:j4 + 1], mhalf_col[:],
                                   ALU.pow).then_inc(rstd_done[which], 1)

            def with_bias(g, j):
                pool.wait_ge(h0_done, g * G + (j + 1))
                at_least(pool, h1_done, g * G + (j + 1 - G))
                pool.tensor_tensor(hp[:, j % G, :], h0[:, j % G, :], proj_b[:], ALU.add).then_inc(hp_done, 1)

            pipeline(pool, GROUPS, G, [
                (lambda g, j: rstd(g, 1, j, var_done[1]), 1),
                (lambda g, j: rstd(g, 0, j, var_done[0]), 0),
                (lambda g, j: rstd(g, 2, j, var_done[2]), 1),
                (with_bias, 1)])

            pool.wait_ge(pool_setup, 3)
            pool.wait_ge(b_weights_in, 16 * 13)
            pool.tensor_tensor(fc2_b[:], fc2_b[:], half_col[:].to_broadcast([P, DIM]), ALU.mult).then_inc(pool_setup, 1)
            pool.wait_ge(pool_setup, 4)
            chain = Chain(pool, pool_chain_b, 16 * G)

            def tt(out, a, b, op):
                chain.wait(chain.step(pool.tensor_tensor(out, a, b, op)))

            with pool.Fori(0, GROUPS) as g:
                chain.turn(g)
                for j in range(G):
                    t, r1, r2 = ve[:, 0, j:j + 1], rs[:, 0, j:j + 1], rs[:, 1, j:j + 1]
                    pool.wait_ge(b_var, g * (3 * G) + j + 1)
                    tt(t, mv[:, 0, j, 1:2], eps_col[:], ALU.add)
                    tt(r1, t, mhalf_col[:], ALU.pow)
                    tt(t, mv[:, 0, j, 1:2], r1, ALU.mult)
                    tt(t, t, r1, ALU.mult)
                    tt(t, t, eps_col[:], ALU.add)
                    tt(r2, t, mhalf_col[:], ALU.pow)
                    pool.tensor_tensor(r2, r2, r1, ALU.mult).then_inc(b_scales, 1)
                for j in range(G):
                    pool.wait_ge(n1_done, g * G + j + 1)
                    pool.wait_ge(n2_done, g * G + j + 1)
                    tt(res[:, j, :], res[:, j, :], nrm[:, j, :], ALU.add)
                    pool.tensor_tensor(res[:, j, :], res[:, j, :], fc2_b[:], ALU.add).then_inc(res1_done, 1)
                for j in range(G):
                    t, r1, r2 = ve[:, 1, j:j + 1], rs[:, 0, j:j + 1], rs[:, 1, j:j + 1]
                    pool.wait_ge(b_var, g * (3 * G) + G + j + 1)
                    tt(t, mv[:, 1, j, 1:2], eps_col[:], ALU.add)
                    tt(r1, t, mhalf_col[:], ALU.pow)
                    tt(t, mv[:, 1, j, 1:2], r1, ALU.mult)
                    tt(t, t, r1, ALU.mult)
                    tt(t, t, half_col[:], ALU.pow)
                    tt(t, t, tiny_col[:], ALU.add)
                    tt(r2, t, one_neg[:], ALU.pow)
                    pool.tensor_tensor(r2, r2, r1, ALU.mult).then_inc(b_scales, 1)
                    pool.wait_ge(qn_done, g * G + j + 1)
                    pool.wait_ge(xx_done, g * G + j + 1)
                    tt(res[:, j, :], res[:, j, :], nrm[:, j, :], ALU.add)
                    pool.tensor_tensor(res[:, j, :], res[:, j, :], o_b[:], ALU.add).then_inc(res2_done, 1)
                for j in range(G):
                    pool.wait_ge(b_var, g * (3 * G) + 2 * G + j + 1)
                    tt(ve[:, 2, j:j + 1], mv[:, 2, j, 1:2], eps_col[:], ALU.add)
                    pool.tensor_tensor(rs[:, 2, j:j + 1], ve[:, 2, j:j + 1], mhalf_col[:],
                                       ALU.pow).then_inc(b_scales, 1)
                chain.end()

            for j in range(G):
                pool.wait_ge(h4_stored[j], 32 * GROUPS)
            pool.iota(tile_start, pattern=[[P, SLOT_TILES]], base=0, channel_multiplier=0,
                      allow_small_or_imprecise_dtypes=True).then_inc(c_consts, 1)
            for i in range(2):
                pool.wait_ge(c_consts, 7 + i)
                pool.iota(token_row[64 * i:64 * i + 64, :], pattern=[[2, TILES]], base=i,
                          channel_multiplier=PATCHES, allow_small_or_imprecise_dtypes=True).then_inc(c_consts, 1)
            pool.wait_ge(c_consts, 9)
            pool.memset(slots_init[:, :, 1], 0.0).then_inc(c_consts, 1)
            pool.iota(slots_init[:, :, 0], pattern=[[0, SLOT_TILES]], base=TOKENS, channel_multiplier=1,
                      allow_small_or_imprecise_dtypes=True).then_inc(c_consts, 1)
            pool.wait_ge(c_consts, 11)
            pool.dma_start(slots_dram.rearrange("(p t) c -> p t c", p=P), slots_init).then_inc(slots_begun, 16)
            pool.wait_ge(slots_begun, 16)
            pool.wait_ge(recs_done, 3)
            chain = Chain(pool, pool_chain_c, 1)
            with pool.Fori(0, TILES) as t:
                chain.turn(t)
                pool.wait_ge(slots_scattered, t * (16 * TOP))
                pool.sem_inc(pool_fence, 1)
                chain.wait(chain.step(pool.tensor_copy(ring[:], recs[:, bass.ds(t, 1), :, :]
                                                       .rearrange("p t k c -> p (t k) c"))))
                pool.sem_inc(pool_fence, 1)
                for k in range(TOP):
                    pool.indirect_dma_start(
                        slots_dram, bass.IndirectOffsetOnAxis(ap=ring[:, k, 0:1], axis=0),
                        ring[:, k, 1:3].bitcast(F32), None).then_inc(slots_scattered, 16)
                chain.end()

            pool.wait_ge(rows_done, 1)
            pool.wait_ge(zeros_stored, 48)

            def rows_of_group(dst, done, g, j):
                j8 = j % GD
                src = slot_rows[:, bass.ds(g * GD + j, G)] if not isinstance(g, int) else \
                    slot_rows[:, g * GD + j:g * GD + j + G]
                pool.tensor_copy(dst[:, j8:j8 + G], src).then_inc(done, 1)

            def gather(g, j):
                if j % G == 0:
                    at_least(pool, gathered[0], (g * 2 + (j // G - 1)) * 16)
                    pool.sem_inc(pool_fence, 1)
                    rows_of_group(gather_rows, gather_rows_done, g, j)
                    pool.wait_ge(gather_rows_done, g * 2 + (j // G + 1))
                if not isinstance(g, int) or g * GD + j >= G:
                    pool.wait_ge(written[d_bank("xgT", j)], d_made(g, "xgT", j - G))
                    pool.sem_inc(pool_fence, 1)
                pool.indirect_dma_start(xg[:, j % G, :], None, xm_dram,
                                        bass.IndirectOffsetOnAxis(ap=gather_rows[:, j % GD:j % GD + 1], axis=0)
                                        ).then_inc(gathered[j % G], 16)

            def add_out(g, j):
                j8 = j % GD
                if j % G == 0:
                    for k in range(G):
                        at_least(pool, added[k], (g * 2 + (j // G - 1)) * 16)
                    pool.sem_inc(pool_fence, 1)
                    rows_of_group(add_rows, add_rows_done, g, j)
                    pool.wait_ge(add_rows_done, g * 2 + (j // G + 1))
                pool.wait_ge(read[d_bank("down", j)], d_made(g, "down", j))
                at_least(pool, added[(j - 2) % G], (g * 2 + ((j - 2) // G + 1)) * 16)
                pool.sem_inc(pool_fence, 1)
                pool.indirect_dma_start(out if j % 2 == 0 else odd_out,
                                        bass.IndirectOffsetOnAxis(ap=add_rows[:, j8:j8 + 1], axis=0),
                                        y[:, j % G, :], None, compute_op=ALU.add).then_inc(added[j % G], 16)

            pipeline(pool, D_TURNS, GD, [(gather, 0), (add_out, 6)])
            for k in range(G):
                pool.wait_ge(added[k], 16 * SLOT_TILES // G)
            for k in range(COMBINE):
                rows = slice(k * (TOKENS // COMBINE), (k + 1) * (TOKENS // COMBINE))
                pool.dma_start(out[rows, :], odd_out[rows, :], accum_op=ALU.add,
                               max_dma_last_dim=4 * DIM).then_inc(combined, 16)
            pool.wait_ge(combined, 16 * COMBINE)

        @block.scalar
        def _(act):
            act.wait_ge(consts_done, 2)
            act.wait_ge(weights_in, 16 * 10)
            def x_turned(g, j):
                act.wait_ge(xnT_mm, g * G + (j + 1))
                for k in range(KX):
                    ins = act.activation(x_nT[:, j % G, k, :], ps_t[:, k // 4, (k % 4) * P:(k % 4 + 1) * P],
                                         ACT.Identity, scale=ln1_gb[:, 0, k:k + 1], bias=ln1_gb[:, 1, k:k + 1])
                ins.then_inc(xnT_done, 1)

            def a_turned(g, j):
                act.wait_ge(anT_mm, g * G + (j + 1))
                src = ps[:, at.bank("anT", j), 0:DIM].rearrange("p (a t) -> p a t", t=64)
                act.activation(aT[:, j % G].rearrange("p k i c t -> p (k i) c t"),
                               src.unsqueeze(2).to_broadcast([P, 2 * KD, 2, 64]), ACT.Copy).then_inc(aT_done, 1)

            def qk_read(g, j):
                act.wait_ge(qk_mm, g * G + (j + 1))
                b = at.bank("qk", j)
                for c in range(2):
                    act.activation(qT[:, j % G, c, :], ps[:, b, c * P:(c + 1) * P], ACT.Identity,
                                   bias=qkv_b[:, c:c + 1])
                for c in range(2):
                    for par in range(2):
                        ins = act.activation(kT[:, j % G, c, par, :], ps[:, b, (2 + c) * P:(3 + c) * P],
                                             ACT.Identity, scale=head_parity[:, par:par + 1],
                                             bias=kb_par[:, c, par:par + 1])
                ins.then_inc(qk_done, 1)

            def exponentials(g, j):
                act.wait_ge(s_sub, g * G + (j + 1))
                act.activation(e[:, j % G], e[:, j % G], ACT.Exp, scale=HD ** -0.5).then_inc(e_done, 1)

            def p_turned(g, j):
                act.wait_ge(pT_mm, g * G + (j + 1))
                act.activation(pT[:, j % 2].rearrange("p a t -> p (a t)"),
                               ps_t[:].rearrange("p b n -> p (b n)"), ACT.Copy).then_inc(pT_done, 1)

            def o_turned(g, j):
                act.wait_ge(oT_mm, g * G + (j + 1))
                b = at.bank("oT", j)
                for k in range(KD):
                    ins = act.activation(oT[:, j % G, k, :], ps[:, b, k * P:(k + 1) * P], ACT.Identity,
                                         bias=qkv_b[:, 4 + k:5 + k])
                ins.then_inc(oT_done, 1)

            def store_h1(g, j):
                act.wait_ge(h1_done, g * G + (j + 1))
                rows = h1_dram[(g * G + j) * P:(g * G + j + 1) * P, :] if isinstance(g, int) else \
                    h1_dram[bass.ds((g * G + j) * P, P), :]
                act.dma_start(rows, h1[:, j % G, :]).then_inc(h1_stored[j % G], 16)

            pipeline(act, GROUPS, G, [(o_turned, 4), (x_turned, 1), (exponentials, 3), (qk_read, 2), (store_h1, 4),
                                      (p_turned, 3), (a_turned, 1)])
            for j in range(G):
                act.wait_ge(h1_stored[j], 16 * GROUPS)

            act.wait_ge(b_weights_in, 16 * 13)

            def turned(g, stage, j, affine=False):
                b = bb.bank(stage, j)
                act.wait_ge(written[b], bb.made(g, stage, j))
                dst = nT[:, :, j * P:(j + 1) * P]
                if affine:
                    for k in range(KD):
                        ins = act.activation(dst[:, k, :], ps[:, b, k * P:(k + 1) * P], ACT.Identity,
                                             scale=ln3_gb[:, 0, k:k + 1], bias=ln3_gb[:, 1, k:k + 1])
                else:
                    ins = act.activation(dst, ps[:, b, 0:DIM].rearrange("p (k t) -> p k t", k=KD), ACT.Copy)
                ins.then_inc(read[b], 1)

            with act.Fori(0, GROUPS) as g:
                for j in range(G):
                    turned(g, "n2T", j, affine=True)
                for c in range(K2):
                    b = bb.bank("fc1", c)
                    act.wait_ge(written[b], bb.made(g, "fc1", c))
                    act.activation(hidT[:, c, :], ps[:, b, :], ACT.Silu, bias=fc1_b[:, c:c + 1]).then_inc(read[b], 1)
                for j in range(G):
                    turned(g, "xxT", j)
                for j in range(G):
                    act.wait_ge(uvb_done, g * G + j + 1)
                    act.activation(uv[:, j, :], uv[:, j, :], ACT.Silu).then_inc(uv_done, 1)
                for j in range(G):
                    b = bb.bank("uyT", j)
                    act.wait_ge(written[b], bb.made(g, "uyT", j))
                    act.activation(uyT[:, j].rearrange("p k t -> p (k t)"), ps[:, b, :],
                                   ACT.Copy).then_inc(read[b], 1)
                for j in range(G):
                    turned(g, "xmT", j)
                for c in range(KS):
                    b = bb.bank("gate", c)
                    act.wait_ge(written[b], bb.made(g, "gate", c))
                    if c >= 2:
                        act.wait_ge(read[bb.bank("up", c - 2)], bb.made(g, "up", c - 2))
                    act.activation(sh_g[:, c % 2, :], ps[:, b, :], ACT.Silu).then_inc(read[b], 1)

            act.wait_ge(read[bb.bank("router", G - 1)], bb.made(GROUPS - 1, "router", G - 1))
            for j in range(G):
                act.wait_ge(h4_stored[j], 32 * GROUPS)
            act.activation(scores_sb, logits[:], ACT.Sigmoid).then_inc(scores_done, 1)

            def x_turned(g, j):
                b = d_bank("xgT", j)
                act.wait_ge(written[b], d_made(g, "xgT", j))
                act.activation(xgT[:, j % G].rearrange("p k t -> p (k t)"), ps[:, b, 0:DIM], ACT.Copy
                               ).then_inc(read[b], 1)

            def gated(g, j):
                b = d_bank("gu", j)
                act.wait_ge(written[b], d_made(g, "gu", j))
                act.activation(act_g[:, j % G, :], ps[:, b, 0:FE], ACT.Silu).then_inc(act_g_done, 1)

            def hidden_turned(g, j):
                b = d_bank("hT", j)
                act.wait_ge(written[b], d_made(g, "hT", j))
                act.activation(hT[:, j % G].rearrange("p k t -> p (k t)"), ps[:, b, 0:FE], ACT.Copy
                               ).then_inc(read[b], 1)

            pipeline(act, D_TURNS, GD, [(gated, GU_LAG), (hidden_turned, HID_LAG), (x_turned, X_LAG)])

        @block.vector
        def _(dve):
            dve.wait_ge(setup, 11)
            dve.tensor_reduce(head_parity[:], head_parity4[:].rearrange("p g c -> p c g"), AX.X,
                              ALU.add).then_inc(vec_setup, 1)
            dve.wait_ge(vec_setup, 1)
            dve.wait_ge(weights_in, 16 * 10)
            for c in range(2):
                dve.tensor_tensor(kb_par[:, c, :], head_parity[:], qkv_b[:, 2 + c:3 + c].to_broadcast([P, 2]),
                                  ALU.mult).then_inc(consts_done, 1)
            for j in range(G):
                for i in range(2):
                    dve.tensor_copy(vblk[:, j, i, :, :, HD], copy_parity[:].unsqueeze(1).to_broadcast([P, PAIRS, 2])
                                    ).then_inc(consts_done, 1)
            dve.wait_ge(quant_in, 64)
            for w in (fc1_w, fc2_w):
                dve.tensor_scalar(w[:], w[:].bitcast(I32), -128.0, None, ALU.add).then_inc(dequantised, 1)
            dve.wait_ge(dequantised, 2)
            for w, scales in ((fc1_w, sh_gu), (fc2_w, uv_w)):
                flat = w[:].rearrange("p k n -> p (k n)")
                dve.tensor_tensor(flat, flat, scales[:].rearrange("p k n -> p (k n)"), ALU.mult
                                  ).then_inc(dequantised, 1)
            def moments(src, st, out, stats_done, ready, number):
                n = src.shape[1]
                parts = (n + 511) // 512
                for i in range(parts):
                    dve.bn_stats(st[:, 6 * i:6 * i + 6], src[:, i * n // parts:(i + 1) * n // parts]
                                 ).then_inc(stats_done, 1)
                dve.wait_ge(stats_done, (number + 1) * parts)
                dve.sem_inc(vec_fence, 1)
                dve.bn_aggr(out, st[:, 0:6 * parts]).then_inc(ready, 1)

            def x_stats(g, j):
                j4 = j % G
                dve.wait_ge(x_loaded[j4], (g + (j // G + 1)) * 16)
                moments(x_in[:, j4, :], stats[:, j4, :], mv[:, 0, j4, :], stats_done[0], var_done[0], g * G + j)

            def x_normed(g, j):
                j4 = j % G
                dve.wait_ge(rstd_done[0], g * G + (j + 1))
                dve.tensor_scalar(x_n[:, j4, :], x_in[:, j4, :], mv[:, 0, j4, 0:1], rs[:, 0, j4:j4 + 1],
                                  ALU.subtract, ALU.mult).then_inc(xn_done, 1)

            def tok_stats(g, j):
                j4 = j % G
                dve.wait_ge(tok_mm, g * G + (j + 1))
                dve.tensor_tensor(t_lin[:, j4, :], ps[:, at.bank("tok", j), 0:DIM], tok_b[:], ALU.add
                                  ).then_inc(tok_free, 1)
                dve.wait_ge(tok_free, g * G + (j + 1))
                moments(t_lin[:, j4, :], stats2[:, j4, :], mv[:, 1, j4, :], stats_done[1], var_done[1], g * G + j)

            def h0_made(g, j):
                j4 = j % G
                dve.wait_ge(rstd_done[1], g * G + (j + 1))
                at_least(dve, hp_done, g * G + (j + 1 - G))
                dve.tensor_scalar(h0[:, j4, :], t_lin[:, j4, :], mv[:, 1, j4, 0:1], rs[:, 1, j4:j4 + 1],
                                  ALU.subtract, ALU.mult).then_inc(h0_part, 1)
                dve.wait_ge(h0_part, (g * G + j) * 2 + 1)
                dve.tensor_tensor(h0[:, j4, :], h0[:, j4, :], ln2_g[:], ALU.mult).then_inc(h0_part, 1)
                dve.wait_ge(h0_part, (g * G + j) * 2 + 2)
                dve.tensor_tensor(h0[:, j4, :], h0[:, j4, :], ln2_b[:], ALU.add).then_inc(h0_done, 1)
                dve.wait_ge(h0_done, g * G + (j + 1))
                moments(h0[:, j4, :], stats3[:, j4, :], mv[:, 2, j4, :], stats_done[2], var_done[2], g * G + j)

            def a_normed(g, j):
                j4 = j % G
                dve.wait_ge(rstd_done[2], g * G + (j + 1))
                dve.tensor_scalar(a_n[:, j4, :], h0[:, j4, :], mv[:, 2, j4, 0:1], rs[:, 2, j4:j4 + 1],
                                  ALU.subtract, ALU.mult).then_inc(an_done, 1)

            def v_read(g, j):
                dve.wait_ge(v_mm, g * G + (j + 1))
                dve.tensor_tensor(
                    vblk[:, j % G, :, :, :, 0:HD].rearrange("p i a c d -> p (i a) c d"),
                    ps[:, at.bank("v", j), :].rearrange("p (a c d) -> p a c d", c=2, d=HD),
                    copy_parity[:].unsqueeze(1).unsqueeze(3).to_broadcast([P, 2 * PAIRS, 2, HD]),
                    ALU.mult).then_inc(v_done, 1)

            def less_max(g, j):
                j4 = j % G
                dve.wait_ge(s_mm, g * G + (j + 1))
                s4 = ps_s[:, :, 0:256].rearrange("p g (a m) -> p g a m", m=64)
                dve.tensor_reduce(smax[:, j4, :].rearrange("p (g a) -> p g a", g=4), s4, AX.X, ALU.max
                                  ).then_inc(max_done, 1)
                dve.wait_ge(max_done, g * G + (j + 1))
                dve.tensor_tensor(e[:, j4].rearrange("p (g a) m -> p g a m", g=4), s4,
                                  smax[:, j4, :].rearrange("p (g a) -> p g a", g=4).unsqueeze(3)
                                  .to_broadcast([P, 4, 4, 64]), ALU.subtract).then_inc(s_sub, 1)

            def o_normed(g, j):
                j4 = j % G
                dve.wait_ge(pv_mm, g * G + (j + 1))
                pv = ps[:, at.bank("pv", j), 0:HEADS * (HD + 1)].rearrange("p (h d) -> p h d", d=HD + 1)
                dve.reciprocal(rsum[:, j4, :], pv[:, :, HD]).then_inc(rsum_done, 1)
                dve.wait_ge(rsum_done, g * G + (j + 1))
                dve.tensor_tensor(o_n[:, j4, :].rearrange("p (h d) -> p h d", d=HD), pv[:, :, 0:HD],
                                  rsum[:, j4, :].unsqueeze(2).to_broadcast([P, HEADS, HD]),
                                  ALU.mult).then_inc(o_done, 1)

            def h1_made(g, j):
                dve.wait_ge(proj_mm, g * G + (j + 1))
                dve.wait_ge(hp_done, g * G + (j + 1))
                at_least(dve, h1_stored[j % G], (g + j // G) * 16)
                dve.tensor_tensor(h1[:, j % G, :], ps[:, at.bank("proj", j), 0:DIM], hp[:, j % G, :], ALU.add
                                  ).then_inc(h1_done, 1)

            pipeline(dve, GROUPS, G, [(less_max, 3), (tok_stats, 1), (h1_made, 4), (x_stats, 0), (h0_made, 1),
                                      (x_normed, 0), (v_read, 2), (a_normed, 1), (o_normed, 3)])

            chain = Chain(dve, vec_chain_b, 3 * G)

            def b_moments(src, st, out):
                chain.wait(chain.step(dve.bn_stats(st, src)))
                dve.sem_inc(vec_fence, 1)
                dve.bn_aggr(out, st).then_inc(b_var, 1)

            def normed(out, which, j, r):
                return dve.tensor_scalar(out, res[:, j, :], mv[:, which, j, 0:1], r, ALU.subtract, ALU.mult)

            def mix_in(g, j):
                dve.wait_ge(b_scales, g * (3 * G) + G + j + 1)
                normed(nrm[:, j, :], 1, j, rs[:, 0, j:j + 1]).then_inc(qn_done, 1)
                normed(lin_in[:, j, :], 1, j, rs[:, 1, j:j + 1]).then_inc(xx_done, 1)

            def moe_in(g, j):
                dve.wait_ge(b_scales, g * (3 * G) + 2 * G + j + 1)
                normed(nrm[:, j, :], 2, j, rs[:, 2, j:j + 1]).then_inc(xm_done, 1)

            dve.wait_ge(b_weights_in, 16 * 13)
            with dve.Fori(0, GROUPS) as g:
                chain.turn(g)
                for j in range(G):
                    dve.wait_ge(h_loaded[j], g * 32 + 32)
                    b_moments(res[:, j, :], stats2[:, j, :], mv[:, 0, j, :])
                for j in range(G):
                    dve.wait_ge(xm_stored[j], g * 32)
                    dve.wait_ge(b_scales, g * (3 * G) + j + 1)
                    normed(nrm[:, j, :], 0, j, rs[:, 0, j:j + 1]).then_inc(n1_done, 1)
                    normed(lin_in[:, j, :], 0, j, rs[:, 1, j:j + 1]).then_inc(n2_done, 1)
                for j in range(G):
                    b = bb.bank("fc2", j)
                    dve.wait_ge(written[b], bb.made(g, "fc2", j))
                    dve.wait_ge(res1_done, g * G + j + 1)
                    dve.scalar_tensor_tensor(out=res[:, j, :], in0=ps[:, b, 0:DIM], scalar=0.5, in1=res[:, j, :],
                                             op0=ALU.mult, op1=ALU.add).then_inc(read[b], 1)
                    dve.wait_ge(read[b], bb.made(g, "fc2", j))
                    b_moments(res[:, j, :], stats3[:, j, :], mv[:, 1, j, :])
                    if j >= 1:
                        mix_in(g, j - 1)
                mix_in(g, G - 1)
                for j in range(G):
                    for h, stage in enumerate(("u", "v")):
                        b = bb.bank(stage, j)
                        dve.wait_ge(written[b], bb.made(g, stage, j))
                        ins = dve.tensor_tensor(uv[:, j, h * GF:(h + 1) * GF], ps[:, b, :], uv_b[:, h * GF:(h + 1) * GF],
                                                ALU.add)
                        ins.then_inc(read[b], 1)
                    dve.wait_ge(read[b], bb.made(g, "v", j))
                    dve.sem_inc(uvb_done, 1)
                for j in range(G):
                    b = bb.bank("mix", j)
                    dve.wait_ge(written[b], bb.made(g, "mix", j))
                    dve.tensor_tensor(uv[:, j, 0:GF], uv[:, j, 0:GF], ps[:, b, :], ALU.mult).then_inc(read[b], 1)
                for j in range(G):
                    b = bb.bank("o", j)
                    dve.wait_ge(written[b], bb.made(g, "o", j))
                    dve.wait_ge(res2_done, g * G + j + 1)
                    dve.tensor_tensor(res[:, j, :], ps[:, b, 0:DIM], res[:, j, :], ALU.add).then_inc(read[b], 1)
                    dve.wait_ge(read[b], bb.made(g, "o", j))
                    b_moments(res[:, j, :], stats3[:, j, :], mv[:, 2, j, :])
                    if j >= 1:
                        moe_in(g, j - 1)
                moe_in(g, G - 1)
                for j in range(G):
                    b = bb.bank("router", j)
                    dve.wait_ge(written[b], bb.made(g, "router", j))
                    dve.tensor_copy(logits[:, bass.ds(g * G + j, 1), :], ps[:, b, 0:EXPERTS].unsqueeze(1)
                                    ).then_inc(read[b], 1)
                for c in range(KS):
                    b = bb.bank("up", c)
                    dve.wait_ge(written[b], bb.made(g, "up", c))
                    dve.wait_ge(read[bb.bank("gate", c)], bb.made(g, "gate", c))
                    dve.tensor_tensor(shT[:, c, :], sh_g[:, c % 2, :], ps[:, b, :], ALU.mult).then_inc(read[b], 1)
                for j in range(G):
                    b = bb.bank("down", j)
                    dve.wait_ge(written[b], bb.made(g, "down", j))
                    dve.tensor_tensor(res[:, j, :], ps[:, b, 0:DIM], res[:, j, :], ALU.add).then_inc(read[b], 1)
                chain.end()

            cn = [0]

            def do(ins):
                cn[0] += 1
                ins.then_inc(vec_chain_c, 1)
                dve.wait_ge(vec_chain_c, cn[0])

            dve.wait_ge(scores_done, 1)
            dve.wait_ge(c_consts, 11)
            dve.wait_ge(router_b_in, 16)
            dve.wait_ge(slots_begun, 16)
            over_tiles = [P, TILES, EXPERTS]
            do(dve.tensor_tensor(biased, scores_sb, router_b[:].unsqueeze(1).to_broadcast(over_tiles), ALU.add))
            s4 = biased.rearrange("p t (g o) -> p (t g) o", o=OF_GROUP)
            do(dve.tensor_tensor(pair_sums[:, :, 0:3], s4[:, :, 0:3], s4[:, :, 1:4], ALU.add))
            do(dve.tensor_tensor(pair_sums[:, :, 3:5], s4[:, :, 0:2], s4[:, :, 2:4], ALU.add))
            do(dve.tensor_tensor(pair_sums[:, :, 5:6], s4[:, :, 0:1], s4[:, :, 3:4], ALU.add))
            do(dve.tensor_reduce(g_score.rearrange("p t g -> p (t g)"), pair_sums, AX.X, ALU.max))

            def ranks(out, v, tiles, n, a, b):
                shape = [P, tiles, n, n]
                mine, others = v.unsqueeze(3).to_broadcast(shape), v.unsqueeze(2).to_broadcast(shape)
                tri = below_e[:, 0:n, 0:n].unsqueeze(1).to_broadcast(shape)
                do(dve.tensor_tensor(b, others, mine, ALU.is_equal))
                do(dve.tensor_tensor(b, b, tri, ALU.mult))
                do(dve.tensor_tensor(a, others, mine, ALU.is_gt))
                do(dve.tensor_tensor(a, a, b, ALU.add))
                do(dve.tensor_reduce(out, a, AX.X, ALU.add))

            def part(x, tiles, n):
                return x.rearrange("p a b c -> p (a b c)")[:, 0:tiles * n * n].rearrange(
                    "p (t a b) -> p t a b", t=tiles, a=n)

            ranks(g_rank, g_score, TILES, EXPERT_GROUPS, part(cmp_a, TILES, EXPERT_GROUPS),
                  part(cmp_b, TILES, EXPERT_GROUPS))
            do(dve.tensor_scalar(g_rank, g_rank, float(TOP_GROUPS), None, ALU.is_lt))
            do(dve.tensor_scalar(g_less, g_rank, -1.0, None, ALU.add))
            per_group = [P, TILES * EXPERT_GROUPS, OF_GROUP]
            m4 = masked.rearrange("p t (g o) -> p (t g) o", o=OF_GROUP)
            do(dve.tensor_tensor(m4, s4, g_rank.rearrange("p t g -> p (t g)").unsqueeze(2).to_broadcast(per_group),
                                 ALU.mult))
            do(dve.tensor_tensor(m4, m4, g_less.rearrange("p t g -> p (t g)").unsqueeze(2).to_broadcast(per_group),
                                 ALU.add))
            for t in range(0, TILES, 8):
                ranks(rank_e[:, t:t + 8, :], masked[:, t:t + 8, :], 8, EXPERTS, cmp_a, cmp_b)
            dve.tensor_scalar(taken, rank_e, float(TOP), None, ALU.is_lt).then_inc(taken_done, 1)
            dve.wait_ge(taken_done, 1)
            do(dve.tensor_tensor(tw, scores_sb, taken, ALU.mult))
            do(dve.tensor_reduce(w_sum, tw, AX.X, ALU.add))
            do(dve.tensor_scalar(w_sum, w_sum, 1e-20, None, ALU.add))
            do(dve.reciprocal(w_sum, w_sum))
            do(dve.scalar_tensor_tensor(out=tw, in0=tw, scalar=ROUTE_SCALE, in1=w_sum.unsqueeze(2)
                                        .to_broadcast(over_tiles), op0=ALU.mult, op1=ALU.mult))
            dve.wait_ge(written[1], b_end[1] + 1)
            flat = "p t e -> p (t e)"
            dve.tensor_copy(totals.rearrange(flat), ps[:, 1, :]).then_inc(read[1], 1)
            dve.wait_ge(read[1], b_end[1] + 1)
            src, dst = totals, cum_a
            for d in (1, 2, 4, 8, 16):
                do(dve.tensor_copy(dst[:, 0:d, :], src[:, 0:d, :]))
                do(dve.tensor_tensor(dst[:, d:, :], src[:, d:, :], src[:, 0:TILES - d, :], ALU.add))
                src, dst = dst, (cum_b if dst is cum_a else cum_a)
            cum = src
            do(dve.tensor_scalar(padded, cum[:, TILES - 1, :], float(P - 1), None, ALU.add))
            do(dve.tensor_copy(ends_a.bitcast(I32), padded))
            do(dve.tensor_scalar(ends_a.bitcast(I32), ends_a.bitcast(I32), 7, 7, ALU.logical_shift_right,
                                 ALU.logical_shift_left))
            do(dve.tensor_copy(padded, ends_a.bitcast(I32)))
            src, dst = padded, ends_a
            for d in (1, 2, 4, 8):
                do(dve.tensor_copy(dst[:, 0:d], src[:, 0:d]))
                do(dve.tensor_tensor(dst[:, d:], src[:, d:], src[:, 0:EXPERTS - d], ALU.add))
                src, dst = dst, (ends_b if dst is ends_a else ends_a)
            ends = src
            do(dve.tensor_tensor(base, ends, padded, ALU.subtract))
            for t in range(0, SLOT_TILES, P):
                n = min(P, SLOT_TILES - t)
                shape = [P, n, EXPERTS]
                do(dve.tensor_tensor(cmp_b.rearrange("p a b c -> p (a b c)")[:, 0:n * EXPERTS]
                                     .rearrange("p (t e) -> p t e", e=EXPERTS),
                                     ends.unsqueeze(1).to_broadcast(shape),
                                     tile_start[:, t:t + n].unsqueeze(2).to_broadcast(shape), ALU.is_le))
                do(dve.tensor_reduce(tile_e[:, t:t + n], cmp_b.rearrange("p a b c -> p (a b c)")[:, 0:n * EXPERTS]
                                     .rearrange("p (t e) -> p t e", e=EXPERTS), AX.X, ALU.add))
            do(dve.tensor_scalar(tile_e, tile_e, float(EXPERTS - 1), None, ALU.min))
            dve.tensor_copy(tile_expert[:], tile_e).then_inc(experts_known, 1)
            do(dve.tensor_tensor(cum, cum, totals, ALU.subtract))
            do(dve.tensor_tensor(cum, cum, base.unsqueeze(1).to_broadcast(over_tiles), ALU.add))
            dve.wait_ge(written[0], b_end[0] + 1)
            dve.tensor_tensor(slot_no.rearrange(flat), ps[:, 0, :], cum.rearrange(flat), ALU.add).then_inc(read[0], 1)
            dve.wait_ge(read[0], b_end[0] + 1)
            for k in range(TOP):
                for what, to in ((slot_no, choice_slot), (tw, choice_w)):
                    do(dve.scalar_tensor_tensor(out=picked, in0=rank_e, scalar=float(k), in1=what,
                                                op0=ALU.is_equal, op1=ALU.mult))
                    do(dve.tensor_reduce(to[:, :, k], picked, AX.X, ALU.add))
            do(dve.tensor_copy(choice_tile.bitcast(I32), choice_slot))
            do(dve.tensor_scalar(choice_tile.bitcast(I32), choice_tile.bitcast(I32), 7, None,
                                 ALU.logical_shift_right))
            do(dve.tensor_copy(choice_at, choice_tile.bitcast(I32)))
            do(dve.tensor_scalar(choice_at, choice_at, float(1 - P * SLOT_TILES), None, ALU.mult))
            do(dve.scalar_tensor_tensor(out=choice_at, in0=choice_slot, scalar=float(SLOT_TILES), in1=choice_at,
                                        op0=ALU.mult, op1=ALU.add))
            dve.tensor_copy(recs[:, :, :, 0], choice_at).then_inc(recs_done, 1)
            recs_f = recs[:].bitcast(F32)
            dve.tensor_copy(recs_f[:, :, :, 1], token_row.unsqueeze(2).to_broadcast([P, TILES, TOP])
                            ).then_inc(recs_done, 1)
            dve.tensor_copy(recs_f[:, :, :, 2], choice_w).then_inc(recs_done, 1)
            dve.wait_ge(slots_in, 16)
            dve.tensor_copy(slot_rows[:], slots[:, :, 0]).then_inc(rows_done, 1)

            def hidden(g, j):
                b = d_bank("gu", j)
                dve.wait_ge(act_g_done, g * GD + (j + 1))
                dve.tensor_tensor(hid[:, j % G, :], act_g[:, j % G, :], ps[:, b, FE:2 * FE], ALU.mult
                                  ).then_inc(read[b], 1)

            def weighed(g, j):
                b = d_bank("down", j)
                dve.wait_ge(written[b], d_made(g, "down", j))
                at_least(dve, added[j % G], (g * 2 + j // G) * 16)
                dve.tensor_scalar(y[:, j % G, :], ps[:, b, 0:DIM], slots[:, bass.ds(g * GD + j, 1), 1]
                                  if not isinstance(g, int) else slots[:, g * GD + j, 1:2], None, ALU.mult
                                  ).then_inc(read[b], 1)

            pipeline(dve, D_TURNS, GD, [(hidden, GU_LAG), (weighed, DOWN_LAG)])

        @block.tensor
        def _(pe):
            pe.wait_ge(consts_done, 2 + 2 * G)
            pe.wait_ge(weights_in, 16 * 10)

            def x_turn(g, j):
                pe.wait_ge(xn_done, g * G + (j + 1))
                turn_banks.free(pe, g, "xnT", j)
                for k in range(KX):
                    ins = pe.transpose(ps_t[:, k // 4, (k % 4) * P:(k % 4 + 1) * P],
                                       x_n[:, j % G, k * P:(k + 1) * P], ident[:])
                ins.then_inc(xnT_mm, 1)

            def patches_out(g, j):
                pe.wait_ge(xnT_done, g * G + (j + 1))
                b = at.free(pe, g, "tok", j)
                for k in range(KX):
                    ins = pe.matmul(ps[:, b, 0:DIM], x_nT[:, j % G, k, :], tok_w[:, k, :],
                                    start=(k == 0), stop=(k == KX - 1))
                ins.then_inc(tok_mm, 1)

            def a_turn(g, j):
                pe.wait_ge(an_done, g * G + (j + 1))
                b = at.free(pe, g, "anT", j)
                for k in range(KD):
                    ins = pe.transpose(ps[:, b, k * P:(k + 1) * P], a_n[:, j % G, k * P:(k + 1) * P], ident[:])
                ins.then_inc(anT_mm, 1)

            def queries_keys(g, j):
                pe.wait_ge(aT_done, g * G + (j + 1))
                b = at.free(pe, g, "qk", j)
                for c in range(4):
                    for k in range(KD):
                        ins = pe.matmul(ps[:, b, c * P:(c + 1) * P], qkv_w[:, k, c * P:(c + 1) * P],
                                        aT[:, j % G, k, :, 0, :], start=(k == 0), stop=(k == KD - 1))
                ins.then_inc(qk_mm, 1)

            def values(g, j):
                b = at.free(pe, g, "v", j)
                for i in range(2):
                    for k in range(KD):
                        ins = pe.matmul(ps[:, b, i * DIM:(i + 1) * DIM],
                                        aT[:, j % G, k, i].rearrange("p c t -> p (c t)"),
                                        qkv_w[:, k, 2 * DIM:3 * DIM], start=(k == 0), stop=(k == KD - 1))
                ins.then_inc(v_mm, 1)

            def scores(g, j):
                pe.wait_ge(qk_done, g * G + (j + 1))
                at_least(pe, s_sub, g * G + j)
                for c in range(2):
                    for i in range(2):
                        for r in range(4):
                            ins = pe.matmul(ps_s[64 * i:64 * i + 64, r, c * P:(c + 1) * P],
                                            qT[32 * r:32 * r + 32, j % G, c, 64 * i:64 * i + 64],
                                            kT[32 * r:32 * r + 32, j % G, c, :, 64 * i:64 * i + 64],
                                            start=True, stop=True)
                ins.then_inc(s_mm, 1)

            def p_turn(g, j):
                pe.wait_ge(e_done, g * G + (j + 1))
                turn_banks.free(pe, g, "pT", j)
                for a in range(PAIRS):
                    ins = pe.transpose(ps_t[:, a // 4, (a % 4) * P:(a % 4 + 1) * P],
                                       e[:, j % G, 2 * a:2 * a + 2].rearrange("p c m -> p (c m)"), ident[:])
                ins.then_inc(pT_mm, 1)

            def heads_out(g, j):
                pe.wait_ge(pT_done, g * G + (j + 1))
                pe.wait_ge(v_done, g * G + (j + 1))
                b = at.free(pe, g, "pv", j)
                for i in range(2):
                    for a in range(PAIRS):
                        ins = pe.matmul(ps[64 * i:64 * i + 64, b, a * 34:a * 34 + 34],
                                        pT[:, j % 2, a, 64 * i:64 * i + 64],
                                        vblk[:, j % G, i, a].rearrange("p c d -> p (c d)"), start=True, stop=True)
                ins.then_inc(pv_mm, 1)

            def o_turn(g, j):
                pe.wait_ge(o_done, g * G + (j + 1))
                b = at.free(pe, g, "oT", j)
                for k in range(KD):
                    ins = pe.transpose(ps[:, b, k * P:(k + 1) * P], o_n[:, j % G, k * P:(k + 1) * P], ident[:])
                ins.then_inc(oT_mm, 1)

            def project(g, j):
                pe.wait_ge(oT_done, g * G + (j + 1))
                b = at.free(pe, g, "proj", j)
                for k in range(KD):
                    ins = pe.matmul(ps[:, b, 0:DIM], oT[:, j % G, k, :], proj_w[:, k, :],
                                    start=(k == 0), stop=(k == KD - 1))
                ins.then_inc(proj_mm, 1)

            pipeline(pe, GROUPS, G, [(scores, 3), (o_turn, 4), (x_turn, 1), (patches_out, 1), (project, 4),
                                     (queries_keys, 2), (p_turn, 3), (values, 2), (heads_out, 3), (a_turn, 1)])

            pe.wait_ge(b_weights_in, 16 * 13)
            pe.wait_ge(dequantised, 4)
            pe.wait_ge(h1_done, TILES)

            def opened(g, stage, j):
                b = bb.bank(stage, j)
                pe.wait_ge(read[b], bb.before(g, stage, j))
                return b

            def turn(g, stage, j, src, chunks, ready, count):
                pe.wait_ge(ready, count)
                b = opened(g, stage, j)
                for k in range(chunks):
                    ins = pe.transpose(ps[:, b, k * P:(k + 1) * P], src[:, k * P:(k + 1) * P], ident[:])
                ins.then_inc(written[b], 1)

            def arrived(g, stage, j):
                pe.wait_ge(read[bb.bank(stage, j)], bb.made(g, stage, j))

            def tokens_out(g, stage, j, left, right, chunks, width):
                b = opened(g, stage, j)
                for k in range(chunks):
                    ins = pe.matmul(ps[:, b, 0:width], left(k), right(k), start=(k == 0), stop=(k == chunks - 1))
                ins.then_inc(written[b], 1)

            def features_out(g, stage, c, w, col):
                b = opened(g, stage, c)
                for k in range(KD):
                    ins = pe.matmul(ps[:, b, :], w[:, k, col:col + P], nT[:, k, :], start=(k == 0), stop=(k == KD - 1))
                ins.then_inc(written[b], 1)

            with pe.Fori(0, GROUPS) as g:
                for j in range(G):
                    turn(g, "n2T", j, lin_in[:, j, :], KD, n2_done, g * G + j + 1)
                for j in range(G):
                    arrived(g, "n2T", j)
                for c in range(K2):
                    features_out(g, "fc1", c, fc1_w, c * P)
                for c in range(K2):
                    arrived(g, "fc1", c)
                for j in range(G):
                    tokens_out(g, "fc2", j, lambda k: hidT[:, k, j * P:(j + 1) * P], lambda k: fc2_w[:, k, :], K2, DIM)
                for j in range(G):
                    turn(g, "xxT", j, lin_in[:, j, :], KD, xx_done, g * G + j + 1)
                for j in range(G):
                    arrived(g, "xxT", j)
                    for h, stage in enumerate(("u", "v")):
                        tokens_out(g, stage, j, lambda k: nT[:, k, j * P:(j + 1) * P],
                                   lambda k: uv_w[:, k, h * GF:(h + 1) * GF], KD, GF)
                for j in range(G):
                    pe.wait_ge(uv_done, g * G + j + 1)
                    b = opened(g, "mix", j)
                    for h in range(MIX_HEADS):
                        ins = pe.matmul(ps[:, b, h * MIX_HD:(h + 1) * MIX_HD], mix_w[:, h, :],
                                        uv[:, j, GF + h * MIX_HD:GF + (h + 1) * MIX_HD], start=True, stop=True)
                    ins.then_inc(written[b], 1)
                for j in range(G):
                    m = bb.bank("mix", j)
                    turn(g, "uyT", j, uv[:, j, 0:GF], KG, read[m], bb.made(g, "mix", j))
                for j in range(G):
                    arrived(g, "uyT", j)
                    tokens_out(g, "o", j, lambda k: uyT[:, j, k, :], lambda k: o_w[:, k, :], KG, DIM)
                for j in range(G):
                    turn(g, "xmT", j, nrm[:, j, :], KD, xm_done, g * G + j + 1)
                for j in range(G):
                    arrived(g, "xmT", j)
                    tokens_out(g, "router", j, lambda k: nT[:, k, j * P:(j + 1) * P], lambda k: router_w[:, k, :],
                               KD, EXPERTS)
                for c in range(KS):
                    features_out(g, "gate", c, sh_gu, c * P)
                    features_out(g, "up", c, sh_gu, FS + c * P)
                for c in range(KS):
                    arrived(g, "up", c)
                for j in range(G):
                    tokens_out(g, "down", j, lambda k: shT[:, k, j * P:(j + 1) * P], lambda k: sh_d[:, k, :], KS, DIM)

            pe.wait_ge(taken_done, 1)
            pe.wait_ge(c_consts, 11)
            for b, left in ((0, earlier), (1, ones)):
                pe.wait_ge(read[b], b_end[b])
                pe.matmul(ps[:, b, :], left[:], taken.rearrange("p t e -> p (t e)"), start=True, stop=True
                          ).then_inc(written[b], 1)

            pe.wait_ge(experts_in, 32)
            pe.wait_ge(experts_known, 1)

            def d_open(g, stage, j):
                b = d_bank(stage, j)
                pe.wait_ge(read[b], d_before(g, stage, j))
                return b

            def expert_of(g, j):
                where = tile_expert[0:1, g * GD + j:g * GD + j + 1] if isinstance(g, int) else \
                    tile_expert[0:1, bass.ds(g * GD + j, 1)]
                return pe.value_load(where, min_val=0, max_val=EXPERTS - 1)

            def gu(g, j):
                x = d_bank("xgT", j)
                e_of = expert_of(g, j)
                pe.wait_ge(read[x], d_made(g, "xgT", j))
                b = d_open(g, "gu", j)
                for k in range(KD):
                    ins = pe.matmul(ps[:, b, :], xgT[:, j % G, k, :],
                                    expert_gu[:, bass.ds(e_of, 1), k, :].rearrange("p e n -> p (e n)"),
                                    start=(k == 0), stop=(k == KD - 1))
                ins.then_inc(written[b], 1)

            def turn_hidden(g, j):
                pe.wait_ge(read[d_bank("gu", j)], d_made(g, "gu", j))
                b = d_open(g, "hT", j)
                for k in range(KFE):
                    ins = pe.transpose(ps[:, b, k * P:(k + 1) * P], hid[:, j % G, k * P:(k + 1) * P], ident[:])
                ins.then_inc(written[b], 1)

            def turn_x(g, j):
                pe.wait_ge(gathered[j % G], (g * 2 + (j // G + 1)) * 16)
                b = d_open(g, "xgT", j)
                for k in range(KD):
                    ins = pe.transpose(ps[:, b, k * P:(k + 1) * P], xg[:, j % G, k * P:(k + 1) * P], ident[:])
                ins.then_inc(written[b], 1)

            def down(g, j):
                e_of = expert_of(g, j)
                pe.wait_ge(read[d_bank("hT", j)], d_made(g, "hT", j))
                b = d_open(g, "down", j)
                for k in range(KFE):
                    ins = pe.matmul(ps[:, b, 0:DIM], hT[:, j % G, k, :],
                                    expert_d[:, bass.ds(e_of, 1), k, :].rearrange("p e n -> p (e n)"),
                                    start=(k == 0), stop=(k == KFE - 1))
                ins.then_inc(written[b], 1)

            pipeline(pe, D_TURNS, GD, [(gu, GU_LAG), (turn_hidden, HID_LAG), (turn_x, X_LAG), (down, DOWN_LAG)])


def layouts(np, x, L0_tok_ln1_g, L0_tok_ln1_b, L0_tok_W, L0_tok_b, L0_tok_ln2_g, L0_tok_ln2_b, L0_attn_qkv_w,
            L0_attn_qkv_b, L0_attn_proj_w, L0_attn_proj_b, L0_ffn_ln_gamma, L0_ffn_ln_beta, L0_ffn_fc1_q,
            L0_ffn_fc1_scales, L0_ffn_fc1_bias, L0_ffn_fc2_q, L0_ffn_fc2_scales, L0_ffn_fc2_bias, L1_attn_u_w,
            L1_attn_u_b, L1_attn_v_w, L1_attn_v_b, L1_attn_o_w, L1_attn_o_b, L1_attn_pos, L1_attn_zero, L1_attn_neg,
            L1_ffn_router_w, L1_ffn_bias, L1_ffn_gate_w, L1_ffn_up_w, L1_ffn_down_w, L1_ffn_sh_gate_w,
            L1_ffn_sh_up_w, L1_ffn_sh_down_w, **unused):
    tokens = x.reshape(64, 3, 8, 16, 8, 16).transpose(0, 2, 4, 3, 5, 1).reshape(TOKENS, PIX)
    order = [8 * c + 2 * r + par for r in range(4) for c in range(2) for par in range(2)]
    cols = np.concatenate([np.arange(16 * h, 16 * h + 16) for h in order])
    v_w = L0_attn_qkv_w[:, 512:][:, cols]
    qkv_w = np.concatenate([L0_attn_qkv_w[:, :512], v_w], axis=1)
    qkv_b = np.concatenate([L0_attn_qkv_b[:512], L0_attn_qkv_b[512:][cols]])
    taps = np.concatenate([L1_attn_neg[:, :IMAGES - 1][:, ::-1], L1_attn_zero, L1_attn_pos[:, :IMAGES - 1]], axis=1)
    j, i = np.arange(IMAGES)[:, None], np.arange(IMAGES)[None, :]
    mix = taps[:, i - j + IMAGES - 1].transpose(1, 0, 2)
    return {
        "fc1_q": L0_ffn_fc1_q, "fc1_s": L0_ffn_fc1_scales, "fc1_b": L0_ffn_fc1_bias.reshape(K2, P).T,
        "fc2_q": L0_ffn_fc2_q, "fc2_s": L0_ffn_fc2_scales, "fc2_b": L0_ffn_fc2_bias,
        "ln3_g": L0_ffn_ln_gamma.reshape(KD, P).T, "ln3_b": L0_ffn_ln_beta.reshape(KD, P).T,
        "uv_w": np.concatenate([L1_attn_u_w.T, L1_attn_v_w.T], axis=1), "uv_b": np.concatenate([L1_attn_u_b, L1_attn_v_b]),
        "mix": mix, "o_w": L1_attn_o_w.T, "o_b": L1_attn_o_b, "router_w": L1_ffn_router_w.T,
        "router_b": L1_ffn_bias,
        "sh_gu": np.concatenate([L1_ffn_sh_gate_w, L1_ffn_sh_up_w], axis=1), "sh_d": L1_ffn_sh_down_w,
        "expert_gu": np.concatenate([L1_ffn_gate_w, L1_ffn_up_w], axis=2), "expert_d": L1_ffn_down_w,
        "x": tokens, "ln1_g": L0_tok_ln1_g.reshape(6, P).T, "ln1_b": L0_tok_ln1_b.reshape(6, P).T,
        "tok_w": L0_tok_W.T, "tok_b": L0_tok_b, "ln2_g": L0_tok_ln2_g, "ln2_b": L0_tok_ln2_b,
        "qkv_w": qkv_w, "qkv_b": qkv_b.reshape(6, P).T, "proj_w": L0_attn_proj_w[cols, :], "proj_b": L0_attn_proj_b,
    }


def kernel(**inputs):
    import numpy as np
    import concourse.bacc as bacc
    from concourse.bass_utils import run_bass_kernel_spmd

    arrays = {"in_" + k: np.ascontiguousarray(v) for k, v in layouts(np, **inputs).items()}
    nc = bacc.Bacc("TRN2", target_bir_lowering=False, num_devices=1)
    io = {k[3:]: nc.dram_tensor(k, a.shape, mybir.dt.from_np(a.dtype), kind="ExternalInput").ap()
          for k, a in arrays.items()}
    io["out"] = nc.dram_tensor("out", (TOKENS + PAD_ROWS, DIM), F32, kind="ExternalOutput").ap()
    build(nc, io)
    r = run_bass_kernel_spmd(nc, [arrays], core_ids=[0])
    return r.results[0]["out"][:TOKENS].reshape(IMAGES, PATCHES, DIM)
```

```python
from contextlib import ExitStack

import concourse.bass as bass
from concourse import mybir

F32 = mybir.dt.float32
I32 = mybir.dt.int32
ALU = mybir.AluOpType
ACT = mybir.ActivationFunctionType
AX = mybir.AxisListType

P = 128
IMAGES, PATCHES, DIM = 64, 64, 256
TOKENS = IMAGES * PATCHES
TILES = TOKENS // P
G = 4
GROUPS = TILES // G
PIX = 768
KX = PIX // P
KD = DIM // P
HEADS, HD = 16, 16
PAIRS = HEADS // 2
EPS = 1e-5
F0 = 1024
K1, K2 = DIM // P, F0 // P
GF = 512
MIX_HEADS, MIX_HD = 8, 64
KG = GF // P
EXPERTS, FE = 16, 256
KFE = FE // P
TOP, EXPERT_GROUPS, TOP_GROUPS, ROUTE_SCALE = 4, 4, 2, 2.5
OF_GROUP = EXPERTS // EXPERT_GROUPS
SLOT_TILES = -(-(TOKENS * TOP // P + EXPERTS - 1) // 8) * 8
GD = 8
assert SLOT_TILES % GD == 0
BLOCKS = TOKENS // P
C_CONSTS = 15
COMBINE = 4
PAD_ROWS = P
FS = 512
KS = FS // P
H = 2
ITEMS = TILES // H
B_PER = 4
B_TURNS = ITEMS // B_PER
WORK = 9728


class Chain:

    def __init__(self, eng, sem, per=0):
        self.eng, self.sem, self.per, self.n, self.base = eng, sem, per, 0, 0

    def turn(self, g, start=0):
        self.n = 0
        self.base = g * self.per + start

    def step(self, ins):
        self.n += 1
        ins.then_inc(self.sem, 1)
        return self.base + self.n

    def wait(self, value):
        self.eng.wait_ge(self.sem, value)

    def end(self):
        assert self.n == self.per, (self.n, self.per)


class Shelf:

    def __init__(self, ap):
        self.ap, self.at = ap, 0

    def take(self, shape):
        n = 1
        for d in shape[1:]:
            n *= d
        assert self.at + n <= self.ap.shape[1], (self.at, n, self.ap.shape)
        ap = self.ap[:, self.at:self.at + n]
        self.at += n
        if len(shape) == 2:
            return ap
        letters = "abcdef"[:len(shape) - 1]
        names = " ".join(letters)
        return ap.rearrange(f"p ({names}) -> p {names}", **dict(zip(letters[1:], shape[2:])))


def at_least(eng, sem, value):
    if not isinstance(value, int) or value > 0:
        eng.wait_ge(sem, value)


def span(start, n):
    return slice(start, start + n) if isinstance(start, int) else bass.ds(start, n)


def pipeline(eng, turns, per, stages, peel=1):
    total = turns * per

    def steps(g, count):
        for j in range(count):
            for fn, lag in stages:
                if not isinstance(g, int) or 0 <= g * per + j - lag < total:
                    fn(g, j - lag)

    for g in range(peel):
        steps(g, per)
    with eng.Fori(peel, turns) as g:
        steps(g, per)
    steps(turns, max(lag for _, lag in stages))


class Turns:

    def __init__(self, uses, per, turns, read, first, banks, peel=1):
        self.uses, self.per, self.turns, self.read, self.peel = uses, per, turns, read, peel
        self.place = {(stage, off % per[stage]): i for i, (stage, off) in enumerate(uses)}
        assert len(self.place) == len(uses)
        self.first, self.banks = first, banks

    def bank(self, stage, off):
        return self.first + self.place[stage, off % self.per[stage]] % self.banks

    def free(self, pe, g, stage, off):
        at = self.place[stage, off % self.per[stage]]
        turn = (off - self.uses[at][1]) // self.per[stage]
        back = 0
        k = at
        while True:
            k -= 1
            if k < 0:
                k, back = len(self.uses) - 1, back + 1
            if k % self.banks != at % self.banks:
                continue
            other, there = self.uses[k]
            n = self.per[other]
            if isinstance(g, int):
                number = (g + turn - back) * n + there
                if number < 0 and back > 3:
                    break
                if 0 <= number < self.turns * n:
                    pe.wait_ge(self.read[other], number + 1)
                    break
            else:
                assert turn == 0 and (self.peel - back) * n + there >= 0, (stage, off, other, there)
                pe.wait_ge(self.read[other], g * n + (there + 1 - back * n))
                break
        return self.bank(stage, off)


def build(nc, io, debug=()):
    with ExitStack() as ctx:
        def sb(name, shape, dt=F32):
            return ctx.enter_context(nc.sbuf_tensor(name, shape, dt))

        def psum(name, shape, dt=F32):
            return ctx.enter_context(nc.psum_tensor(name, shape, dt))

        def sem(name):
            return ctx.enter_context(nc.semaphore(name))

        def dram(name, shape, dt=F32):
            kind = "ExternalOutput" if name in debug else "Internal"
            return nc.dram_tensor(name, shape, dt, kind=kind).ap()

        h1_dram = dram("h1_dram", (TOKENS, DIM))
        xm_dram = dram("xm_dram", (TOKENS + PAD_ROWS, DIM))
        recs_dram = dram("recs_dram", ((EXPERTS * BLOCKS + 1) * P, 2))
        odd_out = dram("odd_out", (TOKENS + PAD_ROWS, DIM))
        out = io["out"]

        ident = sb("ident", [P, P])
        one_col = sb("one_col", [P, 1])
        eps_col = sb("eps_col", [P, 1])
        mhalf_col = sb("mhalf_col", [P, 1])
        head_parity4 = sb("head_parity4", [P, 4, 2])
        head_parity = sb("head_parity", [P, 2])
        copy_parity = sb("copy_parity", [P, 2])
        ln1_gb = sb("ln1_gb", [P, 2, KX])
        tok_b = sb("tok_b", [P, DIM])
        ln2_g = sb("ln2_g", [P, DIM])
        ln2_b = sb("ln2_b", [P, DIM])
        proj_b = sb("proj_b", [P, DIM])
        qkv_b = sb("qkv_b", [P, 6])
        kb_par = sb("kb_par", [P, 2, 2])

        fc1_w = sb("fc1_w", [P, K1, F0])
        fc2_w = sb("fc2_w", [P, K2, DIM])
        fc1_b = sb("fc1_b", [P, K2])
        ln3_gb = sb("ln3_gb", [P, 2, KD])
        fc2_b = sb("fc2_b", [P, DIM])
        uv_w = sb("uv_w", [P, KD, 2 * GF])
        uv_b = sb("uv_b", [P, 2 * GF])
        mix_w = sb("mix_w", [P, MIX_HEADS, P])
        o_w = sb("o_w", [P, KG, DIM])
        o_b = sb("o_b", [P, DIM])
        router_w = sb("router_w", [P, KD, EXPERTS])
        sh_gu = sb("sh_gu", [P, KD, 2 * FS])
        sh_d = sb("sh_d", [P, KS, DIM])
        half_col = sb("half_col", [P, 1])
        one_neg = sb("one_neg", [P, 1])
        tiny_col = sb("tiny_col", [P, 1])

        expert_gu = sb("expert_gu", [P, EXPERTS, KD, 2 * FE])
        expert_d = sb("expert_d", [P, EXPERTS, KFE, DIM])
        work = sb("work", [P, WORK])

        in_gu = Shelf(expert_gu[:].rearrange("p e k n -> p (e k n)"))
        in_d = Shelf(expert_d[:].rearrange("p e k n -> p (e k n)"))
        in_work = Shelf(work[:])
        tok_w = in_work.take([P, KX, DIM])
        qkv_w = in_work.take([P, KD, 3 * DIM])
        proj_w = in_work.take([P, KD, DIM])
        x_in = in_gu.take([P, G, PIX])
        x_n = in_gu.take([P, G, PIX])
        x_nT = in_gu.take([P, G, KX, P])
        t_lin = in_gu.take([P, G, DIM])
        h0 = in_gu.take([P, G, DIM])
        hp = in_gu.take([P, G, DIM])
        a_n = in_gu.take([P, G, DIM])
        aT = in_gu.take([P, G, KD, 2, 2, 64])
        qT = in_gu.take([P, G, 2, P])
        kT = in_d.take([P, G, 2, 2, P])
        vblk = in_d.take([P, G, 2, PAIRS, 2, HD + 1])
        e = in_work.take([P, G, HEADS, 64])
        pT = in_d.take([P, 2, PAIRS, P])
        o_n = in_d.take([P, G, DIM])
        oT = in_work.take([P, G, KD, P])
        h1 = in_work.take([P, G, DIM])
        stats = sb("stats", [P, G, 12])
        stats2 = sb("stats2", [P, G, 6])
        stats3 = sb("stats3", [P, G, 6])
        mv = sb("mv", [P, 3, G, 2])
        ve = sb("ve", [P, 3, G])
        rs = sb("rs", [P, 3, G])
        smax = sb("smax", [P, G, HEADS])
        rsum = sb("rsum", [P, G, HEADS])

        in_work_b = Shelf(work[:])
        in_d_b = Shelf(expert_d[:].rearrange("p e k n -> p (e k n)"))
        res = in_work_b.take([P, 4, H, DIM])
        res3 = in_work_b.take([P, 2, H, DIM])
        n1 = in_work_b.take([P, 2, H, DIM])
        n2 = in_work_b.take([P, 2, H, DIM])
        qn = in_work_b.take([P, 2, H, DIM])
        xx = in_work_b.take([P, 2, H, DIM])
        xm = in_work_b.take([P, 2, H, DIM])
        n2T_s = in_d_b.take([P, 2, KD, H * P])
        xxT_s = in_d_b.take([P, 2, KD, H * P])
        xmT_s = in_d_b.take([P, 2, KD, H * P])
        hidT = in_d_b.take([P, K2, H * P])
        uv = in_d_b.take([P, H, 2 * GF])
        uyT_s = in_d_b.take([P, H, KG, P])
        shT = in_work_b.take([P, KS, H * P])
        sh_g = in_work_b.take([P, 2, H * P])
        b_mv = sb("b_mv", [P, 3, 2, H, 2])
        b_st = sb("b_st", [P, 3, H, 6])
        b_var1 = sb("b_var1", [P, 3, H])
        b_rs = sb("b_rs", [P, 3, 2, 2, H])

        router_b = sb("router_b", [P, EXPERTS])
        ones = sb("ones", [P, P])
        earlier = sb("earlier", [P, P])
        below_e = sb("below_e", [P, EXPERTS, EXPERTS])
        zeros = sb("zeros", [P, DIM])
        tile_expert = sb("tile_expert", [P, SLOT_TILES], I32)
        slot_rows = sb("slot_rows", [P, SLOT_TILES], I32)
        slot_w = sb("slot_w", [P, SLOT_TILES])
        pad_recs = sb("pad_recs", [P, P, 2])
        rank_no = sb("rank_no", [P, TOP, EXPERTS])
        token_row = sb("token_row", [P, TILES])
        tile_no = sb("tile_no", [P, SLOT_TILES])
        my_tile = sb("my_tile", [P, 2])
        first_rec = sb("first_rec", [P, EXPERTS])
        recs = sb("recs", [P, 2, H, TOP, 3], I32)
        next_rec = sb("next_rec", [P, EXPERTS])
        scores = sb("scores", [P, 2, H, EXPERTS])
        biased, masked, rank_e, taken, tw, rec_no = (sb(n, [P, H, EXPERTS]) for n in (
            "biased", "masked", "rank_e", "taken", "tw", "rec_no"))
        pair_sums = sb("pair_sums", [P, H * EXPERT_GROUPS, 6])
        g_score, g_rank, g_less = (sb(n, [P, H, EXPERT_GROUPS]) for n in ("g_score", "g_rank", "g_less"))
        cmp_a, cmp_b = (sb(n, [P, H, EXPERTS, EXPERTS]) for n in ("cmp_a", "cmp_b"))
        is_choice, picked = (sb(n, [P, H, TOP, EXPERTS]) for n in ("is_choice", "picked"))
        w_sum = sb("w_sum", [P, H])
        choice_rec = sb("choice_rec", [P, H, TOP])
        counts, padded, ends_a, ends_b = (sb(n, [P, EXPERTS]) for n in ("counts", "padded", "ends_a", "ends_b"))
        started, starts = (sb(n, [P, 2, EXPERTS]) for n in ("started", "starts"))
        my_e, my_start, my_block = (sb(n, [P, 2]) for n in ("my_e", "my_start", "my_block"))
        block_rows = sb("block_rows", [P, 2], I32)
        tile_e = sb("tile_e", [P, SLOT_TILES])
        gather_rows = sb("gather_rows", [P, GD], I32)
        add_rows = sb("add_rows", [P, GD], I32)
        in_d2 = Shelf(work[:])
        slot_recs = in_d2.take([P, 2, 2 * P])
        ends_at = in_d2.take([P, SLOT_TILES, EXPERTS])
        xg = in_d2.take([P, G, DIM])
        xgT = in_d2.take([P, G, KD, P])
        act_g = in_d2.take([P, G, FE])
        hid = in_d2.take([P, G, FE])
        hT = in_d2.take([P, G, KFE, P])
        y = in_d2.take([P, G, DIM])

        ps = psum("ps", [P, 8, 512])
        ps_s = ps[:, 0:4, :]
        ps_t = ps[:, 4:6, :]
        ps_g = ps[:, 6:8, :]

        weights_in = sem("weights_in")
        setup = sem("setup")
        consts_done = sem("consts_done")
        vec_setup = sem("vec_setup")
        vec_fence = sem("vec_fence")
        x_loaded = [sem(f"x_loaded{j}") for j in range(G)]
        var_done = [sem(f"var_done{n}") for n in range(3)]
        ve_done = [sem(f"ve_done{n}") for n in range(3)]
        rstd_done = [sem(f"rstd_done{n}") for n in range(3)]
        stats_done = [sem(f"stats_done{n}") for n in range(3)]
        h0_part = sem("h0_part")
        h0_done = sem("h0_done")
        max_done = sem("max_done")
        rsum_done = sem("rsum_done")
        xn_done = sem("xn_done")
        xnT_mm = sem("xnT_mm")
        xnT_done = sem("xnT_done")
        tok_mm = sem("tok_mm")
        an_done = sem("an_done")
        tok_free = sem("tok_free")
        anT_mm = sem("anT_mm")
        aT_done = sem("aT_done")
        qk_mm = sem("qk_mm")
        qk_done = sem("qk_done")
        v_mm = sem("v_mm")
        v_done = sem("v_done")
        s_mm = sem("s_mm")
        s_sub = sem("s_sub")
        e_done = sem("e_done")
        pT_mm = sem("pT_mm")
        pT_done = sem("pT_done")
        pv_mm = sem("pv_mm")
        o_done = sem("o_done")
        oT_mm = sem("oT_mm")
        oT_done = sem("oT_done")
        proj_mm = sem("proj_mm")
        hp_done = sem("hp_done")
        h1_done = sem("h1_done")
        h1_stored = [sem(f"h1_stored{j}") for j in range(G)]

        a_steps = [("oT", 4), ("tok", 1), ("qk", 2), ("proj", 4), ("v", 2), ("pv", 3), ("anT", 1)]
        at = Turns([(stage, j - lag) for j in range(G) for stage, lag in a_steps],
                   {stage: G for stage, _ in a_steps}, GROUPS,
                   dict(oT=oT_done, tok=tok_free, proj=h1_done, qk=qk_done, v=v_done, pv=o_done, anT=aT_done), 6, 2)
        turn_banks = Turns([(stage, j - lag) for j in range(G) for stage, lag in (("pT", 3), ("xnT", 0))],
                           dict(xnT=G, pT=G), GROUPS, dict(xnT=xnT_done, pT=pT_done), 4, 1)

        b_weights_in = sem("b_weights_in")
        quant_in = sem("quant_in")
        dequantised = sem("dequantised")
        mix_zeroed = sem("mix_zeroed")
        pool_fence = sem("pool_fence")
        experts_in = sem("experts_in")
        pool_setup = sem("pool_setup")
        h_loaded = [sem(f"h_loaded{j}") for j in range(4)]
        b_stats = [sem(f"b_stats{n}") for n in range(3)]
        b_var = [sem(f"b_var{n}") for n in range(3)]
        b_scales = [sem(f"b_scales{n}") for n in range(3)]
        n1_done = sem("n1_done")
        n2_done = sem("n2_done")
        qn_done = sem("qn_done")
        xx_done = sem("xx_done")
        xm_done = sem("xm_done")
        res1_done = sem("res1_done")
        res2_done = sem("res2_done")
        uv_done = sem("uv_done")
        shg_done = sem("shg_done")
        xm_stored = [sem(f"xm_stored{j}") for j in range(2)]
        h4_stored = [sem(f"h4_stored{j}") for j in range(2)]
        pool_chain_b = [sem(f"pool_chain_b{n}") for n in range(5)]
        PRODUCTS = {"n2T": 1, "fc1": K2 // 2, "fc2": 1, "xxT": 1, "uv": 2 * H, "mix": H, "uyT": H, "o": 1,
                    "xmT": 1, "router": 1, "gu": KS, "down": 1, "count": 1}
        b_made = {stage: sem(f"{stage}_made") for stage in PRODUCTS}
        b_read = {stage: sem(f"{stage}_read") for stage in PRODUCTS}
        B_STEPS = [("fc1", 1), ("xxT", 2), ("uyT", 3), ("gu", 4), ("o", 3), ("count", 4), ("down", 4), ("uv", 2), ("fc2", 1),
                   ("n2T", 0), ("xmT", 3), ("mix", 2), ("router", 3)]
        b_banks = Turns([(stage, (j - lag) * PRODUCTS[stage] + c) for j in range(B_PER) for stage, lag in B_STEPS
                         for c in range(PRODUCTS[stage])],
                        {stage: n * B_PER for stage, n in PRODUCTS.items()}, B_TURNS, b_read, 0, 8)

        def b_count(g, stage, j, c):
            n = PRODUCTS[stage]
            return g * (B_PER * n) + (j * n + c + 1)

        def b_bank(stage, j, c=0):
            return b_banks.bank(stage, j * PRODUCTS[stage] + c)

        def made(eng, g, stage, j, c=0):
            at_least(eng, b_made[stage], b_count(g, stage, j, c))

        def was_read(eng, g, stage, j, c=0):
            at_least(eng, b_read[stage], b_count(g, stage, j, c))

        def item(g, j):
            return g * B_PER + j

        d_written = {stage: sem(f"d_{stage}_written") for stage in ("gu", "hT", "xgT", "down")}
        d_read = {stage: sem(f"d_{stage}_read") for stage in ("gu", "hT", "xgT", "down")}

        router_b_in = sem("router_b_in")
        zeros_stored = sem("zeros_stored")
        c_consts = sem("c_consts")
        recs_begun = sem("recs_begun")
        taken_done = sem("taken_done")
        choose_chain = sem("choose_chain")
        place_chain = sem("place_chain")
        vec_chain_c = sem("vec_chain_c")
        recs_done = sem("recs_done")
        recs_scattered = sem("recs_scattered")
        recs_free = sem("recs_free")
        blocks_known = sem("blocks_known")
        experts_known = sem("experts_known")
        slot_recs_in = sem("slot_recs_in")
        slot_recs_turned = sem("slot_recs_turned")
        rows_done = sem("rows_done")
        gather_rows_done = sem("gather_rows_done")
        add_rows_done = sem("add_rows_done")
        combined = sem("combined")
        gathered = [sem(f"gathered{j}") for j in range(G)]
        act_g_done = sem("act_g_done")
        added = [sem(f"added{j}") for j in range(G)]

        D_BANK = {"gu": 0, "hT": 2, "xgT": 4, "down": 6}

        def d_bank(stage, j):
            return D_BANK[stage] + j % 2

        def d_before(g, stage, j):
            return g * GD + (j - 1)

        def d_made(g, stage, j):
            return g * GD + (j + 1)

        D_TURNS = SLOT_TILES // GD
        X_LAG, GU_LAG, HID_LAG, DOWN_LAG = 0, 1, 2, 3


        block = ctx.enter_context(nc.Block())

        @block.sync
        def _(sp):
            def row(dst, src):
                sp.dma_start(dst, src.rearrange("(a n) -> a n", a=1).to_broadcast([P, src.shape[0]])
                             ).then_inc(weights_in, 16)

            def load_x(g, j):
                at_least(sp, xn_done, g * G + (j + 1 - G))
                sp.dma_start(x_in[:, j % G, :], io["x"][span((g * G + j) * P, P), :]).then_inc(x_loaded[j % G], 16)

            load_x(0, 0)
            sp.dma_start(tok_w[:], io["tok_w"].rearrange("(k p) n -> p k n", p=P)).then_inc(weights_in, 16)
            sp.dma_start(ln1_gb[:, 0, :], io["ln1_g"]).then_inc(weights_in, 16)
            sp.dma_start(ln1_gb[:, 1, :], io["ln1_b"]).then_inc(weights_in, 16)
            row(tok_b[:], io["tok_b"])
            for j in range(1, G):
                load_x(0, j)
            row(ln2_g[:], io["ln2_g"])
            row(ln2_b[:], io["ln2_b"])
            row(proj_b[:], io["proj_b"])
            sp.dma_start(qkv_w[:], io["qkv_w"].rearrange("(k p) n -> p k n", p=P)).then_inc(weights_in, 16)
            sp.dma_start(qkv_b[:], io["qkv_b"]).then_inc(weights_in, 16)
            sp.dma_start(proj_w[:], io["proj_w"].rearrange("(k p) n -> p k n", p=P)).then_inc(weights_in, 16)

            sp.dma_start(fc1_w[:].bitcast(I32), io["fc1_q"].rearrange("(k p) n -> p k n", p=P)).then_inc(quant_in, 16)
            sp.dma_start(fc2_w[:].bitcast(I32), io["fc2_q"].rearrange("(k p) n -> p k n", p=P)).then_inc(quant_in, 16)
            for dst, src in ((sh_gu, io["fc1_s"]), (uv_w, io["fc2_s"])):
                sp.dma_start(dst[:].rearrange("p k n -> p (k n)"), src.rearrange("k n -> (k n)")
                             .rearrange("(a n) -> a n", a=1).to_broadcast([P, 2 * F0])).then_inc(quant_in, 16)

            def b_row(dst, src):
                sp.dma_start(dst, src.rearrange("(a n) -> a n", a=1).to_broadcast([P, src.shape[0]])
                             ).then_inc(b_weights_in, 16)
            sp.dma_start(router_b[:], io["router_b"].rearrange("(a n) -> a n", a=1).to_broadcast([P, EXPERTS])
                         ).then_inc(router_b_in, 16)
            sp.wait_ge(c_consts, C_CONSTS)
            last = EXPERTS * BLOCKS * P
            sp.dma_start(recs_dram[0:last, :].rearrange("(q b x) c -> q b (x c)", q=P, x=P),
                         pad_recs[:].rearrange("p x c -> p (x c)").unsqueeze(1)
                         .to_broadcast([P, EXPERTS * BLOCKS // P, 2 * P])).then_inc(recs_begun, 16)
            sp.dma_start(recs_dram[last:, :].rearrange("(a x) c -> a (x c)", a=1),
                         pad_recs[0:1].rearrange("p x c -> p (x c)")).then_inc(recs_begun, 16)
            sp.dma_start(xm_dram[TOKENS:, :], zeros[:]).then_inc(zeros_stored, 16)
            sp.dma_start(out[TOKENS:, :], zeros[:]).then_inc(zeros_stored, 16)
            sp.dma_start(odd_out.rearrange("(p r) d -> p r d", p=P),
                         zeros[:].unsqueeze(1).to_broadcast([P, (TOKENS + PAD_ROWS) // P, DIM])
                         ).then_inc(zeros_stored, 16)
            b_row(fc2_b[:], io["fc2_b"])
            b_row(uv_b[:], io["uv_b"])
            b_row(o_b[:], io["o_b"])
            sp.dma_start(fc1_b[:], io["fc1_b"]).then_inc(b_weights_in, 16)
            sp.dma_start(ln3_gb[:, 0, :], io["ln3_g"]).then_inc(b_weights_in, 16)
            sp.dma_start(ln3_gb[:, 1, :], io["ln3_b"]).then_inc(b_weights_in, 16)
            sp.wait_ge(mix_zeroed, 1)
            for i in range(2):
                sp.dma_start(mix_w[64 * i:64 * i + 64, :, 64 * i:64 * i + 64], io["mix"]).then_inc(b_weights_in, 16)
            sp.dma_start(o_w[:], io["o_w"].rearrange("(k p) n -> p k n", p=P)).then_inc(b_weights_in, 16)
            sp.dma_start(router_w[:], io["router_w"].rearrange("(k p) n -> p k n", p=P)).then_inc(b_weights_in, 16)
            sp.dma_start(sh_d[:], io["sh_d"].rearrange("(k p) n -> p k n", p=P)).then_inc(b_weights_in, 16)

            with sp.Fori(1, GROUPS) as g:
                for j in range(G):
                    load_x(g, j)
            sp.wait_ge(dequantised, 4)
            sp.dma_start(sh_gu[:], io["sh_gu"].rearrange("(k p) n -> p k n", p=P)).then_inc(b_weights_in, 16)
            sp.dma_start(uv_w[:], io["uv_w"].rearrange("(k p) n -> p k n", p=P)).then_inc(b_weights_in, 16)

            h1_by_item = h1_dram.rearrange("(i q t s) d -> s i q t d", q=ITEMS, t=H, s=2)
            xm_by_item = xm_dram[0:TOKENS, :].rearrange("(i q t s) d -> s i q t d", q=ITEMS, t=H, s=2)
            out_by_item = out[0:TOKENS, :].rearrange("(i q t s) d -> s i q t d", q=ITEMS, t=H, s=2)
            for j in range(G):
                sp.wait_ge(h1_stored[j], 16 * GROUPS + 16)
            sp.wait_ge(h1_done, TILES)

            def of_item(by_item, s_, g, j):
                return by_item[s_][:, span(item(g, j), 1), :, :].rearrange("i q t d -> i (q t) d")

            def load_h1(g, j):
                was_read(sp, g, "o", j - 4)
                for i in range(2):
                    sp.dma_start(res[64 * i:64 * i + 64, j % 4], of_item(h1_by_item, i, g, j)
                                 ).then_inc(h_loaded[j % 4], 16)

            def store_out(g, j):
                was_read(sp, g, "down", j)
                for i in range(2):
                    sp.dma_start(of_item(out_by_item, i, g, j), res3[64 * i:64 * i + 64, j % 2]
                                 ).then_inc(h4_stored[j % 2], 16)

            def store_xm(g, j):
                at_least(sp, xm_done, (item(g, j) + 1) * H)
                for i in range(2):
                    sp.dma_start(of_item(xm_by_item, i, g, j), xm[64 * i:64 * i + 64, j % 2]
                                 ).then_inc(xm_stored[j % 2], 16)

            def load_experts(g, j):
                if isinstance(g, int) and item(g, j) == 3:
                    sp.dma_start(expert_gu[:], io["expert_gu"].rearrange("e (k p) n -> p e k n", p=P)
                                 ).then_inc(experts_in, 16)

            pipeline(sp, B_TURNS, B_PER, [(load_h1, 0), (load_experts, 0), (store_out, 5), (store_xm, 4)], peel=2)
            sp.dma_start(expert_d[:], io["expert_d"].rearrange("e (k p) n -> p e k n", p=P)).then_inc(experts_in, 16)
            for j in range(2):
                sp.wait_ge(h4_stored[j], 16 * ITEMS + 16)
                sp.wait_ge(xm_stored[j], 16 * ITEMS + 16)

        @block.gpsimd
        def _(pool):
            pool.memset(mix_w[:], 0.0).then_inc(mix_zeroed, 1)
            pool.memset(ident[:], 0.0).then_inc(setup, 1)
            pool.memset(one_col[:], 1.0).then_inc(setup, 1)
            pool.memset(eps_col[:], EPS).then_inc(setup, 1)
            pool.memset(mhalf_col[:], -0.5).then_inc(setup, 1)
            pool.memset(head_parity4[:], 1.0).then_inc(setup, 1)
            pool.memset(copy_parity[:], 1.0).then_inc(setup, 1)
            pool.wait_ge(setup, 6)
            pool.affine_select(out=ident[:], in_=ident[:], compare_op=ALU.not_equal, fill=1.0, base=0,
                               pattern=[[-1, P]], channel_multiplier=1).then_inc(setup, 1)
            pool.affine_select(out=head_parity4[:], in_=head_parity4[:], compare_op=ALU.is_ge, fill=0.0, base=0,
                               pattern=[[-32, 4], [-16, 2]], channel_multiplier=1).then_inc(setup, 1)
            pool.affine_select(out=copy_parity[:], in_=copy_parity[:], compare_op=ALU.is_ge, fill=0.0, base=0,
                               pattern=[[-64, 2]], channel_multiplier=1).then_inc(setup, 1)
            pool.wait_ge(setup, 9)
            pool.affine_select(out=head_parity4[:], in_=head_parity4[:], compare_op=ALU.is_ge, fill=0.0, base=15,
                               pattern=[[32, 4], [16, 2]], channel_multiplier=-1).then_inc(setup, 1)
            pool.affine_select(out=copy_parity[:], in_=copy_parity[:], compare_op=ALU.is_ge, fill=0.0, base=63,
                               pattern=[[64, 2]], channel_multiplier=-1).then_inc(setup, 1)

            pool.memset(ones[:], 1.0).then_inc(c_consts, 1)
            pool.memset(earlier[:], 1.0).then_inc(c_consts, 1)
            pool.memset(below_e[:], 1.0).then_inc(c_consts, 1)
            pool.memset(zeros[:], 0.0).then_inc(c_consts, 1)
            pool.wait_ge(c_consts, 4)
            pool.affine_select(out=earlier[:], in_=earlier[:], compare_op=ALU.is_gt, fill=0.0, base=0,
                               pattern=[[1, P]], channel_multiplier=-1).then_inc(c_consts, 1)
            pool.affine_select(out=below_e[:], in_=below_e[:], compare_op=ALU.is_gt, fill=0.0, base=0,
                               pattern=[[1, EXPERTS], [-1, EXPERTS]], channel_multiplier=0).then_inc(c_consts, 1)
            def iota(dst, pattern, base, by_partition):
                pool.iota(dst, pattern=pattern, base=base, channel_multiplier=by_partition,
                          allow_small_or_imprecise_dtypes=True).then_inc(c_consts, 1)

            iota(rank_no[:], [[1, TOP], [0, EXPERTS]], 0, 0)
            iota(tile_no[:], [[1, SLOT_TILES]], 0, 0)
            iota(my_tile[:], [[P, 2]], 0, 1)
            iota(first_rec[:], [[BLOCKS * P, EXPERTS]], 0, 0)
            iota(next_rec[:], [[BLOCKS * P, EXPERTS]], 0, 0)
            for i in range(2):
                pool.wait_ge(c_consts, 11 + i)
                iota(token_row[64 * i:64 * i + 64, :], [[2, TILES]], i, PATCHES)
            pool.wait_ge(c_consts, 13)
            iota(pad_recs[:, :, 0], [[1, P]], TOKENS, 0)
            pool.memset(pad_recs[:, :, 1], 0.0).then_inc(c_consts, 1)
            pool.memset(half_col[:], 0.5).then_inc(pool_setup, 1)
            pool.memset(one_neg[:], -1.0).then_inc(pool_setup, 1)
            pool.memset(tiny_col[:], 1e-8).then_inc(pool_setup, 1)

            pool.wait_ge(setup, 11)
            def rstd(g, which, j, ready):
                j4 = j % G
                pool.wait_ge(ready, g * G + (j + 1))
                pool.tensor_tensor(ve[:, which, j4:j4 + 1], mv[:, which, j4, 1:2], eps_col[:], ALU.add
                                   ).then_inc(ve_done[which], 1)
                pool.wait_ge(ve_done[which], g * G + (j + 1))
                pool.tensor_tensor(rs[:, which, j4:j4 + 1], ve[:, which, j4:j4 + 1], mhalf_col[:],
                                   ALU.pow).then_inc(rstd_done[which], 1)

            def with_bias(g, j):
                pool.wait_ge(h0_done, g * G + (j + 1))
                pool.tensor_tensor(hp[:, j % G, :], h0[:, j % G, :], proj_b[:], ALU.add).then_inc(hp_done, 1)

            pipeline(pool, GROUPS, G, [
                (lambda g, j: rstd(g, 0, j, var_done[0]), 0),
                (lambda g, j: rstd(g, 1, j, var_done[1]), 1),
                (lambda g, j: rstd(g, 2, j, var_done[2]), 1),
                (with_bias, 1)])

            pool.wait_ge(pool_setup, 3)
            pool.wait_ge(b_weights_in, 16 * 13)
            pool.tensor_tensor(fc2_b[:], fc2_b[:], half_col[:].to_broadcast([P, DIM]), ALU.mult).then_inc(pool_setup, 1)
            pool.wait_ge(pool_setup, 4)
            scales_chain = [Chain(pool, pool_chain_b[n], (6 * B_PER, 7 * B_PER, B_PER)[n]) for n in range(3)]
            res_chain = [Chain(pool, pool_chain_b[3 + n], B_PER) for n in range(2)]

            def stepper(chain, g, j, per_item):
                chain.turn(g, j * per_item)

                def tt(out, a, b, op):
                    chain.wait(chain.step(pool.tensor_tensor(out, a, b, op)))
                return tt

            def wide(col):
                return col[:].to_broadcast([P, H])

            def scales1(g, j):
                t, r1, r2 = b_var1[:, 0], b_rs[:, 0, j % 2, 0], b_rs[:, 0, j % 2, 1]
                var = b_mv[:, 0, j % 2, :, 1]
                at_least(pool, b_var[0], (item(g, j) + 1) * H)
                tt = stepper(scales_chain[0], g, j, 6)
                tt(t, var, wide(eps_col), ALU.add)
                tt(r1, t, wide(mhalf_col), ALU.pow)
                tt(t, var, r1, ALU.mult)
                tt(t, t, r1, ALU.mult)
                tt(t, t, wide(eps_col), ALU.add)
                tt(r2, t, wide(mhalf_col), ALU.pow)
                pool.tensor_tensor(r2, r2, r1, ALU.mult).then_inc(b_scales[0], 1)

            def residual1(g, j):
                tt = stepper(res_chain[0], g, j, 1)
                at_least(pool, n1_done, (item(g, j) + 1) * H)
                at_least(pool, n2_done, (item(g, j) + 1) * H)
                tt(res[:, j % 4], res[:, j % 4], n1[:, j % 2], ALU.add)
                pool.tensor_tensor(res[:, j % 4], res[:, j % 4], fc2_b[:].unsqueeze(1).to_broadcast([P, H, DIM]),
                                   ALU.add).then_inc(res1_done, 1)

            def scales2(g, j):
                t, r1, r2 = b_var1[:, 1], b_rs[:, 1, j % 2, 0], b_rs[:, 1, j % 2, 1]
                var = b_mv[:, 1, j % 2, :, 1]
                at_least(pool, b_var[1], (item(g, j) + 1) * H)
                tt = stepper(scales_chain[1], g, j, 7)
                tt(t, var, wide(eps_col), ALU.add)
                tt(r1, t, wide(mhalf_col), ALU.pow)
                tt(t, var, r1, ALU.mult)
                tt(t, t, r1, ALU.mult)
                tt(t, t, wide(half_col), ALU.pow)
                tt(t, t, wide(tiny_col), ALU.add)
                tt(r2, t, wide(one_neg), ALU.pow)
                pool.tensor_tensor(r2, r2, r1, ALU.mult).then_inc(b_scales[1], 1)

            def residual2(g, j):
                tt = stepper(res_chain[1], g, j, 1)
                at_least(pool, qn_done, (item(g, j) + 1) * H)
                at_least(pool, xx_done, (item(g, j) + 1) * H)
                tt(res[:, j % 4], res[:, j % 4], qn[:, j % 2], ALU.add)
                pool.tensor_tensor(res[:, j % 4], res[:, j % 4], o_b[:].unsqueeze(1).to_broadcast([P, H, DIM]),
                                   ALU.add).then_inc(res2_done, 1)

            def scales3(g, j):
                at_least(pool, b_var[2], (item(g, j) + 1) * H)
                tt = stepper(scales_chain[2], g, j, 1)
                tt(b_var1[:, 2], b_mv[:, 2, j % 2, :, 1], wide(eps_col), ALU.add)
                pool.tensor_tensor(b_rs[:, 2, j % 2, 0], b_var1[:, 2], wide(mhalf_col), ALU.pow
                                   ).then_inc(b_scales[2], 1)

            def scatter(g, j):
                at_least(pool, recs_done, (item(g, j) + 1) * 3)
                pool.sem_inc(pool_fence, 1)
                for t in range(H):
                    for k in range(TOP):
                        rec = recs[:, j % 2, t, k, :]
                        pool.indirect_dma_start(
                            recs_dram, bass.IndirectOffsetOnAxis(ap=rec[:, 0:1], axis=0),
                            rec[:, 1:3].bitcast(F32), None).then_inc(recs_scattered, 16)
                at_least(pool, recs_scattered, (item(g, j) + 1) * (16 * TOP * H))
                pool.sem_inc(recs_free, 1)

            pool.wait_ge(recs_begun, 32)
            pipeline(pool, B_TURNS, B_PER, [(scales1, 0), (residual2, 2), (scales3, 3), (residual1, 0), (scales2, 1),
                                            (scatter, 4)])

            for j in range(2):
                pool.wait_ge(h4_stored[j], 16 * ITEMS + 16)
                pool.wait_ge(xm_stored[j], 16 * ITEMS + 16)
            pool.wait_ge(blocks_known, 1)
            for c in range(2):
                pool.indirect_dma_start(slot_recs[:, c, :], None, recs_dram.rearrange("(b x) c -> b (x c)", x=P),
                                        bass.IndirectOffsetOnAxis(ap=block_rows[:, c:c + 1], axis=0)
                                        ).then_inc(slot_recs_in, 16)

            pool.wait_ge(rows_done, 2)
            pool.wait_ge(zeros_stored, 48)

            def rows_of_group(dst, done, g, j):
                j8 = j % GD
                src = slot_rows[:, bass.ds(g * GD + j, G)] if not isinstance(g, int) else \
                    slot_rows[:, g * GD + j:g * GD + j + G]
                pool.tensor_copy(dst[:, j8:j8 + G], src).then_inc(done, 1)

            def gather(g, j):
                if j % G == 0:
                    at_least(pool, gathered[0], (g * 2 + (j // G - 1)) * 16)
                    pool.sem_inc(pool_fence, 1)
                    rows_of_group(gather_rows, gather_rows_done, g, j)
                    pool.wait_ge(gather_rows_done, g * 2 + (j // G + 1))
                if not isinstance(g, int) or g * GD + j >= G:
                    pool.wait_ge(d_written["xgT"], d_made(g, "xgT", j - G))
                    pool.sem_inc(pool_fence, 1)
                pool.indirect_dma_start(xg[:, j % G, :], None, xm_dram,
                                        bass.IndirectOffsetOnAxis(ap=gather_rows[:, j % GD:j % GD + 1], axis=0)
                                        ).then_inc(gathered[j % G], 16)

            def add_out(g, j):
                j8 = j % GD
                if j % G == 0:
                    rows_of_group(add_rows, add_rows_done, g, j)
                    pool.wait_ge(add_rows_done, g * 2 + (j // G + 1))
                pool.wait_ge(d_read["down"], d_made(g, "down", j))
                at_least(pool, added[(j - 2) % G], (g * 2 + ((j - 2) // G + 1)) * 16)
                pool.sem_inc(pool_fence, 1)
                pool.indirect_dma_start(out if j % 2 == 0 else odd_out,
                                        bass.IndirectOffsetOnAxis(ap=add_rows[:, j8:j8 + 1], axis=0),
                                        y[:, j % G, :], None, compute_op=ALU.add).then_inc(added[j % G], 16)

            pipeline(pool, D_TURNS, GD, [(gather, 0), (add_out, 6)])
            for k in range(G):
                pool.wait_ge(added[k], 16 * SLOT_TILES // G)
            for k in range(COMBINE):
                rows = slice(k * (TOKENS // COMBINE), (k + 1) * (TOKENS // COMBINE))
                pool.dma_start(out[rows, :], odd_out[rows, :], accum_op=ALU.add,
                               max_dma_last_dim=4 * DIM).then_inc(combined, 16)
            pool.wait_ge(combined, 16 * COMBINE)

        @block.scalar
        def _(act):
            act.wait_ge(weights_in, 16 * 10)
            def x_turned(g, j):
                act.wait_ge(xnT_mm, g * G + (j + 1))
                for k in range(KX):
                    ins = act.activation(x_nT[:, j % G, k, :], ps_t[:, k // 4, (k % 4) * P:(k % 4 + 1) * P],
                                         ACT.Identity, scale=ln1_gb[:, 0, k:k + 1], bias=ln1_gb[:, 1, k:k + 1])
                ins.then_inc(xnT_done, 1)

            def a_turned(g, j):
                act.wait_ge(anT_mm, g * G + (j + 1))
                src = ps[:, at.bank("anT", j), 0:DIM].rearrange("p (a t) -> p a t", t=64)
                act.activation(aT[:, j % G].rearrange("p k i c t -> p (k i) c t"),
                               src.unsqueeze(2).to_broadcast([P, 2 * KD, 2, 64]), ACT.Copy).then_inc(aT_done, 1)

            def qk_read(g, j):
                if isinstance(g, int) and g * G + j == 0:
                    act.wait_ge(consts_done, 2 + 2 * G)
                act.wait_ge(qk_mm, g * G + (j + 1))
                b = at.bank("qk", j)
                for c in range(2):
                    act.activation(qT[:, j % G, c, :], ps[:, b, c * P:(c + 1) * P], ACT.Identity,
                                   bias=qkv_b[:, c:c + 1])
                for c in range(2):
                    for par in range(2):
                        ins = act.activation(kT[:, j % G, c, par, :], ps[:, b, (2 + c) * P:(3 + c) * P],
                                             ACT.Identity, scale=head_parity[:, par:par + 1],
                                             bias=kb_par[:, c, par:par + 1])
                ins.then_inc(qk_done, 1)

            def exponentials(g, j):
                act.wait_ge(s_sub, g * G + (j + 1))
                act.activation(e[:, j % G], e[:, j % G], ACT.Exp, scale=HD ** -0.5).then_inc(e_done, 1)

            def p_turned(g, j):
                act.wait_ge(pT_mm, g * G + (j + 1))
                act.activation(pT[:, j % 2].rearrange("p a t -> p (a t)"),
                               ps_t[:].rearrange("p b n -> p (b n)"), ACT.Copy).then_inc(pT_done, 1)

            def o_turned(g, j):
                act.wait_ge(oT_mm, g * G + (j + 1))
                b = at.bank("oT", j)
                for k in range(KD):
                    ins = act.activation(oT[:, j % G, k, :], ps[:, b, k * P:(k + 1) * P], ACT.Identity,
                                         bias=qkv_b[:, 4 + k:5 + k])
                ins.then_inc(oT_done, 1)

            def store_h1(g, j):
                act.wait_ge(h1_done, g * G + (j + 1))
                rows = h1_dram[(g * G + j) * P:(g * G + j + 1) * P, :] if isinstance(g, int) else \
                    h1_dram[bass.ds((g * G + j) * P, P), :]
                act.dma_start(rows, h1[:, j % G, :]).then_inc(h1_stored[j % G], 16)

            pipeline(act, GROUPS, G, [(o_turned, 4), (exponentials, 3), (qk_read, 2), (store_h1, 4), (p_turned, 3),
                                      (a_turned, 1), (x_turned, 0)])
            for j in range(G):
                act.wait_ge(h1_stored[j], 16 * GROUPS + 16)

            act.wait_ge(b_weights_in, 16 * 13)

            def turned(stage, dst):
                def copy(g, j):
                    made(act, g, stage, j)
                    src = ps[:, b_bank(stage, j), :].rearrange("p (t k m) -> p t k m", t=H, k=KD)
                    for k in range(KD):
                        to = dst[:, j % 2, k, :].rearrange("p (t m) -> p t m", t=H)
                        if stage == "n2T":
                            ins = act.activation(to, src[:, :, k, :], ACT.Identity,
                                                 scale=ln3_gb[:, 0, k:k + 1], bias=ln3_gb[:, 1, k:k + 1])
                        else:
                            ins = act.activation(to, src[:, :, k, :], ACT.Copy)
                    ins.then_inc(b_read[stage], 1)
                return copy

            def ffn_hidden(g, j):
                for c in range(K2 // 2):
                    made(act, g, "fc1", j, c)
                    for k in range(2):
                        ins = act.activation(hidT[:, 2 * c + k, :], ps[:, b_bank("fc1", j, c), k * H * P:(k + 1) * H * P],
                                             ACT.Silu, bias=fc1_b[:, 2 * c + k:2 * c + k + 1])
                    ins.then_inc(b_read["fc1"], 1)

            def uv_active(g, j):
                for t in range(H):
                    was_read(act, g, "uv", j, 2 * t + 1)
                    act.activation(uv[:, t, :], uv[:, t, :], ACT.Silu).then_inc(uv_done, 1)

            def uy_turned(g, j):
                for t in range(H):
                    made(act, g, "uyT", j, t)
                    act.activation(uyT_s[:, t].rearrange("p k m -> p (k m)"), ps[:, b_bank("uyT", j, t), :],
                                   ACT.Copy).then_inc(b_read["uyT"], 1)

            def shared_gate(g, j):
                for c in range(KS):
                    made(act, g, "gu", j, c)
                    if c >= 2:
                        was_read(act, g, "gu", j, c - 2)
                    act.activation(sh_g[:, c % 2, :], ps[:, b_bank("gu", j, c), 0:H * P], ACT.Silu
                                   ).then_inc(shg_done, 1)

            def router_scores(g, j):
                made(act, g, "router", j)
                act.activation(scores[:, j % 2].rearrange("p t e -> p (t e)"),
                               ps[:, b_bank("router", j), 0:H * EXPERTS], ACT.Sigmoid).then_inc(b_read["router"], 1)

            pipeline(act, B_TURNS, B_PER, [(ffn_hidden, 1), (turned("xxT", xxT_s), 2), (uy_turned, 3), (shared_gate, 4),
                                           (uv_active, 2), (turned("n2T", n2T_s), 0), (turned("xmT", xmT_s), 3),
                                           (router_scores, 3)])

            def x_turned(g, j):
                b = d_bank("xgT", j)
                act.wait_ge(d_written["xgT"], d_made(g, "xgT", j))
                act.activation(xgT[:, j % G].rearrange("p k t -> p (k t)"), ps[:, b, 0:DIM], ACT.Copy
                               ).then_inc(d_read["xgT"], 1)

            def gated(g, j):
                b = d_bank("gu", j)
                act.wait_ge(d_written["gu"], d_made(g, "gu", j))
                act.activation(act_g[:, j % G, :], ps[:, b, 0:FE], ACT.Silu).then_inc(act_g_done, 1)

            def hidden_turned(g, j):
                b = d_bank("hT", j)
                act.wait_ge(d_written["hT"], d_made(g, "hT", j))
                act.activation(hT[:, j % G].rearrange("p k t -> p (k t)"), ps[:, b, 0:FE], ACT.Copy
                               ).then_inc(d_read["hT"], 1)

            pipeline(act, D_TURNS, GD, [(gated, GU_LAG), (hidden_turned, HID_LAG), (x_turned, X_LAG)])

        @block.vector
        def _(dve):
            for stored in h1_stored + h4_stored + xm_stored:
                dve.sem_inc(stored, 16)
            dve.sem_inc(recs_free, 2)
            dve.wait_ge(setup, 11)
            dve.tensor_reduce(head_parity[:], head_parity4[:].rearrange("p g c -> p c g"), AX.X,
                              ALU.add).then_inc(vec_setup, 1)
            dve.wait_ge(vec_setup, 1)
            for j in range(G):
                for i in range(2):
                    dve.tensor_copy(vblk[:, j, i, :, :, HD], copy_parity[:].unsqueeze(1).to_broadcast([P, PAIRS, 2])
                                    ).then_inc(consts_done, 1)
            def moments(src, st, out, stats_done, ready, number):
                n = src.shape[1]
                parts = (n + 511) // 512
                for i in range(parts):
                    dve.bn_stats(st[:, 6 * i:6 * i + 6], src[:, i * n // parts:(i + 1) * n // parts]
                                 ).then_inc(stats_done, 1)
                dve.wait_ge(stats_done, (number + 1) * parts)
                dve.sem_inc(vec_fence, 1)
                dve.bn_aggr(out, st[:, 0:6 * parts]).then_inc(ready, 1)

            def x_stats(g, j):
                j4 = j % G
                dve.wait_ge(x_loaded[j4], (g + (j // G + 1)) * 16)
                moments(x_in[:, j4, :], stats[:, j4, :], mv[:, 0, j4, :], stats_done[0], var_done[0], g * G + j)

            def key_bias(g, j):
                if isinstance(g, int) and g * G + j == 0:
                    dve.wait_ge(weights_in, 16 * 10)
                    for c in range(2):
                        dve.tensor_tensor(kb_par[:, c, :], head_parity[:], qkv_b[:, 2 + c:3 + c].to_broadcast([P, 2]),
                                          ALU.mult).then_inc(consts_done, 1)

            def x_normed(g, j):
                j4 = j % G
                dve.wait_ge(rstd_done[0], g * G + (j + 1))
                dve.tensor_scalar(x_n[:, j4, :], x_in[:, j4, :], mv[:, 0, j4, 0:1], rs[:, 0, j4:j4 + 1],
                                  ALU.subtract, ALU.mult).then_inc(xn_done, 1)

            def tok_stats(g, j):
                j4 = j % G
                dve.wait_ge(tok_mm, g * G + (j + 1))
                dve.tensor_tensor(t_lin[:, j4, :], ps[:, at.bank("tok", j), 0:DIM], tok_b[:], ALU.add
                                  ).then_inc(tok_free, 1)
                dve.wait_ge(tok_free, g * G + (j + 1))
                moments(t_lin[:, j4, :], stats2[:, j4, :], mv[:, 1, j4, :], stats_done[1], var_done[1], g * G + j)

            def h0_made(g, j):
                j4 = j % G
                dve.wait_ge(rstd_done[1], g * G + (j + 1))
                dve.tensor_scalar(h0[:, j4, :], t_lin[:, j4, :], mv[:, 1, j4, 0:1], rs[:, 1, j4:j4 + 1],
                                  ALU.subtract, ALU.mult).then_inc(h0_part, 1)
                dve.wait_ge(h0_part, (g * G + j) * 2 + 1)
                dve.tensor_tensor(h0[:, j4, :], h0[:, j4, :], ln2_g[:], ALU.mult).then_inc(h0_part, 1)
                dve.wait_ge(h0_part, (g * G + j) * 2 + 2)
                dve.tensor_tensor(h0[:, j4, :], h0[:, j4, :], ln2_b[:], ALU.add).then_inc(h0_done, 1)
                dve.wait_ge(h0_done, g * G + (j + 1))
                moments(h0[:, j4, :], stats3[:, j4, :], mv[:, 2, j4, :], stats_done[2], var_done[2], g * G + j)

            def a_normed(g, j):
                j4 = j % G
                dve.wait_ge(rstd_done[2], g * G + (j + 1))
                dve.tensor_scalar(a_n[:, j4, :], h0[:, j4, :], mv[:, 2, j4, 0:1], rs[:, 2, j4:j4 + 1],
                                  ALU.subtract, ALU.mult).then_inc(an_done, 1)

            def v_read(g, j):
                dve.wait_ge(v_mm, g * G + (j + 1))
                dve.tensor_tensor(
                    vblk[:, j % G, :, :, :, 0:HD].rearrange("p i a c d -> p (i a) c d"),
                    ps[:, at.bank("v", j), :].rearrange("p (a c d) -> p a c d", c=2, d=HD),
                    copy_parity[:].unsqueeze(1).unsqueeze(3).to_broadcast([P, 2 * PAIRS, 2, HD]),
                    ALU.mult).then_inc(v_done, 1)

            def less_max(g, j):
                j4 = j % G
                dve.wait_ge(s_mm, g * G + (j + 1))
                s4 = ps_s[:, :, 0:256].rearrange("p g (a m) -> p g a m", m=64)
                dve.tensor_reduce(smax[:, j4, :].rearrange("p (g a) -> p g a", g=4), s4, AX.X, ALU.max
                                  ).then_inc(max_done, 1)
                dve.wait_ge(max_done, g * G + (j + 1))
                dve.tensor_tensor(e[:, j4].rearrange("p (g a) m -> p g a m", g=4), s4,
                                  smax[:, j4, :].rearrange("p (g a) -> p g a", g=4).unsqueeze(3)
                                  .to_broadcast([P, 4, 4, 64]), ALU.subtract).then_inc(s_sub, 1)

            def o_normed(g, j):
                j4 = j % G
                dve.wait_ge(pv_mm, g * G + (j + 1))
                pv = ps[:, at.bank("pv", j), 0:HEADS * (HD + 1)].rearrange("p (h d) -> p h d", d=HD + 1)
                dve.reciprocal(rsum[:, j4, :], pv[:, :, HD]).then_inc(rsum_done, 1)
                dve.wait_ge(rsum_done, g * G + (j + 1))
                dve.tensor_tensor(o_n[:, j4, :].rearrange("p (h d) -> p h d", d=HD), pv[:, :, 0:HD],
                                  rsum[:, j4, :].unsqueeze(2).to_broadcast([P, HEADS, HD]),
                                  ALU.mult).then_inc(o_done, 1)

            def h1_made(g, j):
                dve.wait_ge(proj_mm, g * G + (j + 1))
                dve.wait_ge(hp_done, g * G + (j + 1))
                dve.wait_ge(h1_stored[j % G], (g + j // G) * 16 + 16)
                dve.tensor_tensor(h1[:, j % G, :], ps[:, at.bank("proj", j), 0:DIM], hp[:, j % G, :], ALU.add
                                  ).then_inc(h1_done, 1)

            def dequantise(g, j):
                if isinstance(g, int) and g == 0 and j >= 2:
                    w, scales = ((fc1_w, sh_gu), (fc2_w, uv_w))[j - 2]
                    w, scales = (x[:].rearrange("p k n -> p (k n)") for x in (w, scales))
                    at_least(dve, quant_in, 64)
                    for half in (slice(0, F0), slice(F0, 2 * F0)):
                        dve.scalar_tensor_tensor(out=w[:, half], in0=w[:, half].bitcast(I32), scalar=-128.0,
                                                 in1=scales[:, half], op0=ALU.add, op1=ALU.mult
                                                 ).then_inc(dequantised, 1)

            pipeline(dve, GROUPS, G, [(less_max, 3), (x_stats, 0), (tok_stats, 1), (h1_made, 4), (x_normed, 0),
                                      (key_bias, 0), (h0_made, 1), (v_read, 2), (a_normed, 1), (o_normed, 3), (dequantise, 0)])

            dve.wait_ge(b_weights_in, 16 * 13)

            def b_moments(src, n, g, j):
                for t in range(H):
                    dve.bn_stats(b_st[:, n, t, :], src[:, t, :]).then_inc(b_stats[n], 1)
                at_least(dve, b_stats[n], (item(g, j) + 1) * H)
                dve.sem_inc(vec_fence, 1)
                for t in range(H):
                    dve.bn_aggr(b_mv[:, n, j % 2, t, :], b_st[:, n, t, :]).then_inc(b_var[n], 1)

            def normed(out, src, n, j, which, done):
                for t in range(H):
                    dve.tensor_scalar(out[:, t, :], src[:, t, :], b_mv[:, n, j % 2, t, 0:1],
                                      b_rs[:, n, j % 2, which, t:t + 1], ALU.subtract, ALU.mult).then_inc(done, 1)

            def stats_h1(g, j):
                at_least(dve, h_loaded[j % 4], (g + (j // 4 + 1)) * 32)
                b_moments(res[:, j % 4], 0, g, j)

            def norm_h1(g, j):
                at_least(dve, b_scales[0], item(g, j) + 1)
                at_least(dve, res1_done, item(g, j) - 1)
                normed(n1[:, j % 2], res[:, j % 4], 0, j, 0, n1_done)
                made(dve, g, "n2T", j - 2)
                normed(n2[:, j % 2], res[:, j % 4], 0, j, 1, n2_done)

            def h2_made(g, j):
                made(dve, g, "fc2", j)
                at_least(dve, res1_done, item(g, j) + 1)
                dve.scalar_tensor_tensor(out=res[:, j % 4].rearrange("p t d -> p (t d)"), in0=ps[:, b_bank("fc2", j), :],
                                         scalar=0.5, in1=res[:, j % 4].rearrange("p t d -> p (t d)"),
                                         op0=ALU.mult, op1=ALU.add).then_inc(b_read["fc2"], 1)
                was_read(dve, g, "fc2", j)
                b_moments(res[:, j % 4], 1, g, j)

            def norm_h2(g, j):
                at_least(dve, b_scales[1], item(g, j) + 1)
                made(dve, g, "xxT", j - 2)
                normed(xx[:, j % 2], res[:, j % 4], 1, j, 1, xx_done)
                at_least(dve, res2_done, item(g, j) - 1)
                normed(qn[:, j % 2], res[:, j % 4], 1, j, 0, qn_done)

            def uv_biased(g, j):
                made(dve, g, "uyT", j - 1, H - 1)
                for t in range(H):
                    for h in range(2):
                        made(dve, g, "uv", j, 2 * t + h)
                        dve.tensor_tensor(uv[:, t, h * GF:(h + 1) * GF], ps[:, b_bank("uv", j, 2 * t + h), :],
                                          uv_b[:, h * GF:(h + 1) * GF], ALU.add).then_inc(b_read["uv"], 1)

            def gated(g, j):
                for t in range(H):
                    made(dve, g, "mix", j, t)
                    dve.tensor_tensor(uv[:, t, 0:GF], uv[:, t, 0:GF], ps[:, b_bank("mix", j, t), :], ALU.mult
                                      ).then_inc(b_read["mix"], 1)

            def h3_made(g, j):
                made(dve, g, "o", j)
                at_least(dve, res2_done, item(g, j) + 1)
                at_least(dve, h4_stored[j % 2], (g * 2 + j // 2) * 32 + 16)
                dve.tensor_tensor(res3[:, j % 2].rearrange("p t d -> p (t d)"), ps[:, b_bank("o", j), :],
                                  res[:, j % 4].rearrange("p t d -> p (t d)"), ALU.add).then_inc(b_read["o"], 1)
                was_read(dve, g, "o", j)
                b_moments(res3[:, j % 2], 2, g, j)

            def norm_h3(g, j):
                at_least(dve, b_scales[2], item(g, j) + 1)
                at_least(dve, xm_stored[j % 2], (g * 2 + j // 2) * 32 + 16)
                normed(xm[:, j % 2], res3[:, j % 2], 2, j, 0, xm_done)

            def shared_hidden(g, j):
                for c in range(KS):
                    at_least(dve, shg_done, b_count(g, "gu", j, c))
                    dve.tensor_tensor(shT[:, c, :], sh_g[:, c % 2, :], ps[:, b_bank("gu", j, c), H * P:2 * H * P],
                                      ALU.mult).then_inc(b_read["gu"], 1)

            def shared_out(g, j):
                made(dve, g, "down", j)
                dve.tensor_tensor(res3[:, j % 2].rearrange("p t d -> p (t d)"), ps[:, b_bank("down", j), :],
                                  res3[:, j % 2].rearrange("p t d -> p (t d)"), ALU.add).then_inc(b_read["down"], 1)

            choosing = Chain(dve, choose_chain, 24 * B_PER)
            placing = Chain(dve, place_chain, 3 * B_PER)

            def choose(g, j):
                choosing.turn(g, j * 24)

                def do(ins):
                    choosing.wait(choosing.step(ins))

                def ranks(out, v, n, a, b):
                    shape = [P, H, n, n]
                    mine, others = v.unsqueeze(3).to_broadcast(shape), v.unsqueeze(2).to_broadcast(shape)
                    tri = below_e[:, 0:n, 0:n].unsqueeze(1).to_broadcast(shape)
                    dve.tensor_tensor(a, others, mine, ALU.is_gt)
                    do(dve.tensor_tensor(b, others, mine, ALU.is_equal))
                    do(dve.tensor_tensor(b, b, tri, ALU.mult))
                    do(dve.tensor_tensor(a, a, b, ALU.add))
                    do(dve.tensor_reduce(out, a, AX.X, ALU.add))

                def part(x, n):
                    return x[:].rearrange("p a b c -> p (a b c)")[:, 0:H * n * n].rearrange(
                        "p (t a b) -> p t a b", t=H, a=n)

                was_read(dve, g, "router", j)
                do(dve.tensor_tensor(biased[:], scores[:, j % 2], router_b[:].unsqueeze(1)
                                     .to_broadcast([P, H, EXPERTS]), ALU.add))
                s4 = biased[:].rearrange("p t (g o) -> p (t g) o", o=OF_GROUP)
                do(dve.tensor_tensor(pair_sums[:, :, 0:3], s4[:, :, 0:3], s4[:, :, 1:4], ALU.add))
                do(dve.tensor_tensor(pair_sums[:, :, 3:5], s4[:, :, 0:2], s4[:, :, 2:4], ALU.add))
                do(dve.tensor_tensor(pair_sums[:, :, 5:6], s4[:, :, 0:1], s4[:, :, 3:4], ALU.add))
                do(dve.tensor_reduce(g_score[:].rearrange("p t g -> p (t g)"), pair_sums[:], AX.X, ALU.max))
                ranks(g_rank[:], g_score[:], EXPERT_GROUPS, part(cmp_a, EXPERT_GROUPS), part(cmp_b, EXPERT_GROUPS))
                do(dve.tensor_scalar(g_rank[:], g_rank[:], float(TOP_GROUPS), None, ALU.is_lt))
                do(dve.tensor_scalar(g_less[:], g_rank[:], -1.0, None, ALU.add))
                per_group = [P, H * EXPERT_GROUPS, OF_GROUP]
                m4 = masked[:].rearrange("p t (g o) -> p (t g) o", o=OF_GROUP)
                do(dve.tensor_tensor(m4, s4, g_rank[:].rearrange("p t g -> p (t g)").unsqueeze(2)
                                     .to_broadcast(per_group), ALU.mult))
                do(dve.tensor_tensor(m4, m4, g_less[:].rearrange("p t g -> p (t g)").unsqueeze(2)
                                     .to_broadcast(per_group), ALU.add))
                ranks(rank_e[:], masked[:], EXPERTS, cmp_a[:], cmp_b[:])
                dve.tensor_scalar(taken[:], rank_e[:], float(TOP), None, ALU.is_lt).then_inc(taken_done, 1)
                at_least(dve, taken_done, item(g, j) + 1)
                do(dve.tensor_tensor(tw[:], scores[:, j % 2], taken[:], ALU.mult))
                do(dve.tensor_reduce(w_sum[:], tw[:], AX.X, ALU.add))
                do(dve.tensor_scalar(w_sum[:], w_sum[:], 1e-20, None, ALU.add))
                do(dve.reciprocal(w_sum[:], w_sum[:]))
                do(dve.scalar_tensor_tensor(out=tw[:], in0=tw[:], scalar=ROUTE_SCALE, in1=w_sum[:].unsqueeze(2)
                                            .to_broadcast([P, H, EXPERTS]), op0=ALU.mult, op1=ALU.mult))
                do(dve.tensor_tensor(is_choice[:], rank_e[:].unsqueeze(2).to_broadcast([P, H, TOP, EXPERTS]),
                                     rank_no[:].unsqueeze(1).to_broadcast([P, H, TOP, EXPERTS]), ALU.is_equal))
                do(dve.tensor_tensor(picked[:], is_choice[:], tw[:].unsqueeze(2)
                                     .to_broadcast([P, H, TOP, EXPERTS]), ALU.mult))
                at_least(dve, recs_free, item(g, j) + 1)
                recs_f = recs[:, j % 2].bitcast(F32)
                dve.tensor_reduce(recs_f[:, :, :, 2], picked[:], AX.X, ALU.add).then_inc(recs_done, 1)
                dve.tensor_copy(recs_f[:, :, :, 1], token_row[:, span(item(g, j) * H, H)].unsqueeze(2)
                                .to_broadcast([P, H, TOP])).then_inc(recs_done, 1)
                at_least(dve, recs_done, item(g, j) * 3 + 2)
                assert choosing.n == 24, choosing.n

            def place(g, j):
                placing.turn(g, j * 3)

                def do(ins):
                    placing.wait(placing.step(ins))
                made(dve, g, "count", j)
                b = b_bank("count", j)
                do(dve.tensor_tensor(rec_no[:], ps[:, b, 0:H * EXPERTS].rearrange("p (t e) -> p t e", t=H),
                                     next_rec[:].unsqueeze(1).to_broadcast([P, H, EXPERTS]), ALU.add))
                dve.tensor_tensor(next_rec[:], next_rec[:], ps[:, b, H * EXPERTS:(H + 1) * EXPERTS], ALU.add
                                  ).then_inc(b_read["count"], 1)
                do(dve.tensor_tensor(picked[:], is_choice[:], rec_no[:].unsqueeze(2)
                                     .to_broadcast([P, H, TOP, EXPERTS]), ALU.mult))
                do(dve.tensor_reduce(choice_rec[:], picked[:], AX.X, ALU.add))
                dve.tensor_copy(recs[:, j % 2, :, :, 0], choice_rec[:]).then_inc(recs_done, 1)
                at_least(dve, recs_done, item(g, j) * 3 + 3)

            dve.wait_ge(c_consts, C_CONSTS)
            dve.wait_ge(router_b_in, 16)
            pipeline(dve, B_TURNS, B_PER, [
                (norm_h2, 2), (stats_h1, 0), (choose, 4), (shared_hidden, 4), (h3_made, 3), (place, 4),
                (shared_out, 4),
                (norm_h1, 0), (norm_h3, 3), (uv_biased, 2), (h2_made, 1), (gated, 2)])

            cn = [0]

            def do(ins):
                cn[0] += 1
                ins.then_inc(vec_chain_c, 1)
                dve.wait_ge(vec_chain_c, cn[0])

            do(dve.tensor_tensor(counts[:], next_rec[:], first_rec[:], ALU.subtract))
            do(dve.tensor_scalar(padded[:], counts[:], float(P - 1), None, ALU.add))
            do(dve.tensor_copy(ends_a[:].bitcast(I32), padded[:]))
            do(dve.tensor_scalar(ends_a[:].bitcast(I32), ends_a[:].bitcast(I32), 7, None, ALU.logical_shift_right))
            do(dve.tensor_copy(padded[:], ends_a[:].bitcast(I32)))
            src, dst = padded, ends_a
            for d in (1, 2, 4, 8):
                do(dve.tensor_copy(dst[:, 0:d], src[:, 0:d]))
                do(dve.tensor_tensor(dst[:, d:], src[:, d:], src[:, 0:EXPERTS - d], ALU.add))
                src, dst = dst, (ends_b if dst is ends_a else ends_a)
            ends = src
            both = [P, 2, EXPERTS]
            do(dve.tensor_tensor(started[:], ends[:].unsqueeze(1).to_broadcast(both),
                                 my_tile[:].unsqueeze(2).to_broadcast(both), ALU.is_le))
            do(dve.tensor_reduce(my_e[:], started[:], AX.X, ALU.add))
            do(dve.tensor_tensor(starts[:], started[:], ends[:].unsqueeze(1).to_broadcast(both), ALU.mult))
            do(dve.tensor_reduce(my_start[:], starts[:], AX.X, ALU.max))
            do(dve.scalar_tensor_tensor(out=my_block[:], in0=my_e[:], scalar=float(BLOCKS), in1=my_tile[:],
                                        op0=ALU.mult, op1=ALU.add))
            do(dve.tensor_tensor(my_block[:], my_block[:], my_start[:], ALU.subtract))
            do(dve.tensor_scalar(my_block[:], my_block[:], float(EXPERTS * BLOCKS), None, ALU.min))
            dve.tensor_copy(block_rows[:], my_block[:]).then_inc(blocks_known, 1)
            for j in range(2):
                dve.wait_ge(h4_stored[j], 16 * ITEMS + 16)
            along = [P, SLOT_TILES, EXPERTS]
            do(dve.tensor_tensor(ends_at, ends[:].unsqueeze(1).to_broadcast(along),
                                 tile_no[:].unsqueeze(2).to_broadcast(along), ALU.is_le))
            do(dve.tensor_reduce(tile_e[:], ends_at, AX.X, ALU.add))
            do(dve.tensor_scalar(tile_e[:], tile_e[:], float(EXPERTS - 1), None, ALU.min))
            dve.tensor_copy(tile_expert[:], tile_e[:]).then_inc(experts_known, 1)
            dve.wait_ge(slot_recs_turned, 1)
            dve.tensor_copy(slot_rows[:], ps[:, 0, 0:SLOT_TILES]).then_inc(rows_done, 1)
            dve.tensor_copy(slot_w[:], ps[:, 0, 2 * P:2 * P + SLOT_TILES]).then_inc(rows_done, 1)
            dve.wait_ge(rows_done, 2)

            def hidden(g, j):
                b = d_bank("gu", j)
                dve.wait_ge(act_g_done, g * GD + (j + 1))
                dve.tensor_tensor(hid[:, j % G, :], act_g[:, j % G, :], ps[:, b, FE:2 * FE], ALU.mult
                                  ).then_inc(d_read["gu"], 1)

            def weighed(g, j):
                b = d_bank("down", j)
                dve.wait_ge(d_written["down"], d_made(g, "down", j))
                at_least(dve, added[j % G], (g * 2 + j // G) * 16)
                dve.tensor_scalar(y[:, j % G, :], ps[:, b, 0:DIM], slot_w[:, span(g * GD + j, 1)], None, ALU.mult
                                  ).then_inc(d_read["down"], 1)

            pipeline(dve, D_TURNS, GD, [(hidden, GU_LAG), (weighed, DOWN_LAG)])

        @block.tensor
        def _(pe):
            pe.wait_ge(setup, 11)

            def x_turn(g, j):
                pe.wait_ge(xn_done, g * G + (j + 1))
                turn_banks.free(pe, g, "xnT", j)
                for k in range(KX):
                    ins = pe.transpose(ps_t[:, k // 4, (k % 4) * P:(k % 4 + 1) * P],
                                       x_n[:, j % G, k * P:(k + 1) * P], ident[:])
                ins.then_inc(xnT_mm, 1)

            def patches_out(g, j):
                pe.wait_ge(xnT_done, g * G + (j + 1))
                if isinstance(g, int) and g * G + j == 0:
                    pe.wait_ge(weights_in, 16 * 10)
                b = at.free(pe, g, "tok", j)
                for k in range(KX):
                    ins = pe.matmul(ps[:, b, 0:DIM], x_nT[:, j % G, k, :], tok_w[:, k, :],
                                    start=(k == 0), stop=(k == KX - 1))
                ins.then_inc(tok_mm, 1)

            def a_turn(g, j):
                pe.wait_ge(an_done, g * G + (j + 1))
                b = at.free(pe, g, "anT", j)
                for k in range(KD):
                    ins = pe.transpose(ps[:, b, k * P:(k + 1) * P], a_n[:, j % G, k * P:(k + 1) * P], ident[:])
                ins.then_inc(anT_mm, 1)

            def queries_keys(g, j):
                pe.wait_ge(aT_done, g * G + (j + 1))
                b = at.free(pe, g, "qk", j)
                for c in range(4):
                    for k in range(KD):
                        ins = pe.matmul(ps[:, b, c * P:(c + 1) * P], qkv_w[:, k, c * P:(c + 1) * P],
                                        aT[:, j % G, k, :, 0, :], start=(k == 0), stop=(k == KD - 1))
                ins.then_inc(qk_mm, 1)

            def values(g, j):
                b = at.free(pe, g, "v", j)
                for i in range(2):
                    for k in range(KD):
                        ins = pe.matmul(ps[:, b, i * DIM:(i + 1) * DIM],
                                        aT[:, j % G, k, i].rearrange("p c t -> p (c t)"),
                                        qkv_w[:, k, 2 * DIM:3 * DIM], start=(k == 0), stop=(k == KD - 1))
                ins.then_inc(v_mm, 1)

            def scores(g, j):
                pe.wait_ge(qk_done, g * G + (j + 1))
                at_least(pe, s_sub, g * G + j)
                for c in range(2):
                    for i in range(2):
                        for r in range(4):
                            ins = pe.matmul(ps_s[64 * i:64 * i + 64, r, c * P:(c + 1) * P],
                                            qT[32 * r:32 * r + 32, j % G, c, 64 * i:64 * i + 64],
                                            kT[32 * r:32 * r + 32, j % G, c, :, 64 * i:64 * i + 64],
                                            start=True, stop=True)
                ins.then_inc(s_mm, 1)

            def p_turn(g, j):
                pe.wait_ge(e_done, g * G + (j + 1))
                turn_banks.free(pe, g, "pT", j)
                for a in range(PAIRS):
                    ins = pe.transpose(ps_t[:, a // 4, (a % 4) * P:(a % 4 + 1) * P],
                                       e[:, j % G, 2 * a:2 * a + 2].rearrange("p c m -> p (c m)"), ident[:])
                ins.then_inc(pT_mm, 1)

            def heads_out(g, j):
                pe.wait_ge(pT_done, g * G + (j + 1))
                pe.wait_ge(v_done, g * G + (j + 1))
                b = at.free(pe, g, "pv", j)
                for a in range(PAIRS):
                    for i in range(2):
                        ins = pe.matmul(ps[64 * i:64 * i + 64, b, a * 34:a * 34 + 34],
                                        pT[:, j % 2, a, 64 * i:64 * i + 64],
                                        vblk[:, j % G, i, a].rearrange("p c d -> p (c d)"), start=True, stop=True)
                ins.then_inc(pv_mm, 1)

            def o_turn(g, j):
                pe.wait_ge(o_done, g * G + (j + 1))
                b = at.free(pe, g, "oT", j)
                for k in range(KD):
                    ins = pe.transpose(ps[:, b, k * P:(k + 1) * P], o_n[:, j % G, k * P:(k + 1) * P], ident[:])
                ins.then_inc(oT_mm, 1)

            def project(g, j):
                pe.wait_ge(oT_done, g * G + (j + 1))
                b = at.free(pe, g, "proj", j)
                for k in range(KD):
                    ins = pe.matmul(ps[:, b, 0:DIM], oT[:, j % G, k, :], proj_w[:, k, :],
                                    start=(k == 0), stop=(k == KD - 1))
                ins.then_inc(proj_mm, 1)

            pipeline(pe, GROUPS, G, [(scores, 3), (o_turn, 4), (patches_out, 1), (queries_keys, 2), (project, 4),
                                     (p_turn, 3), (values, 2), (heads_out, 3), (a_turn, 1), (x_turn, 0)])

            pe.wait_ge(b_weights_in, 16 * 13)
            pe.wait_ge(dequantised, 4)
            pe.wait_ge(h1_done, TILES)

            def open_bank(g, stage, j, c=0):
                return b_banks.free(pe, g, stage, j * PRODUCTS[stage] + c)

            def turn(stage, src, ready):
                def step(g, j):
                    at_least(pe, ready, (item(g, j) + 1) * H)
                    b = open_bank(g, stage, j)
                    for t in range(H):
                        for k in range(KD):
                            at_ = (t * KD + k) * P
                            ins = pe.transpose(ps[:, b, at_:at_ + P], src[:, j % 2, t, k * P:(k + 1) * P], ident[:])
                    ins.then_inc(b_made[stage], 1)
                return step

            def tokens_out(b, col, left, right, chunks, width):
                for k in range(chunks):
                    ins = pe.matmul(ps[:, b, col:col + width], left(k), right(k), start=(k == 0),
                                    stop=(k == chunks - 1))
                return ins

            def features_out(b, half, w, col, src):
                for k in range(KD):
                    ins = pe.matmul(ps[:, b, half * H * P:(half + 1) * H * P], w[:, k, col:col + P], src[:, k, :],
                                    start=(k == 0), stop=(k == KD - 1))
                return ins

            def fc1(g, j):
                was_read(pe, g, "n2T", j)
                for c in range(K2 // 2):
                    b = open_bank(g, "fc1", j, c)
                    for half in range(2):
                        ins = features_out(b, half, fc1_w, (2 * c + half) * P, n2T_s[:, j % 2])
                    ins.then_inc(b_made["fc1"], 1)

            def fc2(g, j):
                was_read(pe, g, "fc1", j, K2 // 2 - 1)
                b = open_bank(g, "fc2", j)
                for t in range(H):
                    ins = tokens_out(b, t * DIM, lambda k: hidT[:, k, t * P:(t + 1) * P], lambda k: fc2_w[:, k, :],
                                     K2, DIM)
                ins.then_inc(b_made["fc2"], 1)

            def u_and_v(g, j):
                was_read(pe, g, "xxT", j)
                for t in range(H):
                    for h in range(2):
                        b = open_bank(g, "uv", j, 2 * t + h)
                        tokens_out(b, 0, lambda k: xxT_s[:, j % 2, k, t * P:(t + 1) * P],
                                   lambda k: uv_w[:, k, h * GF:(h + 1) * GF], KD, GF).then_inc(b_made["uv"], 1)

            def mix(g, j):
                for t in range(H):
                    at_least(pe, uv_done, item(g, j) * H + t + 1)
                    b = open_bank(g, "mix", j, t)
                    for h in range(MIX_HEADS):
                        ins = pe.matmul(ps[:, b, h * MIX_HD:(h + 1) * MIX_HD], mix_w[:, h, :],
                                        uv[:, t, GF + h * MIX_HD:GF + (h + 1) * MIX_HD], start=True, stop=True)
                    ins.then_inc(b_made["mix"], 1)

            def uy_turn(g, j):
                for t in range(H):
                    was_read(pe, g, "mix", j, t)
                    b = open_bank(g, "uyT", j, t)
                    for k in range(KG):
                        ins = pe.transpose(ps[:, b, k * P:(k + 1) * P], uv[:, t, k * P:(k + 1) * P], ident[:])
                    ins.then_inc(b_made["uyT"], 1)

            def o_out(g, j):
                was_read(pe, g, "uyT", j, H - 1)
                b = open_bank(g, "o", j)
                for t in range(H):
                    ins = tokens_out(b, t * DIM, lambda k: uyT_s[:, t, k, :], lambda k: o_w[:, k, :], KG, DIM)
                ins.then_inc(b_made["o"], 1)

            def router(g, j):
                was_read(pe, g, "xmT", j)
                b = open_bank(g, "router", j)
                for t in range(H):
                    ins = tokens_out(b, t * EXPERTS, lambda k: xmT_s[:, j % 2, k, t * P:(t + 1) * P],
                                     lambda k: router_w[:, k, :], KD, EXPERTS)
                ins.then_inc(b_made["router"], 1)

            def shared_gate_up(g, j):
                was_read(pe, g, "xmT", j)
                for c in range(KS):
                    b = open_bank(g, "gu", j, c)
                    for half in range(2):
                        ins = features_out(b, half, sh_gu, half * FS + c * P, xmT_s[:, j % 2])
                    ins.then_inc(b_made["gu"], 1)

            def shared_down(g, j):
                was_read(pe, g, "gu", j, KS - 1)
                b = open_bank(g, "down", j)
                for t in range(H):
                    ins = tokens_out(b, t * DIM, lambda k: shT[:, k, t * P:(t + 1) * P], lambda k: sh_d[:, k, :],
                                     KS, DIM)
                ins.then_inc(b_made["down"], 1)

            def count(g, j):
                at_least(pe, taken_done, item(g, j) + 1)
                b = open_bank(g, "count", j)
                for t in range(H + 1):
                    parts = [(ones, i) for i in range(t)] + ([(earlier, t)] if t < H else [])
                    for n, (left, i) in enumerate(parts):
                        ins = pe.matmul(ps[:, b, t * EXPERTS:(t + 1) * EXPERTS], left[:], taken[:, i, :],
                                        start=(n == 0), stop=(n == len(parts) - 1))
                ins.then_inc(b_made["count"], 1)

            b_stage = {"fc1": fc1, "xxT": turn("xxT", xx, xx_done), "uyT": uy_turn, "gu": shared_gate_up, "o": o_out,
                       "down": shared_down, "uv": u_and_v, "fc2": fc2, "n2T": turn("n2T", n2, n2_done),
                       "xmT": turn("xmT", xm, xm_done), "mix": mix, "router": router,
                       "count": count}
            pe.wait_ge(c_consts, C_CONSTS)
            pipeline(pe, B_TURNS, B_PER, [(b_stage[name], lag) for name, lag in B_STEPS])

            pe.wait_ge(slot_recs_in, 32)
            pe.wait_ge(b_read["count"], ITEMS)
            for c in range(2):
                for what in range(2):
                    at_ = (2 * what + c) * P
                    ins = pe.transpose(ps[:, 0, at_:at_ + P],
                                       slot_recs[:, c, :].rearrange("p (x w) -> p w x", w=2)[:, what, :], ident[:])
            ins.then_inc(slot_recs_turned, 1)

            pe.wait_ge(experts_in, 32)
            pe.wait_ge(experts_known, 1)
            pe.wait_ge(rows_done, 2)

            def d_open(g, stage, j):
                b = d_bank(stage, j)
                at_least(pe, d_read[stage], d_before(g, stage, j))
                return b

            def expert_of(g, j):
                where = tile_expert[0:1, g * GD + j:g * GD + j + 1] if isinstance(g, int) else \
                    tile_expert[0:1, bass.ds(g * GD + j, 1)]
                return pe.value_load(where, min_val=0, max_val=EXPERTS - 1)

            def gu(g, j):
                e_of = expert_of(g, j)
                pe.wait_ge(d_read["xgT"], d_made(g, "xgT", j))
                b = d_open(g, "gu", j)
                for k in range(KD):
                    ins = pe.matmul(ps[:, b, :], xgT[:, j % G, k, :],
                                    expert_gu[:, bass.ds(e_of, 1), k, :].rearrange("p e n -> p (e n)"),
                                    start=(k == 0), stop=(k == KD - 1))
                ins.then_inc(d_written["gu"], 1)

            def turn_hidden(g, j):
                pe.wait_ge(d_read["gu"], d_made(g, "gu", j))
                b = d_open(g, "hT", j)
                for k in range(KFE):
                    ins = pe.transpose(ps[:, b, k * P:(k + 1) * P], hid[:, j % G, k * P:(k + 1) * P], ident[:])
                ins.then_inc(d_written["hT"], 1)

            def turn_x(g, j):
                pe.wait_ge(gathered[j % G], (g * 2 + (j // G + 1)) * 16)
                b = d_open(g, "xgT", j)
                for k in range(KD):
                    ins = pe.transpose(ps[:, b, k * P:(k + 1) * P], xg[:, j % G, k * P:(k + 1) * P], ident[:])
                ins.then_inc(d_written["xgT"], 1)

            def down(g, j):
                e_of = expert_of(g, j)
                pe.wait_ge(d_read["hT"], d_made(g, "hT", j))
                b = d_open(g, "down", j)
                for k in range(KFE):
                    ins = pe.matmul(ps[:, b, 0:DIM], hT[:, j % G, k, :],
                                    expert_d[:, bass.ds(e_of, 1), k, :].rearrange("p e n -> p (e n)"),
                                    start=(k == 0), stop=(k == KFE - 1))
                ins.then_inc(d_written["down"], 1)

            pipeline(pe, D_TURNS, GD, [(gu, GU_LAG), (turn_hidden, HID_LAG), (turn_x, X_LAG), (down, DOWN_LAG)])


def layouts(np, x, L0_tok_ln1_g, L0_tok_ln1_b, L0_tok_W, L0_tok_b, L0_tok_ln2_g, L0_tok_ln2_b, L0_attn_qkv_w,
            L0_attn_qkv_b, L0_attn_proj_w, L0_attn_proj_b, L0_ffn_ln_gamma, L0_ffn_ln_beta, L0_ffn_fc1_q,
            L0_ffn_fc1_scales, L0_ffn_fc1_bias, L0_ffn_fc2_q, L0_ffn_fc2_scales, L0_ffn_fc2_bias, L1_attn_u_w,
            L1_attn_u_b, L1_attn_v_w, L1_attn_v_b, L1_attn_o_w, L1_attn_o_b, L1_attn_pos, L1_attn_zero, L1_attn_neg,
            L1_ffn_router_w, L1_ffn_bias, L1_ffn_gate_w, L1_ffn_up_w, L1_ffn_down_w, L1_ffn_sh_gate_w,
            L1_ffn_sh_up_w, L1_ffn_sh_down_w, **unused):
    tokens = x.reshape(64, 3, 8, 16, 8, 16).transpose(0, 2, 4, 3, 5, 1).reshape(TOKENS, PIX)
    order = [8 * c + 2 * r + par for r in range(4) for c in range(2) for par in range(2)]
    cols = np.concatenate([np.arange(16 * h, 16 * h + 16) for h in order])
    v_w = L0_attn_qkv_w[:, 512:][:, cols]
    qkv_w = np.concatenate([L0_attn_qkv_w[:, :512], v_w], axis=1)
    qkv_b = np.concatenate([L0_attn_qkv_b[:512], L0_attn_qkv_b[512:][cols]])
    taps = np.concatenate([L1_attn_neg[:, :IMAGES - 1][:, ::-1], L1_attn_zero, L1_attn_pos[:, :IMAGES - 1]], axis=1)
    j, i = np.arange(IMAGES)[:, None], np.arange(IMAGES)[None, :]
    mix = taps[:, i - j + IMAGES - 1].transpose(1, 0, 2)
    return {
        "fc1_q": L0_ffn_fc1_q, "fc1_s": L0_ffn_fc1_scales, "fc1_b": L0_ffn_fc1_bias.reshape(K2, P).T,
        "fc2_q": L0_ffn_fc2_q, "fc2_s": L0_ffn_fc2_scales, "fc2_b": L0_ffn_fc2_bias,
        "ln3_g": L0_ffn_ln_gamma.reshape(KD, P).T, "ln3_b": L0_ffn_ln_beta.reshape(KD, P).T,
        "uv_w": np.concatenate([L1_attn_u_w.T, L1_attn_v_w.T], axis=1), "uv_b": np.concatenate([L1_attn_u_b, L1_attn_v_b]),
        "mix": mix, "o_w": L1_attn_o_w.T, "o_b": L1_attn_o_b, "router_w": L1_ffn_router_w.T,
        "router_b": L1_ffn_bias,
        "sh_gu": np.concatenate([L1_ffn_sh_gate_w, L1_ffn_sh_up_w], axis=1), "sh_d": L1_ffn_sh_down_w,
        "expert_gu": np.concatenate([L1_ffn_gate_w, L1_ffn_up_w], axis=2), "expert_d": L1_ffn_down_w,
        "x": tokens, "ln1_g": L0_tok_ln1_g.reshape(6, P).T, "ln1_b": L0_tok_ln1_b.reshape(6, P).T,
        "tok_w": L0_tok_W.T, "tok_b": L0_tok_b, "ln2_g": L0_tok_ln2_g, "ln2_b": L0_tok_ln2_b,
        "qkv_w": qkv_w, "qkv_b": qkv_b.reshape(6, P).T, "proj_w": L0_attn_proj_w[cols, :], "proj_b": L0_attn_proj_b,
    }


def kernel(**inputs):
    import numpy as np
    import concourse.bacc as bacc
    from concourse.bass_utils import run_bass_kernel_spmd

    arrays = {"in_" + k: np.ascontiguousarray(v) for k, v in layouts(np, **inputs).items()}
    nc = bacc.Bacc("TRN2", target_bir_lowering=False, num_devices=1)
    io = {k[3:]: nc.dram_tensor(k, a.shape, mybir.dt.from_np(a.dtype), kind="ExternalInput").ap()
          for k, a in arrays.items()}
    io["out"] = nc.dram_tensor("out", (TOKENS + PAD_ROWS, DIM), F32, kind="ExternalOutput").ap()
    build(nc, io)
    r = run_bass_kernel_spmd(nc, [arrays], core_ids=[0])
    return r.results[0]["out"][:TOKENS].reshape(IMAGES, PATCHES, DIM)
```
